# Optimizing a Trainium2 kernel written in Bass

```python
import numpy as np
import jax
import jax.numpy as jnp

def _softmax(x, axis=-1):
    return jax.nn.softmax(x, axis=axis)

def _gelu(x):
    return jax.nn.gelu(x, approximate=True)

def _silu(x):
    return jax.nn.silu(x)

def _sigmoid(x):
    return jax.nn.sigmoid(x)

def _layernorm(x, axis=-1, eps=1e-05):
    m = jnp.mean(x, axis=axis, keepdims=True)
    v = jnp.var(x, axis=axis, keepdims=True)
    return (x - m) / jnp.sqrt(v + eps)

def _scatter_add(tgt, idx, src, axis=0):
    return tgt.at[idx].add(src)

def _segment_sum(src, seg, n):
    return jax.ops.segment_sum(src, seg, n)
kernel_name = 'mk_lm_tower_d1_tok_ids1024_r4_e237c8'

def setup_inputs(seed: int=0):
    np.random.seed(seed)
    _w = jnp.asarray

    def _rec_inputs():
        import jax
        import jax.numpy as jnp
        _rk = jax.random.key(seed)
        x = jax.random.randint(jax.random.fold_in(_rk, 1), (32, 128), 0, 31993, jnp.int32)
        return x
    x = _rec_inputs()

    def _L0_tok_setup():
        import jax, jax.numpy as jnp
        import numpy as np
        EPS = 1e-05

        def layernorm(x, s, b):
            m = jnp.mean(x, axis=-1, keepdims=True)
            v = jnp.mean(jnp.square(x - m), axis=-1, keepdims=True)
            return (x - m) * jax.lax.rsqrt(v + EPS) * s + b

        def ssm(x, a_diag, Bm, Cm, Dm):
            a = jax.nn.sigmoid(a_diag)
            u = jnp.einsum('btd,ds->bts', x, Bm)

            def step(h, u_t):
                h = a * h + u_t
                return (h, h)
            h0 = jnp.zeros((x.shape[0], a.shape[0]), x.dtype)
            _, H = jax.lax.scan(step, h0, jnp.swapaxes(u, 0, 1))
            H = jnp.swapaxes(H, 0, 1)
            return jnp.einsum('bts,sd->btd', H, Cm) + jnp.einsum('btd,de->bte', x, Dm)
        key = jax.random.key(seed)
        ks = jax.random.split(key, 12)
        Bn, T = (4, 512)
        V, Dm, S, L, F = (8000, 256, 64, 4, 1024)

        def xavier(k, shape):
            fan_in, fan_out = (shape[-2], shape[-1])
            lim = float(np.sqrt(6.0 / (fan_in + fan_out)))
            return jax.random.uniform(k, shape, jnp.float32, -lim, lim)
        return {'tokens': jax.random.randint(ks[0], (Bn, T), 0, V), 'emb': jax.random.normal(ks[1], (V, Dm), jnp.float32), 'pos_emb': jax.random.normal(ks[2], (1024, Dm), jnp.float32), 'A_diag': jax.random.uniform(ks[3], (L, S), jnp.float32, -0.5, 0.5), 'B': xavier(ks[4], (L, Dm, S)), 'C': xavier(ks[5], (L, S, Dm)), 'D': xavier(ks[6], (L, Dm, Dm)) * 0.1, 'w1': xavier(ks[7], (L, Dm, F)), 'b1': jnp.zeros((L, F), jnp.float32), 'w2': xavier(ks[8], (L, F, Dm)), 'b2': jnp.zeros((L, Dm), jnp.float32), 'ln1_s': jnp.ones((L, Dm), jnp.float32), 'ln1_b': jnp.zeros((L, Dm), jnp.float32), 'ln2_s': jnp.ones((L, Dm), jnp.float32), 'ln2_b': jnp.zeros((L, Dm), jnp.float32), 'lnf_s': jnp.ones((Dm,), jnp.float32), 'lnf_b': jnp.zeros((Dm,), jnp.float32)}
    _L0_tok_all = _L0_tok_setup()
    _L0_tok_in = {k: v for k, v in _L0_tok_all.items() if k in ('emb', 'pos_emb', 'A_diag', 'B', 'C', 'D', 'w1', 'b1', 'w2', 'b2', 'ln1_s', 'ln1_b', 'ln2_s', 'ln2_b', 'lnf_s', 'lnf_b')}
    del _L0_tok_all

    def _L0_attn_setup():
        import jax, jax.numpy as jnp
        import numpy as np
        CHUNK = 32
        NUM_HEADS = 4
        HEAD_K = 64
        HEAD_V = 64
        EPS = 1e-05

        def l2norm(x, eps=1e-06):
            return x * jax.lax.rsqrt(jnp.sum(x * x, axis=-1, keepdims=True) + eps)

        def causal_depthwise_conv(x, w):
            K = w.shape[1]
            l = x.shape[1]
            xp = jnp.pad(x, ((0, 0), (K - 1, 0), (0, 0)))
            return sum((w[:, k] * xp[:, k:k + l, :] for k in range(K)))

        def delta_rule_chunkwise(q, k, v, beta):
            b, h, l, dk = q.shape
            dv = v.shape[-1]
            c = CHUNK
            n = l // c
            q = l2norm(q)
            k = l2norm(k)
            v = v * beta[..., None]
            k_beta = k * beta[..., None]
            resh = lambda x: x.reshape(b, h, n, c, x.shape[-1])
            q, k, v, k_beta = map(resh, (q, k, v, k_beta))
            tri_strict = jnp.tril(jnp.ones((c, c), dtype=q.dtype), -1)
            attn = -(k_beta @ jnp.swapaxes(k, -1, -2)) * tri_strict

            def body(i, a):
                row = a[..., i, :]
                upd = jnp.einsum('bhnj,bhnjk->bhnk', row, a)
                return a.at[..., i, :].add(upd)
            attn = jax.lax.fori_loop(1, c, body, attn)
            attn = attn + jnp.eye(c, dtype=attn.dtype)
            u = attn @ v
            w = attn @ k_beta
            mask_causal = jnp.tril(jnp.ones((c, c), dtype=q.dtype), 0)
            S0 = jnp.zeros((b, h, dk, dv), dtype=q.dtype)
            to_front = lambda x: jnp.moveaxis(x, 2, 0)

            def step(S, inp):
                q_i, k_i, u_i, w_i = inp
                attn_i = q_i @ jnp.swapaxes(k_i, -1, -2) * mask_causal
                u_new = u_i - w_i @ S
                o_i = q_i @ S + attn_i @ u_new
                S = S + jnp.swapaxes(k_i, -1, -2) @ u_new
                return (S, o_i)
            S, o = jax.lax.scan(step, S0, (to_front(q), to_front(k), to_front(u), to_front(w)))
            o = jnp.moveaxis(o, 0, 2).reshape(b, h, l, dv)
            return (o, S)
        key = jax.random.key(seed)
        ks = jax.random.split(key, 12)
        b, l, d = (4, 1024, 256)
        sc = 0.02
        return {'hidden_states': jax.random.normal(ks[0], (b, l, d), jnp.float32), 'Wq': jax.random.normal(ks[1], (256, 256), jnp.float32) * sc, 'Wk': jax.random.normal(ks[2], (256, 256), jnp.float32) * sc, 'Wv': jax.random.normal(ks[3], (256, 256), jnp.float32) * sc, 'conv_q': jax.random.normal(ks[4], (256, 4), jnp.float32) * 0.1, 'conv_k': jax.random.normal(ks[5], (256, 4), jnp.float32) * 0.1, 'conv_v': jax.random.normal(ks[6], (256, 4), jnp.float32) * 0.1, 'Wb': jax.random.normal(ks[7], (4, 256), jnp.float32) * sc, 'Wmix': jax.random.normal(ks[8], (4, 256), jnp.float32) * sc, 'norm_w': jnp.ones((64,), jnp.float32), 'Wo': jax.random.normal(ks[9], (256, 256), jnp.float32) * sc}
    _L0_attn_all = _L0_attn_setup()
    _L0_attn_in = {k: v for k, v in _L0_attn_all.items() if k in ('Wq', 'Wk', 'Wv', 'conv_q', 'conv_k', 'conv_v', 'Wb', 'Wmix', 'norm_w', 'Wo')}
    del _L0_attn_all

    def _L0_ffn_setup():
        import jax, jax.numpy as jnp
        import numpy as np
        B, S, H = (4, 512, 256)
        E, K, INTER = (16, 2, 128)
        ALPHA, LIMIT = (1.702, 7.0)
        key = jax.random.key(seed)
        ks = jax.random.split(key, 6)
        return {'hidden_states': jax.random.normal(ks[0], (B, S, H), jnp.float32), 'router_weight': jax.random.normal(ks[1], (H, E), jnp.float32) * 0.02, 'gate_up_proj': jax.random.normal(ks[2], (E, H, 2 * INTER), jnp.float32) * 0.02, 'gate_up_proj_bias': jax.random.normal(ks[3], (E, 2 * INTER), jnp.float32) * 0.02, 'down_proj': jax.random.normal(ks[4], (E, INTER, H), jnp.float32) * 0.02, 'down_proj_bias': jax.random.normal(ks[5], (E, H), jnp.float32) * 0.02}
    _L0_ffn_all = _L0_ffn_setup()
    _L0_ffn_in = {k: v for k, v in _L0_ffn_all.items() if k in ('router_weight', 'gate_up_proj', 'gate_up_proj_bias', 'down_proj', 'down_proj_bias')}
    del _L0_ffn_all
    return {'x': x, 'L0_tok_emb': _L0_tok_in['emb'], 'L0_tok_pos_emb': _L0_tok_in['pos_emb'], 'L0_tok_A_diag': _L0_tok_in['A_diag'], 'L0_tok_B': _L0_tok_in['B'], 'L0_tok_C': _L0_tok_in['C'], 'L0_tok_D': _L0_tok_in['D'], 'L0_tok_w1': _L0_tok_in['w1'], 'L0_tok_b1': _L0_tok_in['b1'], 'L0_tok_w2': _L0_tok_in['w2'], 'L0_tok_b2': _L0_tok_in['b2'], 'L0_tok_ln1_s': _L0_tok_in['ln1_s'], 'L0_tok_ln1_b': _L0_tok_in['ln1_b'], 'L0_tok_ln2_s': _L0_tok_in['ln2_s'], 'L0_tok_ln2_b': _L0_tok_in['ln2_b'], 'L0_tok_lnf_s': _L0_tok_in['lnf_s'], 'L0_tok_lnf_b': _L0_tok_in['lnf_b'], 'L0_attn_Wq': _L0_attn_in['Wq'], 'L0_attn_Wk': _L0_attn_in['Wk'], 'L0_attn_Wv': _L0_attn_in['Wv'], 'L0_attn_conv_q': _L0_attn_in['conv_q'], 'L0_attn_conv_k': _L0_attn_in['conv_k'], 'L0_attn_conv_v': _L0_attn_in['conv_v'], 'L0_attn_Wb': _L0_attn_in['Wb'], 'L0_attn_Wmix': _L0_attn_in['Wmix'], 'L0_attn_norm_w': _L0_attn_in['norm_w'], 'L0_attn_Wo': _L0_attn_in['Wo'], 'L0_ffn_router_weight': _L0_ffn_in['router_weight'], 'L0_ffn_gate_up_proj': _L0_ffn_in['gate_up_proj'], 'L0_ffn_gate_up_proj_bias': _L0_ffn_in['gate_up_proj_bias'], 'L0_ffn_down_proj': _L0_ffn_in['down_proj'], 'L0_ffn_down_proj_bias': _L0_ffn_in['down_proj_bias']}

def reference(x, L0_tok_emb, L0_tok_pos_emb, L0_tok_A_diag, L0_tok_B, L0_tok_C, L0_tok_D, L0_tok_w1, L0_tok_b1, L0_tok_w2, L0_tok_b2, L0_tok_ln1_s, L0_tok_ln1_b, L0_tok_ln2_s, L0_tok_ln2_b, L0_tok_lnf_s, L0_tok_lnf_b, L0_attn_Wq, L0_attn_Wk, L0_attn_Wv, L0_attn_conv_q, L0_attn_conv_k, L0_attn_conv_v, L0_attn_Wb, L0_attn_Wmix, L0_attn_norm_w, L0_attn_Wo, L0_ffn_router_weight, L0_ffn_gate_up_proj, L0_ffn_gate_up_proj_bias, L0_ffn_down_proj, L0_ffn_down_proj_bias):
    import jax
    import jax.numpy as jnp

    def _L0_tok_ref(tokens, emb, pos_emb, A_diag, B, C, D, w1, b1, w2, b2, ln1_s, ln1_b, ln2_s, ln2_b, lnf_s, lnf_b):
        import jax, jax.numpy as jnp
        import numpy as np
        EPS = 1e-05

        def layernorm(x, s, b):
            m = jnp.mean(x, axis=-1, keepdims=True)
            v = jnp.mean(jnp.square(x - m), axis=-1, keepdims=True)
            return (x - m) * jax.lax.rsqrt(v + EPS) * s + b

        def ssm(x, a_diag, Bm, Cm, Dm):
            a = jax.nn.sigmoid(a_diag)
            u = jnp.einsum('btd,ds->bts', x, Bm)

            def step(h, u_t):
                h = a * h + u_t
                return (h, h)
            h0 = jnp.zeros((x.shape[0], a.shape[0]), x.dtype)
            _, H = jax.lax.scan(step, h0, jnp.swapaxes(u, 0, 1))
            H = jnp.swapaxes(H, 0, 1)
            return jnp.einsum('bts,sd->btd', H, Cm) + jnp.einsum('btd,de->bte', x, Dm)
        T = tokens.shape[1]
        x = emb[tokens] + pos_emb[:T][None]
        L = A_diag.shape[0]
        for l in range(L):
            x = x + ssm(layernorm(x, ln1_s[l], ln1_b[l]), A_diag[l], B[l], C[l], D[l])
            h = layernorm(x, ln2_s[l], ln2_b[l])
            h = jax.nn.gelu(jnp.einsum('btd,df->btf', h, w1[l]) + b1[l], approximate=False)
            x = x + jnp.einsum('btf,fd->btd', h, w2[l]) + b2[l]
        return layernorm(x, lnf_s, lnf_b)

    def _L0_attn_ref(hidden_states, Wq, Wk, Wv, conv_q, conv_k, conv_v, Wb, Wmix, norm_w, Wo):
        import jax, jax.numpy as jnp
        import numpy as np
        CHUNK = 32
        NUM_HEADS = 4
        HEAD_K = 64
        HEAD_V = 64
        EPS = 1e-05

        def l2norm(x, eps=1e-06):
            return x * jax.lax.rsqrt(jnp.sum(x * x, axis=-1, keepdims=True) + eps)

        def causal_depthwise_conv(x, w):
            K = w.shape[1]
            l = x.shape[1]
            xp = jnp.pad(x, ((0, 0), (K - 1, 0), (0, 0)))
            return sum((w[:, k] * xp[:, k:k + l, :] for k in range(K)))

        def delta_rule_chunkwise(q, k, v, beta):
            b, h, l, dk = q.shape
            dv = v.shape[-1]
            c = CHUNK
            n = l // c
            q = l2norm(q)
            k = l2norm(k)
            v = v * beta[..., None]
            k_beta = k * beta[..., None]
            resh = lambda x: x.reshape(b, h, n, c, x.shape[-1])
            q, k, v, k_beta = map(resh, (q, k, v, k_beta))
            tri_strict = jnp.tril(jnp.ones((c, c), dtype=q.dtype), -1)
            attn = -(k_beta @ jnp.swapaxes(k, -1, -2)) * tri_strict

            def body(i, a):
                row = a[..., i, :]
                upd = jnp.einsum('bhnj,bhnjk->bhnk', row, a)
                return a.at[..., i, :].add(upd)
            attn = jax.lax.fori_loop(1, c, body, attn)
            attn = attn + jnp.eye(c, dtype=attn.dtype)
            u = attn @ v
            w = attn @ k_beta
            mask_causal = jnp.tril(jnp.ones((c, c), dtype=q.dtype), 0)
            S0 = jnp.zeros((b, h, dk, dv), dtype=q.dtype)
            to_front = lambda x: jnp.moveaxis(x, 2, 0)

            def step(S, inp):
                q_i, k_i, u_i, w_i = inp
                attn_i = q_i @ jnp.swapaxes(k_i, -1, -2) * mask_causal
                u_new = u_i - w_i @ S
                o_i = q_i @ S + attn_i @ u_new
                S = S + jnp.swapaxes(k_i, -1, -2) @ u_new
                return (S, o_i)
            S, o = jax.lax.scan(step, S0, (to_front(q), to_front(k), to_front(u), to_front(w)))
            o = jnp.moveaxis(o, 0, 2).reshape(b, h, l, dv)
            return (o, S)
        x = hidden_states
        b, l, d = x.shape
        h, dk, dv = (NUM_HEADS, HEAD_K, HEAD_V)
        q = jax.nn.silu(causal_depthwise_conv(x @ Wq.T, conv_q))
        k = jax.nn.silu(causal_depthwise_conv(x @ Wk.T, conv_k))
        v = jax.nn.silu(causal_depthwise_conv(x @ Wv.T, conv_v))
        v_token = v.reshape(b, l, h, dv)
        qh = q.reshape(b, l, h, dk).transpose(0, 2, 1, 3)
        kh = k.reshape(b, l, h, dk).transpose(0, 2, 1, 3)
        vh = v_token.transpose(0, 2, 1, 3)
        beta = jax.nn.sigmoid(x @ Wb.T).transpose(0, 2, 1)
        o, S = delta_rule_chunkwise(qh, kh, vh, beta)
        o = o.transpose(0, 2, 1, 3)
        mix = jax.nn.sigmoid(x @ Wmix.T)[..., None]
        o = mix * o + (1.0 - mix) * v_token
        o = o * jax.lax.rsqrt(jnp.mean(o * o, axis=-1, keepdims=True) + EPS) * norm_w
        o = o.reshape(b, l, h * dv) @ Wo.T
        return o

    def _L0_ffn_ref(hidden_states, router_weight, gate_up_proj, gate_up_proj_bias, down_proj, down_proj_bias):
        import jax, jax.numpy as jnp
        import numpy as np
        B, S, H = (4, 512, 256)
        E, K, INTER = (16, 2, 128)
        ALPHA, LIMIT = (1.702, 7.0)
        b, s, h = hidden_states.shape
        x = hidden_states.reshape(-1, h)
        logits = x @ router_weight
        topk_w, topk_i = jax.lax.top_k(logits, K)
        topk_w = jax.nn.softmax(topk_w, axis=-1)
        one_hot = (topk_i[..., None] == jnp.arange(E)[None, None, :]).astype(topk_w.dtype)
        scores = jnp.einsum('tk,tke->te', topk_w, one_hot)
        gu = jnp.einsum('th,ehf->tef', x, gate_up_proj) + gate_up_proj_bias
        gate = gu[..., ::2]
        up = gu[..., 1::2]
        gate = jnp.minimum(gate, LIMIT)
        up = jnp.clip(up, -LIMIT, LIMIT)
        glu = gate * jax.nn.sigmoid(gate * ALPHA)
        act = (up + 1.0) * glu
        out = jnp.einsum('tei,eih,te->th', act, down_proj, scores)
        out = out + jnp.einsum('te,eh->th', scores, down_proj_bias)
        return out.reshape(b, s, h)
    h = _L0_tok_ref(x, L0_tok_emb, L0_tok_pos_emb, L0_tok_A_diag, L0_tok_B, L0_tok_C, L0_tok_D, L0_tok_w1, L0_tok_b1, L0_tok_w2, L0_tok_b2, L0_tok_ln1_s, L0_tok_ln1_b, L0_tok_ln2_s, L0_tok_ln2_b, L0_tok_lnf_s, L0_tok_lnf_b)
    h = h + _L0_attn_ref(_layernorm(h, axis=-1), L0_attn_Wq, L0_attn_Wk, L0_attn_Wv, L0_attn_conv_q, L0_attn_conv_k, L0_attn_conv_v, L0_attn_Wb, L0_attn_Wmix, L0_attn_norm_w, L0_attn_Wo)
    h = h + _L0_ffn_ref(_layernorm(h, axis=-1), L0_ffn_router_weight, L0_ffn_gate_up_proj, L0_ffn_gate_up_proj_bias, L0_ffn_down_proj, L0_ffn_down_proj_bias)
    return h

_drawn_inputs = setup_inputs


def setup_inputs(seed=0):
    import zlib

    import numpy as np

    out = dict(_drawn_inputs(seed))
    spreads = {'L0_tok_b1': (0.0, 0.1),
     'L0_tok_b2': (0.0, 0.1),
     'L0_tok_ln1_s': (1.0, 0.2),
     'L0_tok_ln1_b': (0.0, 0.1),
     'L0_tok_ln2_s': (1.0, 0.2),
     'L0_tok_ln2_b': (0.0, 0.1),
     'L0_tok_lnf_s': (1.0, 0.2),
     'L0_tok_lnf_b': (0.0, 0.1),
     'L0_attn_norm_w': (1.0, 0.2)}
    factors = {'L0_attn_Wb': 6.003, 'L0_ffn_gate_up_proj_bias': 32.252, 'L0_ffn_down_proj_bias': 4.165}
    for name, (base, spread) in spreads.items():
        noise = np.random.default_rng([zlib.crc32(name.encode()), seed]).standard_normal(out[name].shape)
        drawn = base * np.exp(spread * noise) if base else spread * noise
        out[name] = jnp.asarray(drawn.astype(out[name].dtype))
    for name, factor in factors.items():
        out[name] = (out[name] * factor).astype(out[name].dtype)
    return out
```

```python
from contextlib import ExitStack

import concourse.bass as bass
from concourse import mybir

ALU = mybir.AluOpType
ACT = mybir.ActivationFunctionType
F32 = mybir.dt.float32
F32R = mybir.dt.float32r
F16 = mybir.dt.float16
I32 = mybir.dt.int32
U32 = mybir.dt.uint32
AX = mybir.AxisListType

P = 128
HI, LO = 0, 1
PASSES = ((HI, HI), (HI, LO), (LO, HI))
EPS = 1e-5
L2_EPS = 1e-6


def tower(nc, sems, x, ident, half, lnf_sb, ids, emb, pos, A_diag, Bw, Cw, Dw, w1, w2, b2, cols, lnf):
    V, DM = emb.shape
    NSEQ, T = ids.shape[1], P
    S, L = A_diag.shape
    FF = w1.shape[2]
    GT = 4
    NG = NSEQ // GT
    GN = GT * P
    NH2 = DM // P
    NF = FF // P
    NCOL = cols.shape[2]
    assert GN == 512 and NH2 == 2 and 2 * S == P and NG == 8 and NF == 8

    with ExitStack() as ctx:
        def sb(name, shape, dt=F32):
            return ctx.enter_context(nc.sbuf_tensor(name, shape, dt))

        def sem(name):
            sems.append(nc.alloc_semaphore(name=name))
            return sems[-1]

        def bank(name):
            return ctx.enter_context(nc.psum_tensor(name, [P, 512], F32))

        ids_sb = sb("ids_sb", [P, NSEQ], I32)
        idf = sb("idf", [P, NSEQ])
        idneg = sb("idneg", [P, NSEQ])
        idx = sb("idx", [P, NSEQ], I32)
        pos_sb = sb("pos_sb", [P, DM])
        a_col = sb("a_col", [P, L])
        a_sig = sb("a_sig", [P, L])
        runmask = sb("runmask", [P, GT, T])
        decay = sb("decay", [P, GT, T])
        st_d = sb("st_d", [P, NH2, DM])
        st_b = sb("st_b", [P, NH2, 2, S])
        st_c = sb("st_c", [P, DM])
        st_w1 = sb("st_w1", [P, NH2, FF])
        st_w2 = sb("st_w2", [P, NF, DM])
        st_b2 = sb("st_b2", [P, DM])
        st_cols = sb("st_cols", [P, NCOL])
        d_w = sb("d_w", [P, 2, NH2, DM], F32R)
        b_w = sb("b_w", [P, 2, NH2, P], F32R)
        c_w = sb("c_w", [P, DM], F32R)
        c_t = sb("c_t", [P, DM], F32R)
        w1_w = sb("w1_w", [P, 2, NH2, FF], F32R)
        w2_w = sb("w2_w", [P, 2, NF, DM], F32R)
        b2_bc = sb("b2_bc", [P, DM])
        col = sb("col", [P, NCOL])
        stats = sb("stats", [P, GT, 6])
        mv = sb("mv", [P, GT, 2])
        veps = sb("veps", [P, GT])
        rstd = sb("rstd", [P, GT])
        hn = sb("hn", [P, GT, DM])
        full = sb("full", [P, NH2, GN])
        h1 = sb("h1", [P, 2, NH2, GN], F32R)
        h2 = [sb(f"h2_{i}", [P, 2, NH2, GN], F32R) for i in range(2)]
        hs = sb("hs", [P, GN])
        hs_w = sb("hs_w", [P, 2, GN], F32R)
        gfull = sb("gfull", [P, 2, GN])
        g_w = sb("g_w", [P, 2, 2, GN], F32R)

        TR = [bank(f"TR{i}") for i in range(2)]
        MID = [bank(f"MID{i}") for i in range(2)]
        ACC = [bank(f"ACC{i}") for i in range(2)]
        UY = [bank(f"UY{i}") for i in range(2)]

        ld_ids = sem("ld_ids")
        ld_const = sem("ld_const")
        ids_step = sem("ids_step")
        idx_ready = sem("idx_ready")
        gathered = [sem(f"gathered{g}") for g in range(NG)]
        ident_step = sem("ident_step")
        ident_ready = sem("ident_ready")
        run_step = sem("run_step")
        asig_ready = sem("asig_ready")
        decay_ready = sem("decay_ready")
        ld_ssm = sem("ld_ssm")
        ld_w1 = sem("ld_w1")
        ld_w2 = sem("ld_w2")
        ld_par = sem("ld_par")
        par_ready = sem("par_ready")
        whi_done = sem("whi_done")
        wlo_done = sem("wlo_done")
        bn_done = sem("bn_done")
        mv_done = sem("mv_done")
        veps_done = sem("veps_done")
        rstd_ready = sem("rstd_ready")
        norm_ready = sem("norm_ready")
        tr_done = sem("tr_done")
        evac_done = sem("evac_done")
        lo_done = sem("lo_done")
        u_done = sem("u_done")
        scan_done = sem("scan_done")
        hshi_done = sem("hshi_done")
        hslo_done = sem("hslo_done")
        y_done = sem("y_done")
        xupd_done = sem("xupd_done")
        b2_done = sem("b2_done")
        up_done = sem("up_done")
        gelu_done = sem("gelu_done")
        glo_done = sem("glo_done")
        down_done = sem("down_done")
        x_ready = sem("x_ready")

        w1_d = w1.rearrange("l (h p) f -> l p h f", p=P)
        w2_d = w2.rearrange("l (f p) d -> l p f d", p=P)
        d_d = Dw.rearrange("l (h p) e -> l p h e", p=P)
        b_d = Bw.rearrange("l (h p) s -> l p h s", p=P)

        def at(ap, l):
            return ap[bass.ds(l, 1)].rearrange("o p h f -> (o p) h f")

        def xg(g):
            return x[:, bass.ds(g * GT, GT), :]

        primed = (b2_done, down_done, evac_done, gelu_done, glo_done, hshi_done, hslo_done, lo_done, mv_done,
                  norm_ready, par_ready, scan_done, tr_done, up_done, wlo_done, xupd_done, y_done)
        block = ctx.enter_context(nc.Block())

        @block.sync
        def _(sp):
            for s in primed:
                sp.sem_inc(s, 1)
            sp.dma_start(ids_sb[:], ids).then_inc(ld_ids, 16)
            sp.dma_start(pos_sb[:], pos[0:P, :]).then_inc(ld_const, 16)
            for i in range(2):
                sp.dma_start(a_col[S * i:S * i + S, :], A_diag).then_inc(ld_const, 16)
                sp.dma_start(lnf_sb[:, i, :], lnf[i:i + 1, :].partition_broadcast(P)).then_inc(ld_const, 16)
            with sp.Fori(0, L) as l:
                sp.wait_ge(wlo_done, 1 + l * 4)
                sp.wait_ge(par_ready, 1 + l * 2)
                sp.dma_start(st_d[:], at(d_d, l)).then_inc(ld_ssm, 16)
                for i in range(2):
                    sp.dma_start(st_b[:, :, i, :], at(b_d, l)).then_inc(ld_ssm, 16)
                    sp.dma_start(st_c[S * i:S * i + S, :], Cw[bass.ds(l, 1)].rearrange("o s d -> (o s) d")).then_inc(ld_ssm, 16)
                sp.dma_start(st_cols[:], cols[bass.ds(l, 1)].rearrange("o p c -> (o p) c")).then_inc(ld_par, 16)
                sp.dma_start(st_b2[:], b2[bass.ds(l, 1), :].partition_broadcast(P)).then_inc(ld_par, 16)
                sp.dma_start(st_w1[:], at(w1_d, l)).then_inc(ld_w1, 16)
                sp.dma_start(st_w2[:], at(w2_d, l)).then_inc(ld_w2, 16)

        @block.gpsimd
        def _(pool):
            def ln_rstd(n):
                pool.wait_ge(mv_done, 1 + n * GT + GT)
                pool.nop(nofuse=True)
                pool.wait_ge(norm_ready, 1 + n * GT)
                pool.nop(nofuse=True)
                pool.tensor_scalar(veps[:], mv[:, :, 1], EPS, None, ALU.add).then_inc(veps_done, 1)
                pool.wait_ge(veps_done, n + 2)
                pool.tensor_tensor(rstd[:], veps[:], half[:].to_broadcast([P, GT]), ALU.pow).then_inc(rstd_ready, 1)

            def pool_unit(k, g, last=False):
                if not last:
                    ln_rstd(2 * k + 1)
                n2 = 2 * k + 2 - last
                ln_rstd(n2)
                if True:
                    pool.wait_ge(norm_ready, 1 + n2 * GT + GT)
                    pool.tensor_tensor(xg(g), xg(g), b2_bc[:].unsqueeze(1).to_broadcast([P, GT, DM]), ALU.add).then_inc(b2_done, 1)

            pool.memset(half[:], -0.5).then_inc(veps_done, 1)
            pool.memset(ident[:], 0.0).then_inc(ident_step, 1)
            pool.memset(runmask[:], 1.0).then_inc(run_step, 1)
            pool.wait_ge(ident_step, 1)
            pool.affine_select(out=ident[:], in_=ident[:], compare_op=ALU.not_equal, fill=1.0, base=0,
                               pattern=[[-1, P]], channel_multiplier=1).then_inc(ident_ready, 1)
            pool.wait_ge(run_step, 1)
            pool.memset(runmask[:, :, 0:1], 0.0).then_inc(run_step, 1)
            pool.wait_ge(idx_ready, 1)
            for s in range(NSEQ):
                pool.indirect_dma_start(x[:, s, :], None, emb, bass.IndirectOffsetOnAxis(ap=idx[:, s:s + 1], axis=0))\
                    .then_inc(gathered[s // GT], 16)
            with pool.Fori(0, L) as l:
                pool.wait_ge(ld_par, l * 32 + 32)
                pool.wait_ge(gelu_done, 1 + l * (2 * NF * NG) + 2)
                pool.nop(nofuse=True)
                pool.tensor_copy(col[:], st_cols[:]).then_inc(par_ready, 1)
                pool.wait_ge(b2_done, 1 + l * NG)
                pool.nop(nofuse=True)
                pool.tensor_copy(b2_bc[:], st_b2[:]).then_inc(par_ready, 1)
                pool.wait_ge(par_ready, 1 + l * 2 + 2)
                ln_rstd(l * (2 * NG))
                with pool.Fori(0, NG - 1) as g:
                    pool_unit(l * NG + g, g)
                pool_unit(l * NG + NG - 1, NG - 1, last=True)

        @block.scalar
        def _(act):
            def evac(n, k, w, dst, halves=(0, 1)):
                for h in halves:
                    act.wait_ge(tr_done, 1 + n * 2 + h + 1)
                    if w == 0:
                        act.wait_ge(y_done, 1 + k * 2)
                    else:
                        act.wait_ge(up_done, 1 + k * NF)
                    act.wait_ge(lo_done, 1 + n * 2)
                    sc, bi = col[:, 4 * w + h:4 * w + h + 1], col[:, 4 * w + 2 + h:4 * w + 3 + h]
                    act.activation(dst[:, HI, h, :], TR[h][:], ACT.Identity, scale=sc, bias=bi).then_inc(evac_done, 1)
                    act.activation(full[:, h, :], TR[h][:], ACT.Identity, scale=sc, bias=bi).then_inc(evac_done, 1)

            def ssm_act(k, s, par, last=False):
                if s in (6, 7) and not last:
                    evac(2 * k + 1, k + 1, 0, h1, (s - 6,))
                elif s == 2:
                    act.wait_ge(scan_done, 1 + k + 1)
                    act.wait_ge(y_done, 1 + k * 2)
                    act.activation(hs_w[:, HI, :], hs[:], ACT.Copy).then_inc(hshi_done, 1)
                elif s == 8:
                    evac(2 * k + 2 - last, k, 1, h2[par])

            def gelu(k, f):
                m = f % 2
                act.wait_ge(up_done, 1 + k * NF + f + 1 + NF)
                act.wait_ge(down_done, 1 + k * NF + f)
                act.wait_ge(glo_done, 1 + k * NF + f)
                act.activation(g_w[:, m, HI, :], MID[m][:], ACT.Gelu, bias=col[:, 8 + f:9 + f]).then_inc(gelu_done, 1)
                act.activation(gfull[:, m, :], MID[m][:], ACT.Gelu, bias=col[:, 8 + f:9 + f]).then_inc(gelu_done, 1)

            act.sem_inc(gelu_done, 2)
            act.wait_ge(ld_const, 80)
            act.activation(a_sig[:], a_col[:], ACT.Sigmoid).then_inc(asig_ready, 1)
            act.wait_ge(asig_ready, 1)
            act.activation(a_col[:, 0:1], a_sig[:, 0:1], ACT.Gelu).then_inc(asig_ready, 1)
            with act.Fori(0, L) as l:
                act.wait_ge(ld_ssm, l * 80 + 80)
                act.wait_ge(y_done, 1 + l * (2 * NG))
                act.activation(d_w[:, HI], st_d[:], ACT.Copy).then_inc(whi_done, 1)
                act.activation(b_w[:, HI], st_b[:].rearrange("p h i s -> p h (i s)"), ACT.Copy).then_inc(whi_done, 1)
                act.activation(c_w[0:S, :], st_c[0:S, :], ACT.Copy).then_inc(whi_done, 1)
                act.activation(c_t[S:P, :], st_c[S:P, :], ACT.Copy).then_inc(whi_done, 1)
                act.wait_ge(down_done, 1 + l * (NG * NF) + 1)
                act.wait_ge(ld_w1, l * 16 + 16)
                act.activation(w1_w[:, HI], st_w1[:], ACT.Copy).then_inc(whi_done, 1)
                act.wait_ge(ld_w2, l * 16 + 16)
                act.activation(w2_w[:, HI], st_w2[:], ACT.Copy).then_inc(whi_done, 1)
                act.wait_ge(par_ready, 1 + l * 2 + 2)
                evac(l * (2 * NG), l * NG, 0, h1)
                for s in range(9):
                    ssm_act(l * NG, s, 0)
                def unit(k, par, last=False):
                    for f in range(9):
                        if f < NF:
                            gelu(k - 1, f)
                        ssm_act(k, f, par, last)
                with act.Fori(0, (NG - 2) // 2) as i:
                    unit(l * NG + i * 2 + 1, 1)
                    unit(l * NG + i * 2 + 2, 0)
                unit(l * NG + NG - 1, 1, last=True)
                for f in range(NF):
                    gelu(l * NG + NG - 1, f)

        @block.vector
        def _(dve):
            def ln_stats(n, g, ready, count):
                dve.wait_ge(ready, count)
                dve.wait_ge(mv_done, 1 + n * GT)
                dve.nop(nofuse=True)
                for t in range(GT):
                    dve.bn_stats(stats[:, t, :], x[:, bass.ds(g * GT + t, 1), :]).then_inc(bn_done, 1)
                dve.wait_ge(bn_done, n * GT + GT)
                dve.nop(nofuse=True)
                dve.wait_ge(norm_ready, 1 + n * GT)
                dve.nop(nofuse=True)
                for t in range(GT):
                    dve.bn_aggr(mv[:, t, :], stats[:, t, :]).then_inc(mv_done, 1)

            def ln_norm(n, g):
                dve.wait_ge(rstd_ready, n + 1)
                dve.wait_ge(tr_done, 1 + n * 2)
                for t in range(GT):
                    dve.tensor_scalar(hn[:, t, :], x[:, bass.ds(g * GT + t, 1), :], mv[:, t, 0:1], rstd[:, t:t + 1],
                                      ALU.subtract, ALU.mult).then_inc(norm_ready, 1)

            def lows(n, dst, halves=(0, 1)):
                for h in halves:
                    dve.wait_ge(evac_done, 1 + n * 4 + 2 * h + 2)
                    dve.tensor_tensor(dst[:, LO, h, :], full[:, h, :], dst[:, HI, h, :].bitcast(F32), ALU.subtract)\
                        .then_inc(lo_done, 1)

            def ssm_dve(k, g, s, par, last=False):
                n1, n2 = 2 * k + 1, 2 * k + 2 - last
                if s == 2:
                    dve.wait_ge(u_done, k + 1)
                    dve.wait_ge(hshi_done, 1 + k)
                    dve.wait_ge(hslo_done, 1 + k)
                    dve.tensor_tensor_scan(hs[:], decay[:].rearrange("p g t -> p (g t)"), UY[0][:], 0.0, ALU.mult, ALU.add)\
                        .then_inc(scan_done, 1)
                    dve.wait_ge(hshi_done, 1 + k + 1)
                    dve.tensor_tensor(hs_w[:, LO, :], hs[:], hs_w[:, HI, :].bitcast(F32), ALU.subtract).then_inc(hslo_done, 1)
                if s == 3 and not last:
                    ln_stats(n1, g + 1, x_ready, 2 * k + 4)
                if s == 4:
                    x_update(k, g, 0)
                if s == 5:
                    if not last:
                        ln_norm(n1, g + 1)
                    x_update(k, g, 1)
                    ln_stats(n2, g, xupd_done, 1 + 2 * k + 2)
                if s == 6:
                    if not last:
                        lows(n1, h1, (0,))
                    ln_norm(n2, g)
                if s == 7 and not last:
                    lows(n1, h1, (1,))
                if s == 8:
                    lows(n2, h2[par])

            def x_update(k, g, j):
                dve.wait_ge(y_done, 1 + k * 2 + j + 1)
                xx = x[:, bass.ds(g * GT + 2 * j, 2), :]
                dve.tensor_tensor(xx, xx, UY[j][:].rearrange("p (a d) -> p a d", a=2), ALU.add).then_inc(xupd_done, 1)

            def glo(k, f):
                m = f % 2
                dve.wait_ge(gelu_done, 1 + 2 * (k * NF + f) + 4)
                dve.tensor_tensor(g_w[:, m, LO, :], gfull[:, m, :], g_w[:, m, HI, :].bitcast(F32), ALU.subtract)\
                    .then_inc(glo_done, 1)

            def mlp_add(k, g):
                dve.wait_ge(down_done, 1 + k * NF + NF + 1)
                dve.wait_ge(b2_done, 1 + k + 1)
                for j in range(2):
                    xx = x[:, bass.ds(g * GT + 2 * j, 2), :]
                    dve.tensor_tensor(xx, xx, ACC[j][:].rearrange("p (a d) -> p a d", a=2), ALU.add).then_inc(x_ready, 1)

            dve.sem_inc(glo_done, 1)
            dve.wait_ge(ld_ids, 16)
            dve.tensor_copy(idf[:], ids_sb[:]).then_inc(ids_step, 1)
            dve.wait_ge(ids_step, 1)
            dve.tensor_scalar(idneg[:], idf[:], 0.0, float(V), ALU.is_lt, ALU.mult).then_inc(ids_step, 1)
            dve.wait_ge(ids_step, 2)
            dve.tensor_tensor(idneg[:], idneg[:], idf[:], ALU.add).then_inc(ids_step, 1)
            dve.wait_ge(ids_step, 3)
            dve.tensor_scalar(idx[:], idneg[:], 0.0, float(V - 1), ALU.max, ALU.min).then_inc(idx_ready, 1)
            dve.wait_ge(ld_const, 80)
            for g in range(NG):
                dve.wait_ge(gathered[g], 16 * GT)
                for j in range(2):
                    xx = x[:, g * GT + 2 * j:g * GT + 2 * j + 2, :]
                    dve.tensor_tensor(xx, xx, pos_sb[:].unsqueeze(1).to_broadcast([P, 2, DM]), ALU.add).then_inc(x_ready, 1)
            dve.wait_ge(asig_ready, 2)
            dve.wait_ge(run_step, 2)
            with dve.Fori(0, L) as l:
                dve.wait_ge(scan_done, 1 + l * NG)
                dve.tensor_scalar(decay[:], runmask[:], a_sig[:, bass.ds(l, 1)], None, ALU.mult).then_inc(decay_ready, 1)
                dve.wait_ge(decay_ready, l + 1)
                ln_stats(l * (2 * NG), 0, x_ready, l * (2 * NG) + 2)
                ln_norm(l * (2 * NG), 0)
                dve.wait_ge(whi_done, l * 6 + 4)
                dve.tensor_tensor(d_w[:, LO], st_d[:], d_w[:, HI].bitcast(F32), ALU.subtract).then_inc(wlo_done, 1)
                dve.tensor_tensor(b_w[:, LO], st_b[:].rearrange("p h i s -> p h (i s)"), b_w[:, HI].bitcast(F32), ALU.subtract)
                dve.tensor_tensor(c_w[S:P, :], st_c[S:P, :], c_t[S:P, :].bitcast(F32), ALU.subtract).then_inc(wlo_done, 1)
                lows(l * (2 * NG), h1)
                for s in range(1, 9):
                    ssm_dve(l * NG, 0, s, 0)
                    if s == 2:
                        dve.wait_ge(whi_done, l * 6 + 5)
                        dve.tensor_tensor(w1_w[:, LO], st_w1[:], w1_w[:, HI].bitcast(F32), ALU.subtract).then_inc(wlo_done, 1)
                    if s == 4:
                        dve.wait_ge(whi_done, l * 6 + 6)
                        dve.tensor_tensor(w2_w[:, LO], st_w2[:], w2_w[:, HI].bitcast(F32), ALU.subtract).then_inc(wlo_done, 1)
                def unit(k, g, par, last=False):
                    for f in range(9):
                        if f < NF:
                            glo(k - 1, f)
                        ssm_dve(k, g, f, par, last)
                    mlp_add(k - 1, g - 1)
                with dve.Fori(0, (NG - 2) // 2) as i:
                    unit(l * NG + i * 2 + 1, i * 2 + 1, 1)
                    unit(l * NG + i * 2 + 2, i * 2 + 2, 0)
                unit(l * NG + NG - 1, NG - 1, 1, last=True)
                for f in range(NF):
                    glo(l * NG + NG - 1, f)
                mlp_add(l * NG + NG - 1, NG - 1)

        @block.tensor
        def _(pe):
            def transposes(n):
                pe.wait_ge(norm_ready, 1 + n * GT + GT)
                pe.wait_ge(evac_done, 1 + n * 4)
                for h in range(2):
                    for t in range(GT):
                        last = pe.transpose(TR[h][:, t * P:(t + 1) * P], hn[:, t, h * P:(h + 1) * P], ident[:])
                    last.then_inc(tr_done, 1)

            def ssm_pe(k, s, first=False, last=False):
                if s == 1:
                    n1 = 2 * k - 1 + first
                    pe.wait_ge(lo_done, 1 + n1 * 2 + 2)
                    pe.wait_ge(xupd_done, 1 + k * 2)
                    for i, (h, (a, b)) in enumerate([(h, p) for h in range(2) for p in PASSES]):
                        last = pe.matmul(UY[0][:], b_w[:, a, h, :], h1[:, b, h, :], start=(i == 0), stop=(i == 5))
                    last.then_inc(u_done, 1)
                if s in (3, 4):
                    j = s - 3
                    pe.wait_ge(hslo_done, 1 + k + 1)
                    for t in range(2 * j, 2 * j + 2):
                        o = UY[j][:, (t % 2) * DM:(t % 2 + 1) * DM]
                        tok = slice(t * P, (t + 1) * P)
                        pe.matmul(o, hs_w[:, HI, tok], c_w[:], start=True, stop=False)
                        pe.matmul(o, hs_w[:, LO, tok], c_w[:], start=False, stop=False)
                        for i, (h, (a, b)) in enumerate([(h, p) for h in range(2) for p in PASSES]):
                            last_mm = pe.matmul(o, h1[:, a, h, tok], d_w[:, b, h, :], start=False, stop=(i == 5))
                    last_mm.then_inc(y_done, 1)
                if s == 5 and not last:
                    transposes(2 * k + 1)
                if s == 7:
                    transposes(2 * k + 2 - last)

            def up(k, f, par, last=False):
                m = f % 2
                if f == 0:
                    n2 = 2 * k + 2 - last
                    pe.wait_ge(lo_done, 1 + n2 * 2 + 2)
                pe.wait_ge(gelu_done, 1 + 2 * (k * NF + f))
                fs = slice(f * P, (f + 1) * P)
                for i, (h, (a, b)) in enumerate([(h, p) for h in range(2) for p in PASSES]):
                    last = pe.matmul(MID[m][:], w1_w[:, a, h, fs], h2[par][:, b, h, :], start=(i == 0), stop=(i == 5))
                last.then_inc(up_done, 1)

            def down(k, f):
                m = f % 2
                if f == 0:
                    pe.wait_ge(x_ready, 2 * k + 2 * NG)
                pe.wait_ge(glo_done, 1 + k * NF + f + 2)
                for t in range(GT):
                    o = ACC[t // 2][:, (t % 2) * DM:(t % 2 + 1) * DM]
                    tok = slice(t * P, (t + 1) * P)
                    for i, (a, b) in enumerate(PASSES):
                        last = pe.matmul(o, g_w[:, m, a, tok], w2_w[:, b, f, :], start=(f == 0 and i == 0 and t % 2 == 0),
                                         stop=(f == NF - 1 and i == 2), skip_group_check=True)
                last.then_inc(down_done, 1)

            pe.sem_inc(up_done, NF)
            pe.sem_inc(down_done, 1)
            pe.wait_ge(ident_ready, 1)
            with pe.Fori(0, L) as l:
                transposes(l * (2 * NG))
                pe.wait_ge(wlo_done, 1 + l * 4 + 2)
                for s in range(9):
                    ssm_pe(l * NG, s, first=True)
                pe.wait_ge(wlo_done, 1 + l * 4 + 4)
                pe.nop(nofuse=True)

                def unit(k, par, last=False):
                    for f in range(9):
                        if f < NF:
                            up(k - 1, f, 1 - par)
                        if f >= 1:
                            down(k - 1, f - 1)
                        ssm_pe(k, f, last=last)
                with pe.Fori(0, (NG - 2) // 2) as i:
                    unit(l * NG + i * 2 + 1, 1)
                    unit(l * NG + i * 2 + 2, 0)
                unit(l * NG + NG - 1, 1, last=True)
                for f in range(9):
                    if f < NF:
                        up(l * NG + NG - 1, f, 1, last=True)
                    if f >= 1:
                        down(l * NG + NG - 1, f - 1)


def attention(nc, sems, x, ident, half, lnf_sb, wqkv, wbm, wo, conv, norm_w, scr_g, scr_b, scr_t):
    NSEQ, DM = x.shape[1], x.shape[2]
    GT = 4
    NG = NSEQ // GT
    GN = GT * P
    NH2 = DM // P
    HD = 64
    NHD = DM // HD
    NQ = GT * NHD
    C = 32
    NC = P // C
    NCH = 3 * NH2
    NB = NG // 2

    with ExitStack() as ctx:
        def sb(name, shape, dt=F32):
            return ctx.enter_context(nc.sbuf_tensor(name, shape, dt))

        def sem(name):
            return sems.enter_context(nc.semaphore(name))

        bk = [ctx.enter_context(nc.psum_tensor(f"bk{i}", [P, 512], F32)) for i in range(8)]
        TR, QKV, TOK, VT, BACK = bk[0:2], bk[2:4], bk[4:6], bk[6], bk[7]

        st_bm = sb("st_bm", [P, NH2, 2 * NHD])
        qkv_w = sb("qkv_w", [P, 2, NH2, 3 * DM], F32R)
        bm_w = sb("bm_w", [P, 2, NH2, P], F32R)
        bm_z = sb("bm_z", [P, 2, NH2, P])
        wo_w = sb("wo_w", [P, 2, NH2, DM], F32R)
        cw = sb("cw", [P, NCH, 4])
        nw = sb("nw", [P, 1])
        causal = sb("causal", [P, 2, P])
        strict = sb("strict", [P, C, C])
        tcm = sb("tcm", [P, C, C])

        stats = sb("stats2", [P, GT, 6])
        mv = sb("mv2", [P, GT, 2])
        veps = sb("veps2", [P, GT])
        rstd = sb("rstd2", [P, GT])
        hn = sb("hn2", [P, GT, DM])
        a_w = sb("a_w", [P, 2, NH2, GN], F32R)
        bmT = sb("bmT", [2 * NHD, GN])
        bm = sb("bm", [P, 2 * GT, 2 * NHD])
        cv = sb("cv", [P, 2, GN])
        sg = sb("sg", [P, 2, GN])
        qkv_t = sb("qkv_t", [P, NCH, GN])
        sq = sb("sq", [P, 2, GN])
        ss = sb("ss", [P, GT, 2 * NHD])
        sse = sb("sse", [P, GT, 2 * NHD])
        rs = sb("rs", [P, GT, 2 * NHD])
        qkn = sb("qkn", [P, 2, GN])
        qk_w = sb("qk_w", [P, 2, GT, 4, P], F16)
        v = sb("v", [P, 2 * GT, DM])
        graw = sb("graw", [P, NQ, P])
        st_qkv = graw[:].rearrange("p q t -> p (q t)")[:, 0:NH2 * 3 * DM].rearrange("p (h c) -> p h c", h=NH2)
        g_w = sb("g_w2", [P, 2, 2, NQ, P], F16)
        kq = sb("kq", [P, 2, 2, P])
        kq_w = sb("kq_w", [P, 2, 2, NQ, P], F16)
        gcm = sb("gcm", [P, C, C])
        bcm = sb("bcm", [P, C])
        acm = sb("acm", [P, C, C])
        prod = sb("prod", [P, C * C])
        scm = sb("scm", [P, C, C])
        t_w = sb("t_w", [P, C, 2, C], F16)
        tt = sb("tt", [P, 2 * NQ, 2, C], F16)
        r = sb("r", [P, NQ, HD])
        st_wo = r[:].rearrange("p q d -> p (q d)")[:, 0:NH2 * DM].rearrange("p (h c) -> p h c", h=NH2)
        r_w = sb("r_w", [P, 2, NQ, HD], F16)
        u_w = sb("u_w", [P, 2, NQ, HD], F16)
        om = qkv_t[:, 0:2, :].rearrange("p c n -> p (c n)").rearrange("p (t d) -> p t d", t=GT)
        vm = qkv_t[:, 2:4, :].rearrange("p c n -> p (c n)").rearrange("p (t d) -> p t d", t=GT)
        omix = sb("omix", [P, GT, NHD])
        full = sb("full2", [P, NH2, GN])

        names = """ld_w whi wlo masks bmz m_bn m_mv m_veps m_rstd m_norm fin1 fin2 tr_done a_hi a_lo
        bmT_done bm_sig bm_tr bm_done beta_out qkv_done tap0 conv_done sig_done silu_done tok_done v_tr v_done
        sq_done ss_done sse_done rs_done qkn_done back_done qk_hi qk_lo gk_done graw_done kq_done kq_hi kq_lo
        g_hi g_lo g_out gcm_in ps_r a_step t_hi t_lo t_out tt_in ps1 r_done r_hi r_lo ps2 u_hi u_lo o_done
        om1 vm1 omix1 osq oss osse ors o3 otr o_hi o_full o_lo wo_done x_out""".split()
        S = {n: sem("a_" + n) for n in names}

        xg = lambda g: x[:, bass.ds(g * GT, GT), :]
        primed = """a_lo a_step beta_out bm_tr g_out gcm_in gk_done kq_lo m_mv m_norm o3 o_done o_lo om1 ors otr qk_lo
        qkn_done qkv_done rs_done silu_done t_hi tok_done tr_done u_lo v_tr vm1 x_out""".split()
        block = ctx.enter_context(nc.Block())

        @block.sync
        def _(sp):
            for n in primed:
                sp.sem_inc(S[n], 1)
            sp.dma_start(st_qkv, wqkv.rearrange("(h p) c -> p h c", p=P)).then_inc(S["ld_w"], 16)
            sp.dma_start(st_bm[:], wbm.rearrange("(h p) c -> p h c", p=P)).then_inc(S["ld_w"], 16)
            sp.dma_start(st_wo, wo.rearrange("(h p) c -> p h c", p=P)).then_inc(S["ld_w"], 16)
            sp.dma_start(cw[:], conv.rearrange("(c p) k -> p c k", p=P)).then_inc(S["ld_w"], 16)
            sp.dma_start(nw[:], norm_w).then_inc(S["ld_w"], 16)
            scr_b_v = scr_b.rearrange("(b s h) t -> h b s t", b=2, h=NHD)
            with sp.Fori(0, NB) as b:
                for gi in range(2):
                    m = b * 2 + gi
                    sp.wait_ge(S["bm_sig"], m + 1)
                    sp.wait_ge(S["gcm_in"], 1 + b * 32)
                    sp.dma_start(scr_b_v[:, gi], bmT[0:NHD, :].rearrange("h (s t) -> h s t", s=GT)).then_inc(S["beta_out"], 16)
                    sp.wait_ge(S["graw_done"], m * 8 + 8)
                    for n in range(NC):
                        src = graw[C * n:C * n + C, :, C * n:C * n + C]
                        dst = scr_g.rearrange("(g q n) i j -> g n i q j", g=2, n=NC)[gi, n]
                        sp.dma_start(dst, src).then_inc(S["g_out"], 16)
                sp.wait_ge(S["g_out"], 1 + b * 128 + 128)
                sp.nop(nofuse=True)
                sp.wait_ge(S["beta_out"], 1 + b * 32 + 32)
                sp.wait_ge(S["a_step"], 1 + b * 3)
                sp.dma_start(gcm[:], scr_g).then_inc(S["gcm_in"], 16)
                sp.dma_start(bcm[:], scr_b.rearrange("q (n i) -> (q n) i", n=NC)).then_inc(S["gcm_in"], 16)
                sp.wait_ge(S["t_lo"], b + 1)
                sp.dma_start(scr_t, t_w[:].rearrange("p j s i -> p j (s i)")).then_inc(S["t_out"], 16)
                sp.wait_ge(S["t_out"], b * 16 + 16)
                sp.nop(nofuse=True)
                sp.wait_ge(S["u_lo"], 1 + b * 16)
                for n in range(NC):
                    sp.dma_start(tt[C * n:C * n + C].rearrange("j q s i -> j q (s i)"),
                                 scr_t.rearrange("(q n) j x -> n j q x", n=NC)[n]).then_inc(S["tt_in"], 16)

        @block.gpsimd
        def _(pool):
            def rstd_of(n):
                pool.wait_ge(S["m_mv"], 1 + n * GT + GT)
                pool.nop(nofuse=True)
                pool.wait_ge(S["m_norm"], 1 + n * GT)
                pool.nop(nofuse=True)
                pool.tensor_scalar(veps[:], mv[:, :, 1], EPS, None, ALU.add).then_inc(S["m_veps"], 1)
                pool.wait_ge(S["m_veps"], n + 1)
                pool.tensor_tensor(rstd[:], veps[:], half[:].to_broadcast([P, GT]), ALU.pow).then_inc(S["m_rstd"], 1)

            pool.memset(bm_z[:], 0.0).then_inc(S["bmz"], 1)
            pool.memset(causal[:], 1.0).then_inc(S["masks"], 1)
            pool.memset(strict[:], -1.0).then_inc(S["masks"], 1)
            pool.memset(tcm[:], 0.0).then_inc(S["masks"], 1)
            pool.wait_ge(S["masks"], 3)
            pool.affine_select(out=causal[:], in_=causal[:], compare_op=ALU.is_ge, fill=0.0, base=0,
                               pattern=[[0, 2], [1, P]], channel_multiplier=-1).then_inc(S["masks"], 1)
            pool.affine_select(out=strict[:], in_=strict[:], compare_op=ALU.is_gt, fill=0.0, base=0,
                               pattern=[[1, C], [-1, C]], channel_multiplier=0).then_inc(S["masks"], 1)
            pool.affine_select(out=tcm[:], in_=tcm[:], compare_op=ALU.not_equal, fill=1.0, base=0,
                               pattern=[[1, C], [-1, C]], channel_multiplier=0).then_inc(S["masks"], 1)
            with pool.Fori(0, NB) as b:
                pool.wait_ge(S["x_out"], 1 + b * 4)
                for gi in range(2):
                    m = b * 2 + gi
                    rstd_of(2 * m)
                    rstd_of(2 * m + 1)
                    for c in range(NCH):
                        pool.wait_ge(S["sig_done"], m * NCH + c + 1)
                        pool.wait_ge(S["tok_done"], 1 + m * 4)
                        pool.wait_ge(S["v_tr"], 1 + m * 2)
                        pool.tensor_tensor(qkv_t[:, c, :], cv[:, c % 2, :], sg[:, c % 2, :], ALU.mult).then_inc(S["silu_done"], 1)
                    for t in range(GT):
                        pool.wait_ge(S["ss_done"], m * GT + t + 1)
                        pool.nop(nofuse=True)
                        pool.wait_ge(S["rs_done"], 1 + m * GT + t)
                        pool.nop(nofuse=True)
                        pool.tensor_scalar(sse[:, t, :], ss[:, t, :], L2_EPS, None, ALU.add).then_inc(S["sse_done"], 1)
                        pool.wait_ge(S["sse_done"], m * GT + t + 1)
                        pool.wait_ge(S["qkn_done"], 1 + m * GT)
                        pool.tensor_tensor(rs[:, t, :], sse[:, t, :], half[:].to_broadcast([P, 2 * NHD]), ALU.pow).then_inc(S["rs_done"], 1)
                    for j in range(8):
                        q2 = slice(4 * (j // 2) + j % 2, 4 * (j // 2) + 4, 2)
                        pool.wait_ge(S["kq_hi"], m * 8 + j + 1)
                        pool.tensor_tensor(kq_w[:, gi, LO, q2, :], kq[:, j % 2], kq_w[:, gi, HI, q2, :], ALU.subtract).then_inc(S["kq_lo"], 1)
                        pool.wait_ge(S["g_hi"], m * 8 + j + 1)
                        pool.tensor_tensor(g_w[:, gi, LO, q2, :], graw[:, q2, :], g_w[:, gi, HI, q2, :], ALU.subtract).then_inc(S["g_lo"], 1)
                for gi in range(2):
                    m = b * 2 + gi
                    pool.wait_ge(S["omix1"], m + 1)
                    pool.wait_ge(S["o3"], 1 + m)
                    pool.tensor_tensor(vm.rearrange("p t (h d) -> p t h d", h=NHD), v[:, gi * GT:gi * GT + GT, :].rearrange("p t (h d) -> p t h d", h=NHD),
                                       omix[:].unsqueeze(3).to_broadcast([P, GT, NHD, HD]), ALU.mult).then_inc(S["vm1"], 1)
                    pool.wait_ge(S["oss"], m + 1)
                    pool.nop(nofuse=True)
                    pool.tensor_scalar(sse[:, :, 0:NHD], ss[:, :, 0:NHD], 1.0 / HD, EPS, ALU.mult, ALU.add).then_inc(S["osse"], 1)
                    pool.wait_ge(S["osse"], m + 1)
                    pool.tensor_tensor(rs[:, :, 0:NHD], sse[:, :, 0:NHD], half[:].unsqueeze(2).to_broadcast([P, GT, NHD]), ALU.pow).then_inc(S["ors"], 1)

        @block.scalar
        def _(act):
            def hi_qk(m, t):
                act.wait_ge(S["back_done"], m * GT + t + 1)
                act.wait_ge(S["gk_done"], 1 + m * 8)
                act.activation(qk_w[:, HI, t], BACK[:].rearrange("p (c t) -> p c t", c=4), ACT.Copy).then_inc(S["qk_hi"], 1)

            act.wait_ge(S["ld_w"], 80)
            act.activation(qkv_w[:, HI], st_qkv, ACT.Copy).then_inc(S["whi"], 1)
            act.wait_ge(S["bmz"], 2)
            act.activation(bm_w[:, HI], bm_z[:, 0], ACT.Copy).then_inc(S["whi"], 1)
            act.activation(wo_w[:, HI], st_wo, ACT.Copy).then_inc(S["whi"], 1)
            act.wait_ge(S["wlo"], 3)
            act.activation(sg[:, 0, 0:4], cw[:, 0, :], ACT.Sigmoid).then_inc(S["whi"], 1)
            act.wait_ge(S["whi"], 4)
            with act.Fori(0, NB) as b:
                act.wait_ge(S["x_out"], 1 + b * 4)
                for gi in range(2):
                    m = b * 2 + gi
                    for h in range(2):
                        act.wait_ge(S["tr_done"], 1 + m * 2 + h + 1)
                        act.wait_ge(S["qkv_done"], 1 + m * NCH)
                        act.activation(a_w[:, HI, h, :], TR[h][:], ACT.Copy).then_inc(S["a_hi"], 1)
                    act.wait_ge(S["bmT_done"], m + 1)
                    act.wait_ge(S["bm_tr"], 1 + m)
                    act.wait_ge(S["beta_out"], 1 + m * 16)
                    act.activation(bmT[:], QKV[1][0:2 * NHD, :], ACT.Sigmoid).then_inc(S["bm_sig"], 1)
                    act.wait_ge(S["bm_tr"], 1 + m + 1)
                    act.activation(bm[:, gi * GT:gi * GT + GT, :], VT[:, 0:GT * 2 * NHD].rearrange("p (t c) -> p t c", t=GT), ACT.Copy).then_inc(S["bm_done"], 1)
                    for c in range(NCH + 1):
                        n = m * NCH + c
                        if c < NCH:
                            act.wait_ge(S["qkv_done"], 1 + n + 1)
                            act.wait_ge(S["silu_done"], 1 + (n - 1 if c >= 2 else m * NCH))
                            act.activation(cv[:, c % 2, :], QKV[c % 2][:], ACT.Copy, scale=cw[:, c, 3:4]).then_inc(S["tap0"], 1)
                        if c >= 1:
                            d = (c - 1) % 2
                            act.wait_ge(S["conv_done"], n * 3)
                            act.activation(sg[:, d, :], cv[:, d, :], ACT.Sigmoid).then_inc(S["sig_done"], 1)
                    for t in range(GT):
                        act.wait_ge(S["tok_done"], 1 + m * 4 + t + 1)
                        if t >= 2:
                            act.wait_ge(S["ss_done"], m * GT + t - 1)
                        act.activation(sq[:, t % 2, :], TOK[t % 2][:], ACT.Square).then_inc(S["sq_done"], 1)
                        if t % 2 == 1:
                            act.wait_ge(S["v_tr"], 1 + m * 2 + t // 2 + 1)
                            act.activation(v[:, gi * GT + t - 1:gi * GT + t + 1, :], VT[:].rearrange("p (t d) -> p t d", t=2), ACT.Copy).then_inc(S["v_done"], 1)
                        if t >= 1:
                            hi_qk(m, t - 1)
                    hi_qk(m, GT - 1)
                    for j in range(8):
                        q2 = slice(4 * (j // 2) + j % 2, 4 * (j // 2) + 4, 2)
                        gb = QKV[j % 2][:].rearrange("p (h c t) -> p h c t", h=2, c=2)
                        act.wait_ge(S["gk_done"], 1 + m * 8 + j + 1)
                        act.wait_ge(S["g_out"], 1 + m * 64)
                        act.activation(graw[:, q2, :], gb[:, :, 1, :], ACT.Copy).then_inc(S["graw_done"], 1)
                        act.wait_ge(S["kq_done"], m * 8 + j + 1)
                        act.activation(kq_w[:, gi, HI, q2, :], kq[:, j % 2], ACT.Copy).then_inc(S["kq_hi"], 1)
                        act.wait_ge(S["graw_done"], m * 8 + j + 1)
                        act.activation(g_w[:, gi, HI, q2, :], graw[:, q2, :], ACT.Copy).then_inc(S["g_hi"], 1)
                act.wait_ge(S["a_step"], 1 + b * 3 + 3)
                act.activation(t_w[:, :, 0, :], scm[:], ACT.Copy).then_inc(S["t_hi"], 1)
                for gi in range(2):
                    m = b * 2 + gi
                    for n in range(NC):
                        rows = slice(C * n, C * n + C)
                        for j in range(2):
                            q8 = slice(8 * j, 8 * j + 8)
                            if n == 0:
                                act.wait_ge(S["v_done"], m * 2 + 2)
                                act.activation(r_w[rows, HI, q8, :], v[rows, gi * GT + 2 * j:gi * GT + 2 * j + 2, :].rearrange("p t (h d) -> p (t h) d", h=NHD), ACT.Copy).then_inc(S["r_hi"], 1)
                            else:
                                act.wait_ge(S["r_done"], m * 6 + (n - 1) * 2 + j + 1)
                                act.activation(r_w[rows, HI, q8, :], r[rows, q8, :], ACT.Copy).then_inc(S["r_hi"], 1)
                        for j in range(2):
                            q8 = slice(8 * j, 8 * j + 8)
                            act.wait_ge(S["ps2"], m * 8 + n * 2 + j + 1)
                            act.wait_ge(S["o_done"], 1 + m * 2)
                            act.activation(u_w[rows, HI, q8, :], QKV[j][rows, :].rearrange("p (q d) -> p q d", q=8), ACT.Copy).then_inc(S["u_hi"], 1)
                    act.wait_ge(S["om1"], 1 + m * 4 + 4)
                    act.activation(full[:], om.rearrange("p t d -> p (t d)").rearrange("p (h n) -> p h n", h=2), ACT.Square).then_inc(S["osq"], 1)
                    for h in range(2):
                        act.wait_ge(S["otr"], 1 + m * 2 + h + 1)
                        act.wait_ge(S["oss"], m + 1)
                        act.activation(a_w[:, HI, h, :], TR[h][:], ACT.Copy, scale=nw[:]).then_inc(S["o_hi"], 1)
                        act.activation(full[:, h, :], TR[h][:], ACT.Copy, scale=nw[:]).then_inc(S["o_full"], 1)

        @block.vector
        def _(dve):
            def lo_qk(m, t):
                dve.wait_ge(S["qk_hi"], m * GT + t + 1)
                dve.tensor_tensor(qk_w[:, LO, t], BACK[:].rearrange("p (c t) -> p c t", c=4), qk_w[:, HI, t], ALU.subtract).then_inc(S["qk_lo"], 1)

            def stats_of(n, g):
                dve.wait_ge(S["m_mv"], 1 + n * GT)
                dve.nop(nofuse=True)
                for t in range(GT):
                    dve.bn_stats(stats[:, t, :], x[:, bass.ds(g * GT + t, 1), :]).then_inc(S["m_bn"], 1)
                dve.wait_ge(S["m_bn"], n * GT + GT)
                dve.nop(nofuse=True)
                dve.wait_ge(S["m_norm"], 1 + n * GT)
                dve.nop(nofuse=True)
                for t in range(GT):
                    dve.bn_aggr(mv[:, t, :], stats[:, t, :]).then_inc(S["m_mv"], 1)

            dve.wait_ge(S["ld_w"], 80)
            dve.wait_ge(S["bmz"], 1)
            dve.tensor_copy(bm_z[:, 0, :, 0:2 * NHD], st_bm[:]).then_inc(S["bmz"], 1)
            dve.wait_ge(S["whi"], 3)
            dve.tensor_tensor(qkv_w[:, LO], st_qkv, qkv_w[:, HI].bitcast(F32), ALU.subtract).then_inc(S["wlo"], 1)
            dve.tensor_tensor(bm_w[:, LO], bm_z[:, 0], bm_w[:, HI].bitcast(F32), ALU.subtract).then_inc(S["wlo"], 1)
            dve.tensor_tensor(wo_w[:, LO], st_wo, wo_w[:, HI].bitcast(F32), ALU.subtract).then_inc(S["wlo"], 1)
            dve.wait_ge(S["masks"], 6)
            with dve.Fori(0, NB) as b:
                for gi in range(2):
                    m = b * 2 + gi
                    stats_of(2 * m, m)
                    dve.wait_ge(S["m_rstd"], 2 * m + 1)
                    for t in range(GT):
                        xx = x[:, bass.ds(m * GT + t, 1), :]
                        dve.tensor_scalar(xx, xx, mv[:, t, 0:1], rstd[:, t:t + 1], ALU.subtract, ALU.mult).then_inc(S["m_norm"], 1)
                    dve.wait_ge(S["m_norm"], 1 + 2 * m * GT + GT)
                    dve.tensor_tensor(xg(m), xg(m), lnf_sb[:, 0:1, :].to_broadcast([P, GT, DM]), ALU.mult).then_inc(S["fin1"], 1)
                    dve.wait_ge(S["fin1"], m + 1)
                    dve.tensor_tensor(xg(m), xg(m), lnf_sb[:, 1:2, :].to_broadcast([P, GT, DM]), ALU.add).then_inc(S["fin2"], 1)
                    dve.wait_ge(S["fin2"], m + 1)
                    stats_of(2 * m + 1, m)
                    dve.wait_ge(S["m_rstd"], 2 * m + 2)
                    dve.wait_ge(S["tr_done"], 1 + m * 2)
                    dve.wait_ge(S["otr"], 1 + b * 4)
                    for t in range(GT):
                        dve.tensor_scalar(hn[:, t, :], x[:, bass.ds(m * GT + t, 1), :], mv[:, t, 0:1], rstd[:, t:t + 1], ALU.subtract, ALU.mult)\
                            .then_inc(S["m_norm"], 1)
                    for h in range(2):
                        dve.wait_ge(S["a_hi"], m * 2 + h + 1)
                        dve.tensor_tensor(a_w[:, LO, h, :], TR[h][:], a_w[:, HI, h, :].bitcast(F32), ALU.subtract).then_inc(S["a_lo"], 1)
                    for c in range(NCH):
                        n = m * NCH + c
                        dve.wait_ge(S["tap0"], n + 1)
                        src = QKV[c % 2][:].rearrange("p (s t) -> p s t", s=GT)
                        dst = cv[:, c % 2, :].rearrange("p (s t) -> p s t", s=GT)
                        for k in range(1, 4):
                            if k > 1:
                                dve.wait_ge(S["conv_done"], n * 3 + k - 1)
                            dve.scalar_tensor_tensor(dst[:, :, k:P], src[:, :, 0:P - k], cw[:, c, 3 - k:4 - k], dst[:, :, k:P], ALU.mult, ALU.add)\
                                .then_inc(S["conv_done"], 1)
                    for t in range(GT):
                        dve.wait_ge(S["sq_done"], m * GT + t + 1)
                        if t == 0:
                            dve.wait_ge(S["ors"], 1 + b * 2)
                        dve.tensor_reduce(ss[:, t, :], sq[:, t % 2, :].rearrange("p (h d) -> p h d", d=HD), AX.X, ALU.add).then_inc(S["ss_done"], 1)
                        dve.wait_ge(S["rs_done"], 1 + m * GT + t + 1)
                        if t >= 2:
                            dve.wait_ge(S["back_done"], m * GT + t - 1)
                        dve.tensor_tensor(qkn[:, t % 2, :].rearrange("p (h d) -> p h d", d=HD), TOK[t % 2][:].rearrange("p (h d) -> p h d", d=HD),
                                          rs[:, t, :].unsqueeze(2).to_broadcast([P, 2 * NHD, HD]), ALU.mult).then_inc(S["qkn_done"], 1)
                        if t >= 1:
                            lo_qk(m, t - 1)
                    lo_qk(m, GT - 1)
                    for j in range(8):
                        gb = QKV[j % 2][:].rearrange("p (h c t) -> p h c t", h=2, c=2)
                        dve.wait_ge(S["graw_done"], m * 8 + j + 1)
                        if j >= 2:
                            dve.wait_ge(S["kq_lo"], 1 + m * 8 + j - 1)
                        else:
                            dve.wait_ge(S["kq_lo"], 1 + m * 8)
                        dve.tensor_tensor(kq[:, j % 2], gb[:, :, 0, :], causal[:], ALU.mult).then_inc(S["kq_done"], 1)
                dve.wait_ge(S["gcm_in"], 1 + b * 32 + 32)
                dve.tensor_tensor(acm[:], gcm[:], bcm[:].unsqueeze(2).to_broadcast([P, C, C]), ALU.mult).then_inc(S["a_step"], 1)
                dve.wait_ge(S["a_step"], 1 + b * 3 + 1)
                dve.tensor_tensor(acm[:], acm[:], strict[:], ALU.mult).then_inc(S["a_step"], 1)
                dve.wait_ge(S["a_step"], 1 + b * 3 + 2)
                for i in range(1, C):
                    pr = prod[:, 0:i * i].rearrange("p (k j) -> p k j", j=i)
                    base = b * (2 * (C - 1)) + 2 * (i - 1)
                    if i > 1:
                        dve.wait_ge(S["ps_r"], base)
                    dve.tensor_tensor(pr, acm[:, i, 0:i].unsqueeze(1).to_broadcast([P, i, i]),
                                      tcm[:, 0:i, 0:i].rearrange("p j k -> p k j"), ALU.mult).then_inc(S["ps_r"], 1)
                    dve.wait_ge(S["ps_r"], base + 1)
                    dve.tensor_reduce(tcm[:, i, 0:i], pr, AX.X, ALU.add).then_inc(S["ps_r"], 1)
                dve.wait_ge(S["ps_r"], b * (2 * (C - 1)) + 2 * (C - 1))
                dve.wait_ge(S["t_hi"], 1 + b)
                dve.tensor_tensor(scm[:], tcm[:].rearrange("p i j -> p j i"), bcm[:].unsqueeze(2).to_broadcast([P, C, C]), ALU.mult).then_inc(S["a_step"], 1)
                dve.wait_ge(S["a_step"], 1 + b * 3 + 3)
                dve.wait_ge(S["t_hi"], 1 + b + 1)
                dve.tensor_tensor(t_w[:, :, 1, :], scm[:], t_w[:, :, 0, :], ALU.subtract).then_inc(S["t_lo"], 1)
                for gi in range(2):
                    m = b * 2 + gi
                    vq = v[:, gi * GT:gi * GT + GT, :].rearrange("p t (h d) -> p (t h) d", h=NHD)
                    for n in range(NC):
                        rows = slice(C * n, C * n + C)
                        for j in range(2):
                            q8 = slice(8 * j, 8 * j + 8)
                            if n > 0:
                                dve.wait_ge(S["ps1"], m * 6 + (n - 1) * 2 + j + 1)
                                dve.tensor_tensor(r[rows, q8, :], vq[rows, q8, :], TR[j][rows, :].rearrange("p (q d) -> p q d", q=8), ALU.subtract).then_inc(S["r_done"], 1)
                        for j in range(2):
                            q8 = slice(8 * j, 8 * j + 8)
                            dve.wait_ge(S["r_hi"], m * 8 + 2 * n + j + 1)
                            dve.tensor_tensor(r_w[rows, LO, q8, :], (vq if n == 0 else r)[rows, q8, :], r_w[rows, HI, q8, :], ALU.subtract).then_inc(S["r_lo"], 1)
                        for j in range(2):
                            q8 = slice(8 * j, 8 * j + 8)
                            dve.wait_ge(S["u_hi"], m * 8 + 2 * n + j + 1)
                            dve.tensor_tensor(u_w[rows, LO, q8, :], QKV[j][rows, :].rearrange("p (q d) -> p q d", q=8), u_w[rows, HI, q8, :], ALU.subtract).then_inc(S["u_lo"], 1)
                    mix = bm[:, gi * GT:gi * GT + GT, NHD:2 * NHD]
                    dve.wait_ge(S["vm1"], 1 + m)
                    dve.tensor_scalar(omix[:], mix, -1.0, 1.0, ALU.mult, ALU.add).then_inc(S["omix1"], 1)
                    for j in range(2):
                        dve.wait_ge(S["o_done"], 1 + m * 2 + j + 1)
                        dve.tensor_tensor(om[:, 2 * j:2 * j + 2, :].rearrange("p t (h d) -> p t h d", h=NHD), TOK[j][:].rearrange("p (t h d) -> p t h d", t=2, h=NHD),
                                          mix[:, 2 * j:2 * j + 2].unsqueeze(3).to_broadcast([P, 2, NHD, HD]), ALU.mult).then_inc(S["om1"], 1)
                    dve.wait_ge(S["vm1"], 1 + m + 1)
                    dve.wait_ge(S["om1"], 1 + m * 4 + 2)
                    dve.tensor_tensor(om, om, vm, ALU.add).then_inc(S["om1"], 2)
                    dve.wait_ge(S["osq"], m + 1)
                    dve.tensor_reduce(ss[:, :, 0:NHD], full[:].rearrange("p a n -> p (a n)").rearrange("p (t h d) -> p t h d", t=GT, h=NHD), AX.X, ALU.add).then_inc(S["oss"], 1)
                    dve.wait_ge(S["ors"], 1 + m + 1)
                    dve.wait_ge(S["otr"], 1 + m * 2)
                    dve.wait_ge(S["tr_done"], 1 + b * 4 + 4)
                    dve.tensor_tensor(hn[:].rearrange("p t (h d) -> p t h d", h=NHD), om.rearrange("p t (h d) -> p t h d", h=NHD),
                                      rs[:, :, 0:NHD].unsqueeze(3).to_broadcast([P, GT, NHD, HD]), ALU.mult).then_inc(S["o3"], 1)
                    for h in range(2):
                        dve.wait_ge(S["o_full"], m * 2 + h + 1)
                        dve.tensor_tensor(a_w[:, LO, h, :], full[:, h, :], a_w[:, HI, h, :].bitcast(F32), ALU.subtract).then_inc(S["o_lo"], 1)
                    for j in range(2):
                        dve.wait_ge(S["wo_done"], m * 2 + j + 1)
                        xx = x[:, bass.ds(m * GT + 2 * j, 2), :]
                        dve.tensor_tensor(xx, xx, bk[6 + j][:].rearrange("p (a d) -> p a d", a=2), ALU.add).then_inc(S["x_out"], 1)

        @block.tensor
        def _(pe):
            def back(m, t):
                pe.wait_ge(S["qkn_done"], 1 + m * GT + t + 1)
                pe.wait_ge(S["qk_lo"], 1 + m * GT + t)
                for c in range(4):
                    last = pe.transpose(BACK[:, c * P:(c + 1) * P], qkn[:, t % 2, c * P:(c + 1) * P], ident[:])
                last.then_inc(S["back_done"], 1)

            hp = [(h, p) for h in range(2) for p in PASSES]
            pe.wait_ge(S["wlo"], 3)
            with pe.Fori(0, NB) as b:
                pe.wait_ge(S["x_out"], 1 + b * 4)
                for gi in range(2):
                    m = b * 2 + gi
                    pe.wait_ge(S["m_norm"], 1 + (2 * m + 2) * GT)
                    pe.wait_ge(S["a_lo"], 1 + m * 2)
                    pe.wait_ge(S["o_lo"], 1 + b * 4)
                    for h in range(2):
                        for t in range(GT):
                            last = pe.transpose(TR[h][:, t * P:(t + 1) * P], hn[:, t, h * P:(h + 1) * P], ident[:])
                        last.then_inc(S["tr_done"], 1)
                    pe.wait_ge(S["a_lo"], 1 + m * 2 + 2)
                    for i, (h, (p, q)) in enumerate(hp):
                        last = pe.matmul(QKV[1][:], bm_w[:, p, h, :], a_w[:, q, h, :], start=(i == 0), stop=(i == 5))
                    last.then_inc(S["bmT_done"], 1)
                    pe.wait_ge(S["bm_sig"], m + 1)
                    pe.nop(nofuse=True)
                    for t in range(GT):
                        last = pe.transpose(VT[:, t * 2 * NHD:(t + 1) * 2 * NHD], bmT[:, t * P:(t + 1) * P], ident[0:2 * NHD, 0:2 * NHD])
                    last.then_inc(S["bm_tr"], 1)
                    for c in range(NCH):
                        n = m * NCH + c
                        if c >= 2:
                            pe.wait_ge(S["conv_done"], (n - 1) * 3)
                        for i, (h, (p, q)) in enumerate(hp):
                            last = pe.matmul(QKV[c % 2][:], qkv_w[:, p, h, c * P:(c + 1) * P], a_w[:, q, h, :], start=(i == 0), stop=(i == 5))
                        last.then_inc(S["qkv_done"], 1)
                    pe.wait_ge(S["bm_done"], m + 1)
                    for t in range(GT):
                        pe.wait_ge(S["silu_done"], 1 + (m * NCH + (4 if t == 0 else 6)))
                        if t >= 2:
                            pe.wait_ge(S["qkn_done"], 1 + m * GT + t - 1)
                        for c in range(4):
                            last = pe.transpose(TOK[t % 2][:, c * P:(c + 1) * P], qkv_t[:, c, t * P:(t + 1) * P], ident[:])
                        last.then_inc(S["tok_done"], 1)
                        pe.wait_ge(S["silu_done"], 1 + m * NCH + 6)
                        if t == 2:
                            pe.wait_ge(S["v_done"], m * 2 + 1)
                        for c in range(2):
                            last = pe.transpose(VT[:, (t % 2) * DM + c * P:(t % 2) * DM + (c + 1) * P], qkv_t[:, 4 + c, t * P:(t + 1) * P], ident[:])
                        if t % 2 == 1:
                            last.then_inc(S["v_tr"], 1)
                        if t >= 1:
                            back(m, t - 1)
                    back(m, GT - 1)
                    for j in range(8):
                        t = j // 2
                        pe.wait_ge(S["qk_lo"], 1 + m * GT + t + 1)
                        if j >= 2:
                            pe.wait_ge(S["kq_done"], m * 8 + j - 1)
                        for hh in range(2):
                            hd = j % 2 + 2 * hh
                            rows = slice((hd % 2) * HD, (hd % 2) * HD + HD)
                            for i, (p, q) in enumerate(PASSES):
                                o = QKV[j % 2][:, hh * 256:(hh + 1) * 256].rearrange("p (c t) -> p c t", c=2)
                                last = pe.matmul(o, qk_w[rows, p, t, 2 + hd // 2, :], qk_w[rows, q, t, hd // 2::2, :], start=(i == 0), stop=(i == 2))
                        last.then_inc(S["gk_done"], 1)
                pe.wait_ge(S["tt_in"], b * 64 + 64)
                for gi in range(2):
                    m = b * 2 + gi
                    pe.wait_ge(S["kq_lo"], 1 + m * 8 + 8)
                    pe.nop(nofuse=True)
                    pe.wait_ge(S["g_lo"], m * 8 + 8)
                    pe.nop(nofuse=True)
                    for n in range(NC):
                        rows = slice(C * n, C * n + C)
                        if n > 0:
                            for j in range(2):
                                pe.wait_ge(S["u_lo"], 1 + m * 8 + (n - 1) * 2 + j + 1)
                                pe.nop(nofuse=True)
                                for q in range(8 * j, 8 * j + 8):
                                    for i, (p, s) in enumerate(PASSES):
                                        last = pe.matmul(TR[j][rows, (q % 8) * HD:(q % 8 + 1) * HD], g_w[0:C * n, gi, p, q, rows], u_w[0:C * n, s, q, :],
                                                         start=(i == 0), stop=(i == 2))
                                last.then_inc(S["ps1"], 1)
                        for j in range(2):
                            pe.wait_ge(S["r_lo"], m * 8 + 2 * n + j + 1)
                            pe.nop(nofuse=True)
                            for q in range(8 * j, 8 * j + 8):
                                for i, (p, s) in enumerate(PASSES):
                                    last = pe.matmul(QKV[j][rows, (q % 8) * HD:(q % 8 + 1) * HD], tt[rows, gi * NQ + q, p, :], r_w[rows, s, q, :],
                                                     start=(i == 0), stop=(i == 2))
                            last.then_inc(S["ps2"], 1)
                    for j in range(2):
                        pe.wait_ge(S["u_lo"], 1 + m * 8 + 6 + j + 1)
                        pe.wait_ge(S["om1"], 1 + m * 4)
                        for q in range(8 * j, 8 * j + 8):
                            for i, (p, s) in enumerate(PASSES):
                                last = pe.matmul(TOK[j][:, (q % 8) * HD:(q % 8 + 1) * HD], kq_w[:, gi, p, q, :], u_w[:, s, q, :], start=(i == 0), stop=(i == 2))
                        last.then_inc(S["o_done"], 1)
                    pe.wait_ge(S["o3"], 1 + m + 1)
                    for h in range(2):
                        for t in range(GT):
                            last = pe.transpose(TR[h][:, t * P:(t + 1) * P], hn[:, t, h * P:(h + 1) * P], ident[:])
                        last.then_inc(S["otr"], 1)
                    pe.wait_ge(S["o_lo"], 1 + m * 2 + 2)
                    pe.wait_ge(S["x_out"], 1 + m * 2)
                    for j in range(2):
                        for t in range(2 * j, 2 * j + 2):
                            tok = slice(t * P, (t + 1) * P)
                            for i, (h, (p, q)) in enumerate(hp):
                                last = pe.matmul(bk[6 + j][:, (t % 2) * DM:(t % 2 + 1) * DM], a_w[:, p, h, tok], wo_w[:, q, h, :], start=(i == 0), stop=(i == 5))
                        last.then_inc(S["wo_done"], 1)


def experts(nc, sems, x, ident, half, wr, wgu, bgu, wd, bd, out):
    NSEQ, DM = x.shape[1], x.shape[2]
    GT = 4
    NG = NSEQ // GT
    GN = GT * P
    E = wr.shape[1]
    INTER = wd.shape[1]
    LIMIT, ALPHA = 7.0, 1.702
    assert INTER == P
    with ExitStack() as ctx:
        def sb(name, shape, dt=F32):
            return ctx.enter_context(nc.sbuf_tensor(name, shape, dt))

        bk = [ctx.enter_context(nc.psum_tensor(f"mk{i}", [P, 512], F32)) for i in range(8)]
        GATE, UP, DN, TR = bk[0:2], bk[2:4], bk[4:6], bk[6:8]
        gu_w = sb("gu_w", [P, 2, E, 2, 2 * P], F32R)
        dn_w = sb("dn_w", [P, 2, E, DM], F32R)
        r_w = sb("rt_w", [P, 2, 2, P], F32R)
        r_z = sb("rt_z", [P, 2, P])
        st = sb("st_e", [P, 2, 2, 2 * P])
        st_d = sb("st_ed", [P, 2, DM])
        st_r = sb("st_r", [P, 2, E])
        bcol = sb("bcol", [P, 2, E])
        bd_sb = sb("bd_sb", [E, DM])
        iota = sb("iota_e", [P, E])
        stats = sb("stats3", [P, GT, 6])
        mv = sb("mv3", [P, GT, 2])
        veps = sb("veps3", [P, GT])
        rstd = sb("rstd3", [P, GT])
        hn = sb("hn3", [P, GT, DM])
        m_w = sb("m_w", [P, 2, 2, GN], F32R)
        lgT = sb("lgT", [E, GN])
        lg = sb("lg", [P, GT, E])
        mx = sb("mx", [P, GT, 8])
        ix = sb("ix", [P, GT, 8], U32)
        ixf = sb("ixf", [P, GT, 2])
        df = sb("df", [P, GT, 2])
        wt = sb("wt", [P, GT, 2])
        oh = sb("oh", [P, GT, E])
        sc = sb("sc3", [P, GT, E])
        scT = sb("scT", [E, GN])
        gs = sb("gs", [P, 2, GN])
        sg = sb("sg3", [P, 2, GN])
        us = sb("us", [P, 2, GN])
        gl = sb("gl", [P, 2, GN])
        ac = sb("ac", [P, 2, GN])
        ac_w = sb("ac_w", [P, 2, 2, GN], F32R)

        names = """ld ldw ldd whi wlo wdone rz iot bn mvd ve rstd norm tr hi lo lgt lgs lgb lgd mxd ixd dfd wtd ohd scd scb scs bdn xacc
        gate up gsd sgd usd gld acd achi aclo dn fin outd""".split()
        S = {n: sems.enter_context(nc.semaphore("e_" + n)) for n in names}
        primed = """acd achi bdn dn gld gsd ixd lgb lo mvd norm ohd scs tr up usd wtd xacc""".split()
        block = ctx.enter_context(nc.Block())
        gu_d = wgu.rearrange("e (h p) c -> e p h c", p=P)

        @block.sync
        def _(sp):
            for n in primed:
                sp.sem_inc(S[n], 1)
            sp.dma_start(st_r[:], wr.rearrange("(h p) e -> p h e", p=P)).then_inc(S["ld"], 16)
            sp.dma_start(bcol[:], bgu).then_inc(S["ld"], 16)
            sp.dma_start(bd_sb[:], bd).then_inc(S["ld"], 16)
            for e in range(E):
                if e >= 2:
                    sp.wait_ge(S["wlo"], 2 * (e - 1) + 1)
                sp.dma_start(st[:, e % 2], gu_d[e]).then_inc(S["ldw"] if e % 2 == 0 else S["ldd"], 16)
                sp.dma_start(st_d[:, e % 2], wd[e]).then_inc(S["ldw"] if e % 2 == 0 else S["ldd"], 16)
            out_v = out.rearrange("b t d -> t b d")
            with sp.Fori(0, NG) as g:
                sp.wait_ge(S["xacc"], 1 + (g + 1) * (E * GT + 2))
                sp.dma_start(out_v[:, bass.ds(g * GT, GT), :], x[:, bass.ds(g * GT, GT), :]).then_inc(S["outd"], 16)
            sp.wait_ge(S["outd"], 16 * NG)

        @block.gpsimd
        def _(pool):
            pool.memset(r_z[:], 0.0).then_inc(S["rz"], 1)
            pool.iota(iota[:], [[1, E]], base=0, channel_multiplier=0, allow_small_or_imprecise_dtypes=True).then_inc(S["iot"], 1)
            with pool.Fori(0, NG) as g:
                pool.wait_ge(S["mvd"], 1 + g * GT + GT)
                pool.nop(nofuse=True)
                pool.wait_ge(S["norm"], 1 + g * GT)
                pool.nop(nofuse=True)
                pool.tensor_scalar(veps[:], mv[:, :, 1], EPS, None, ALU.add).then_inc(S["ve"], 1)
                pool.wait_ge(S["ve"], g + 1)
                pool.tensor_tensor(rstd[:], veps[:], half[:].to_broadcast([P, GT]), ALU.pow).then_inc(S["rstd"], 1)
                for e in range(E):
                    n = g * E + e
                    pool.wait_ge(S["sgd"], n + 1)
                    pool.wait_ge(S["gsd"], 1 + n + 1)
                    if e >= 2:
                        pool.wait_ge(S["acd"], 1 + n - 1)
                    else:
                        pool.wait_ge(S["acd"], 1 + g * E)
                    pool.tensor_tensor(gl[:, e % 2], gs[:, e % 2], sg[:, e % 2], ALU.mult).then_inc(S["gld"], 1)

        @block.scalar
        def _(act):
            act.wait_ge(S["ld"], 48)
            act.wait_ge(S["rz"], 2)
            act.activation(r_w[:, HI], r_z[:], ACT.Copy).then_inc(S["whi"], 1)
            for e in range(E):
                act.wait_ge(S["ldw"] if e % 2 == 0 else S["ldd"], 32 * (e // 2 + 1))
                act.activation(gu_w[:, HI, e], st[:, e % 2], ACT.Copy).then_inc(S["whi"], 1)
                act.activation(dn_w[:, HI, e], st_d[:, e % 2], ACT.Copy).then_inc(S["whi"], 1)
            act.activation(ac[:, 0, 0:2], bcol[:, 0, 0:2], ACT.Sigmoid).then_inc(S["wdone"], 1)
            act.wait_ge(S["wdone"], 1)
            with act.Fori(0, NG) as g:
                for h in range(2):
                    act.wait_ge(S["tr"], 1 + g * 2 + h + 1)
                    act.wait_ge(S["up"], 1 + g * E)
                    act.activation(m_w[:, HI, h, :], TR[h][:], ACT.Copy).then_inc(S["hi"], 1)
                act.wait_ge(S["lgt"], g + 1)
                act.wait_ge(S["lgb"], 1 + g)
                act.activation(lgT[:], DN[0][0:E, :], ACT.Copy).then_inc(S["lgs"], 1)
                act.wait_ge(S["lgb"], 1 + g + 1)
                act.wait_ge(S["ixd"], 1 + g * GT)
                act.activation(lg[:], DN[1][:, 0:GT * E].rearrange("p (t e) -> p t e", t=GT), ACT.Copy).then_inc(S["lgd"], 1)
                act.wait_ge(S["dfd"], 2 * g + 2)
                act.wait_ge(S["ohd"], 1 + 3 * g)
                act.activation(wt[:], df[:], ACT.Sigmoid).then_inc(S["wtd"], 1)
                act.wait_ge(S["scb"], g + 1)
                act.wait_ge(S["bdn"], 1 + 2 * g)
                act.activation(scT[:], TR[0][0:E, :], ACT.Copy).then_inc(S["scs"], 1)
                for e in range(E):
                    n = g * E + e
                    act.wait_ge(S["gsd"], 1 + n + 1)
                    act.wait_ge(S["gld"], 1 + (n - 1 if e >= 2 else g * E))
                    act.activation(sg[:, e % 2], gs[:, e % 2], ACT.Sigmoid, scale=ALPHA).then_inc(S["sgd"], 1)
                    act.wait_ge(S["acd"], 1 + n + 1)
                    act.wait_ge(S["dn"], 1 + (n - 1 if e >= 2 else g * E))
                    act.activation(ac_w[:, e % 2, HI], ac[:, e % 2], ACT.Copy).then_inc(S["achi"], 1)

        @block.vector
        def _(dve):
            dve.wait_ge(S["ld"], 48)
            dve.wait_ge(S["rz"], 1)
            dve.tensor_copy(r_z[:, :, 0:E], st_r[:]).then_inc(S["rz"], 1)
            dve.tensor_scalar(bcol[:, 1, :], bcol[:, 1, :], 1.0, None, ALU.add).then_inc(S["iot"], 1)
            dve.wait_ge(S["whi"], 1)
            dve.tensor_tensor(r_w[:, LO], r_z[:], r_w[:, HI].bitcast(F32), ALU.subtract).then_inc(S["wlo"], 1)
            for e in range(E):
                dve.wait_ge(S["whi"], 2 * e + 3)
                dve.tensor_tensor(gu_w[:, LO, e], st[:, e % 2], gu_w[:, HI, e].bitcast(F32), ALU.subtract).then_inc(S["wlo"], 1)
                dve.tensor_tensor(dn_w[:, LO, e], st_d[:, e % 2], dn_w[:, HI, e].bitcast(F32), ALU.subtract).then_inc(S["wlo"], 1)
            dve.wait_ge(S["iot"], 2)
            with dve.Fori(0, NG) as g:
                dve.wait_ge(S["mvd"], 1 + g * GT)
                for t in range(GT):
                    dve.bn_stats(stats[:, t, :], x[:, bass.ds(g * GT + t, 1), :]).then_inc(S["bn"], 1)
                dve.wait_ge(S["bn"], g * GT + GT)
                dve.nop(nofuse=True)
                dve.wait_ge(S["norm"], 1 + g * GT)
                dve.nop(nofuse=True)
                for t in range(GT):
                    dve.bn_aggr(mv[:, t, :], stats[:, t, :]).then_inc(S["mvd"], 1)
                dve.wait_ge(S["rstd"], g + 1)
                dve.wait_ge(S["tr"], 1 + g * 2)
                for t in range(GT):
                    dve.tensor_scalar(hn[:, t, :], x[:, bass.ds(g * GT + t, 1), :], mv[:, t, 0:1], rstd[:, t:t + 1], ALU.subtract, ALU.mult).then_inc(S["norm"], 1)
                for h in range(2):
                    dve.wait_ge(S["hi"], g * 2 + h + 1)
                    dve.tensor_tensor(m_w[:, LO, h, :], TR[h][:], m_w[:, HI, h, :].bitcast(F32), ALU.subtract).then_inc(S["lo"], 1)
                dve.wait_ge(S["lgd"], g + 1)
                dve.nop(nofuse=True)
                for t in range(GT):
                    dve.max(mx[:, t, :], lg[:, t, :]).then_inc(S["mxd"], 1)
                dve.wait_ge(S["mxd"], g * GT + GT)
                dve.nop(nofuse=True)
                for t in range(GT):
                    dve.max_index(ix[:, t, :], mx[:, t, :], lg[:, t, :]).then_inc(S["ixd"], 1)
                dve.wait_ge(S["ixd"], 1 + g * GT + GT)
                dve.tensor_copy(ixf[:], ix[:, :, 0:2]).then_inc(S["ixd"], 0) if False else dve.tensor_copy(ixf[:], ix[:, :, 0:2])
                dve.wait_ge(S["wtd"], 1 + g)
                dve.tensor_tensor(df[:, :, 0], mx[:, :, 0], mx[:, :, 1], ALU.subtract).then_inc(S["dfd"], 1)
                dve.tensor_tensor(df[:, :, 1], mx[:, :, 1], mx[:, :, 0], ALU.subtract).then_inc(S["dfd"], 1)
                dve.wait_ge(S["wtd"], 1 + g + 1)
                for k in range(2):
                    dst = (oh, sc)[k]
                    dve.tensor_tensor(dst[:], iota[:].unsqueeze(1).to_broadcast([P, GT, E]), ixf[:, :, k:k + 1].to_broadcast([P, GT, E]), ALU.is_equal)\
                        .then_inc(S["scd"], 1)
                    dve.wait_ge(S["scd"], g * 3 + k + 1)
                    dve.tensor_tensor(dst[:], dst[:], wt[:, :, k:k + 1].to_broadcast([P, GT, E]), ALU.mult).then_inc(S["ohd"], 1)
                dve.wait_ge(S["ohd"], 1 + g * 3 + 2)
                dve.tensor_tensor(sc[:], sc[:], oh[:], ALU.add).then_inc(S["ohd"], 1)
                dve.sem_inc(S["scd"], 1)
                for j in range(2):
                    dve.wait_ge(S["bdn"], 1 + 2 * g + j + 1)
                    xx = x[:, bass.ds(g * GT + 2 * j, 2), :]
                    dve.tensor_tensor(xx, xx, DN[j][:].rearrange("p (a d) -> p a d", a=2), ALU.add).then_inc(S["xacc"], 1)
                dve.wait_ge(S["xacc"], 1 + g * (E * GT + 2) + 2)

                def combine(e):
                    n = g * E + e
                    dve.wait_ge(S["aclo"], n + 1)
                    for t in range(GT):
                        if t % 2 == 0:
                            dve.wait_ge(S["dn"], 1 + n + 1)
                        if e > 0 and t == 0:
                            dve.wait_ge(S["xacc"], 1 + g * (E * GT + 2) + 2 + GT * e)
                        xx = x[:, bass.ds(g * GT + t, 1), :]
                        dve.scalar_tensor_tensor(xx, DN[t // 2][:, (t % 2) * DM:(t % 2 + 1) * DM].unsqueeze(1), sc[:, t, e:e + 1], xx, ALU.mult, ALU.add)\
                            .then_inc(S["xacc"], 1)

                for e in range(E):
                    n = g * E + e
                    dve.wait_ge(S["gate"], n + 1)
                    if e >= 2:
                        dve.wait_ge(S["gld"], 1 + n - 1)
                    dve.tensor_scalar(gs[:, e % 2], GATE[e % 2][:], bcol[:, 0, e:e + 1], LIMIT, ALU.add, ALU.min).then_inc(S["gsd"], 1)
                    dve.wait_ge(S["up"], 1 + n + 1)
                    dve.tensor_scalar(us[:, e % 2], UP[e % 2][:], bcol[:, 1, e:e + 1], 1.0 - LIMIT, ALU.add, ALU.max).then_inc(S["usd"], 1)
                    if e >= 1:
                        combine(e - 1)
                    dve.wait_ge(S["gld"], 1 + n + 1)
                    dve.wait_ge(S["usd"], 1 + n + 1)
                    dve.wait_ge(S["achi"], 1 + (n - 1 if e >= 2 else g * E))
                    dve.scalar_tensor_tensor(ac[:, e % 2], us[:, e % 2], 1.0 + LIMIT, gl[:, e % 2], ALU.min, ALU.mult).then_inc(S["acd"], 1)
                    dve.wait_ge(S["achi"], 1 + n + 1)
                    dve.tensor_tensor(ac_w[:, e % 2, LO], ac[:, e % 2], ac_w[:, e % 2, HI].bitcast(F32), ALU.subtract).then_inc(S["aclo"], 1)
                combine(E - 1)

        @block.tensor
        def _(pe):
            hp = [(h, p) for h in range(2) for p in PASSES]
            pe.wait_ge(S["wlo"], 2 * E + 1)
            with pe.Fori(0, NG) as g:
                pe.wait_ge(S["norm"], 1 + g * GT + GT)
                pe.wait_ge(S["lo"], 1 + g * 2)
                pe.wait_ge(S["scs"], 1 + g)
                for h in range(2):
                    for t in range(GT):
                        last = pe.transpose(TR[h][:, t * P:(t + 1) * P], hn[:, t, h * P:(h + 1) * P], ident[:])
                    last.then_inc(S["tr"], 1)
                pe.wait_ge(S["lo"], 1 + g * 2 + 2)
                pe.wait_ge(S["xacc"], 1 + g * (E * GT + 2))
                for i, (h, (a, b)) in enumerate(hp):
                    last = pe.matmul(DN[0][:], r_w[:, a, h, :], m_w[:, b, h, :], start=(i == 0), stop=(i == 5))
                last.then_inc(S["lgt"], 1)
                pe.wait_ge(S["lgs"], g + 1)
                pe.nop(nofuse=True)
                for t in range(GT):
                    last = pe.transpose(DN[1][:, t * E:(t + 1) * E], lgT[:, t * P:(t + 1) * P], ident[0:E, 0:E])
                last.then_inc(S["lgb"], 1)
                pe.wait_ge(S["ohd"], 1 + 3 * g + 3)
                for t in range(GT):
                    last = pe.transpose(TR[0][0:E, t * P:(t + 1) * P], sc[:, t, :], ident[:])
                last.then_inc(S["scb"], 1)
                pe.wait_ge(S["scs"], 1 + g + 1)
                pe.wait_ge(S["lgd"], g + 1)
                for j in range(2):
                    for t in range(2 * j, 2 * j + 2):
                        last = pe.matmul(DN[j][:, (t % 2) * DM:(t % 2 + 1) * DM], scT[:, t * P:(t + 1) * P], bd_sb[:], start=True, stop=True)
                    last.then_inc(S["bdn"], 1)

                def down(e):
                    n = g * E + e
                    pe.wait_ge(S["aclo"], n + 1)
                    pe.wait_ge(S["xacc"], 1 + g * (E * GT + 2) + 2 + GT * e)
                    for t in range(GT):
                        for i, (a, b) in enumerate(PASSES):
                            last = pe.matmul(DN[t // 2][:, (t % 2) * DM:(t % 2 + 1) * DM], ac_w[:, e % 2, a, t * P:(t + 1) * P], dn_w[:, b, e, :],
                                             start=(i == 0), stop=(i == 2))
                    last.then_inc(S["dn"], 1)

                for e in range(E):
                    n = g * E + e
                    pe.wait_ge(S["gsd"], 1 + (n - 1 if e >= 2 else g * E))
                    for i, (h, (a, b)) in enumerate(hp):
                        last = pe.matmul(GATE[e % 2][:], gu_w[:, a, e, h, 0:P], m_w[:, b, h, :], start=(i == 0), stop=(i == 5))
                    last.then_inc(S["gate"], 1)
                    pe.wait_ge(S["usd"], 1 + (n - 1 if e >= 2 else g * E))
                    for i, (h, (a, b)) in enumerate(hp):
                        last = pe.matmul(UP[e % 2][:], gu_w[:, a, e, h, P:2 * P], m_w[:, b, h, :], start=(i == 0), stop=(i == 5))
                    last.then_inc(S["up"], 1)
                    if e >= 1:
                        down(e - 1)
                down(E - 1)


def program(nc, ids, emb, pos, A_diag, Bw, Cw, Dw, w1, w2, b2, cols, lnf, wqkv, wbm, wo, conv, norm_w, wr, wgu, bgu, wd, bd, out):
    NSEQ, DM = ids.shape[1], emb.shape[1]
    scr_g = nc.dram_tensor("scr_g", (P, 32, 32), F32, kind="Internal").ap()
    scr_b = nc.dram_tensor("scr_b", (32, P), F32, kind="Internal").ap()
    scr_t = nc.dram_tensor("scr_t", (P, 32, 64), F16, kind="Internal").ap()
    with ExitStack() as ctx:
        x = ctx.enter_context(nc.sbuf_tensor("x", [P, NSEQ, DM], F32))
        ident = ctx.enter_context(nc.sbuf_tensor("ident", [P, P], F32))
        half = ctx.enter_context(nc.sbuf_tensor("half", [P, 1], F32))
        lnf_sb = ctx.enter_context(nc.sbuf_tensor("lnf_sb", [P, 2, DM], F32))
        tower_sems = []
        tower(nc, tower_sems, x, ident, half, lnf_sb, ids, emb, pos, A_diag, Bw, Cw, Dw, w1, w2, b2, cols, lnf)
        nc.all_engine_barrier()
        nc.clear_and_free_semaphores(tower_sems)
        nc.all_engine_barrier()
        attention(nc, ctx, x, ident, half, lnf_sb, wqkv, wbm, wo, conv, norm_w, scr_g, scr_b, scr_t)
        experts(nc, ctx, x, ident, half, wr, wgu, bgu, wd, bd, out)


def kernel(**inputs):
    import numpy as np
    import concourse.bacc as bacc
    from concourse.bass_utils import run_bass_kernel_spmd as run

    a = {k: np.asarray(v) for k, v in inputs.items()}
    tok, attn, ffn = "L0_tok_", "L0_attn_", "L0_ffn_"

    def columns(v):
        return v.reshape(v.shape[0], -1, P).transpose(0, 2, 1)

    gate_up, gate_up_bias = a[ffn + "gate_up_proj"], a[ffn + "gate_up_proj_bias"]
    arrays = {
        "ids": a["x"].T, "emb": a[tok + "emb"], "pos": a[tok + "pos_emb"], "A_diag": a[tok + "A_diag"].T,
        "Bw": a[tok + "B"], "Cw": a[tok + "C"], "Dw": a[tok + "D"], "w1": a[tok + "w1"], "w2": a[tok + "w2"], "b2": a[tok + "b2"],
        "cols": np.concatenate([columns(a[tok + n]) for n in ("ln1_s", "ln1_b", "ln2_s", "ln2_b", "b1")], axis=2),
        "lnf": np.stack([a[tok + "lnf_s"], a[tok + "lnf_b"]]),
        "wqkv": np.concatenate([a[attn + n].T for n in ("Wq", "Wk", "Wv")], axis=1),
        "wbm": np.concatenate([a[attn + "Wb"].T, a[attn + "Wmix"].T], axis=1),
        "wo": a[attn + "Wo"].T,
        "conv": np.concatenate([a[attn + n] for n in ("conv_q", "conv_k", "conv_v")]),
        "norm_w": np.concatenate([a[attn + "norm_w"]] * 2)[:, None],
        "wr": a[ffn + "router_weight"],
        "wgu": np.concatenate([gate_up[:, :, 0::2], gate_up[:, :, 1::2]], axis=2),
        "bgu": np.stack([gate_up_bias[:, 0::2].T, gate_up_bias[:, 1::2].T], axis=1),
        "wd": a[ffn + "down_proj"], "bd": a[ffn + "down_proj_bias"],
    }
    arrays = {k: np.ascontiguousarray(v) for k, v in arrays.items()}
    nc = bacc.Bacc("TRN2", target_bir_lowering=False, num_devices=1)
    aps = {k: nc.dram_tensor(k, v.shape, mybir.dt.from_np(v.dtype), kind="ExternalInput").ap() for k, v in arrays.items()}
    shape = (a["x"].shape[0], a["x"].shape[1], a[tok + "emb"].shape[1])
    aps["out"] = nc.dram_tensor("out", shape, F32, kind="ExternalOutput").ap()
    program(nc, **aps)
    return run(nc, [arrays], core_ids=[0]).results[0]["out"]
```

```python
from contextlib import ExitStack

import concourse.bass as bass
from concourse import mybir

ALU = mybir.AluOpType
ACT = mybir.ActivationFunctionType
F32 = mybir.dt.float32
F32R = mybir.dt.float32r
F16 = mybir.dt.float16
BF16 = mybir.dt.bfloat16
I32 = mybir.dt.int32
U32 = mybir.dt.uint32
AX = mybir.AxisListType

P = 128
HI, LO = 0, 1
PASSES = ((HI, HI), (HI, LO), (LO, HI))
EPS = 1e-5
L2_EPS = 1e-6


def tower(nc, sems, x, ident, half, lnf_sb, ids, emb, pos, A_diag, Bw, Cw, Dw, w1, w2, b2, cols, lnf):
    V, DM = emb.shape
    NSEQ, T = ids.shape[1], P
    S, L = A_diag.shape
    FF = w1.shape[2]
    GT = 4
    NG = NSEQ // GT
    GN = GT * P
    NH2 = DM // P
    NF = FF // P
    NCOL = cols.shape[2]
    assert GN == 512 and NH2 == 2 and 2 * S == P and NG == 8 and NF == 8

    with ExitStack() as ctx:
        def sb(name, shape, dt=F32):
            return ctx.enter_context(nc.sbuf_tensor(name, shape, dt))

        def sem(name):
            sems.append(nc.alloc_semaphore(name=name))
            return sems[-1]

        def bank(name):
            return ctx.enter_context(nc.psum_tensor(name, [P, 512], F32))

        ids_sb = sb("ids_sb", [P, NSEQ], I32)
        idf = sb("idf", [P, NSEQ])
        idneg = sb("idneg", [P, NSEQ])
        idx = sb("idx", [P, NSEQ], I32)
        pos_sb = sb("pos_sb", [P, DM])
        a_col = sb("a_col", [P, L])
        a_sig = sb("a_sig", [P, L])
        runmask = sb("runmask", [P, GT, T])
        decay = sb("decay", [P, GT, T])
        st_d = sb("st_d", [P, NH2, DM])
        st_b = sb("st_b", [P, NH2, 2, S])
        st_c = sb("st_c", [P, DM])
        st_w1 = sb("st_w1", [P, NH2, FF])
        st_w2 = sb("st_w2", [P, NF, DM])
        st_b2 = sb("st_b2", [P, DM])
        st_cols = sb("st_cols", [P, NCOL])
        d_w = sb("d_w", [P, 2, NH2, DM], F32R)
        b_w = sb("b_w", [P, 2, NH2, P], F32R)
        c_w = sb("c_w", [P, DM], F32R)
        c_t = sb("c_t", [P, DM], F32R)
        w1_w = sb("w1_w", [P, 2, NH2, FF], F32R)
        w2_w = sb("w2_w", [P, 2, NF, DM], F32R)
        b2_bc = sb("b2_bc", [P, DM])
        col = sb("col", [P, NCOL])
        stats = sb("stats", [P, GT, 6])
        mv = sb("mv", [P, GT, 2])
        veps = sb("veps", [P, GT])
        rstd = sb("rstd", [P, GT])
        hn = sb("hn", [P, GT, DM])
        full = sb("full", [P, NH2, GN])
        h1 = sb("h1", [P, 2, NH2, GN], F32R)
        h2 = [sb(f"h2_{i}", [P, 2, NH2, GN], F32R) for i in range(2)]
        hs = sb("hs", [P, GN])
        hs_w = sb("hs_w", [P, 2, GN], F32R)
        gfull = sb("gfull", [P, 2, GN])
        g_w = sb("g_w", [P, 2, 2, GN], F32R)

        TR = [bank(f"TR{i}") for i in range(2)]
        MID = [bank(f"MID{i}") for i in range(2)]
        ACC = [bank(f"ACC{i}") for i in range(2)]
        UY = [bank(f"UY{i}") for i in range(2)]

        ld_ids = sem("ld_ids")
        ld_const = sem("ld_const")
        ids_step = sem("ids_step")
        idx_ready = sem("idx_ready")
        gathered = [sem(f"gathered{g}") for g in range(NG)]
        ident_step = sem("ident_step")
        ident_ready = sem("ident_ready")
        run_step = sem("run_step")
        asig_ready = sem("asig_ready")
        decay_ready = sem("decay_ready")
        ld_ssm = sem("ld_ssm")
        ld_w1 = sem("ld_w1")
        ld_w2 = sem("ld_w2")
        ld_par = sem("ld_par")
        par_ready = sem("par_ready")
        whi_done = sem("whi_done")
        wlo_done = sem("wlo_done")
        bn_done = sem("bn_done")
        mv_done = sem("mv_done")
        veps_done = sem("veps_done")
        rstd_ready = sem("rstd_ready")
        norm_ready = sem("norm_ready")
        tr_done = sem("tr_done")
        evac_done = sem("evac_done")
        lo_done = sem("lo_done")
        u_done = sem("u_done")
        scan_done = sem("scan_done")
        hshi_done = sem("hshi_done")
        hslo_done = sem("hslo_done")
        y_done = sem("y_done")
        xupd_done = sem("xupd_done")
        b2_done = sem("b2_done")
        up_done = sem("up_done")
        gelu_done = sem("gelu_done")
        glo_done = sem("glo_done")
        down_done = sem("down_done")
        x_ready = sem("x_ready")

        w1_d = w1.rearrange("l (h p) f -> l p h f", p=P)
        w2_d = w2.rearrange("l (f p) d -> l p f d", p=P)
        d_d = Dw.rearrange("l (h p) e -> l p h e", p=P)
        b_d = Bw.rearrange("l (h p) s -> l p h s", p=P)

        def at(ap, l):
            return ap[bass.ds(l, 1)].rearrange("o p h f -> (o p) h f")

        def xg(g):
            return x[:, bass.ds(g * GT, GT), :]

        primed = (b2_done, down_done, evac_done, gelu_done, glo_done, hshi_done, hslo_done, lo_done, mv_done,
                  norm_ready, par_ready, scan_done, tr_done, up_done, wlo_done, xupd_done, y_done)
        block = ctx.enter_context(nc.Block())

        @block.sync
        def _(sp):
            for s in primed:
                sp.sem_inc(s, 1)
            sp.dma_start(ids_sb[:], ids).then_inc(ld_ids, 16)
            sp.dma_start(pos_sb[:], pos[0:P, :]).then_inc(ld_const, 16)
            for i in range(2):
                sp.dma_start(a_col[S * i:S * i + S, :], A_diag).then_inc(ld_const, 16)
                sp.dma_start(lnf_sb[:, i, :], lnf[i:i + 1, :].partition_broadcast(P)).then_inc(ld_const, 16)
            with sp.Fori(0, L) as l:
                sp.wait_ge(wlo_done, 1 + l * 4)
                sp.wait_ge(par_ready, 1 + l * 2)
                sp.dma_start(st_d[:], at(d_d, l)).then_inc(ld_ssm, 16)
                for i in range(2):
                    sp.dma_start(st_b[:, :, i, :], at(b_d, l)).then_inc(ld_ssm, 16)
                    sp.dma_start(st_c[S * i:S * i + S, :], Cw[bass.ds(l, 1)].rearrange("o s d -> (o s) d")).then_inc(ld_ssm, 16)
                sp.dma_start(st_cols[:], cols[bass.ds(l, 1)].rearrange("o p c -> (o p) c")).then_inc(ld_par, 16)
                sp.dma_start(st_b2[:], b2[bass.ds(l, 1), :].partition_broadcast(P)).then_inc(ld_par, 16)
                sp.dma_start(st_w1[:], at(w1_d, l)).then_inc(ld_w1, 16)
                sp.dma_start(st_w2[:], at(w2_d, l)).then_inc(ld_w2, 16)

        @block.gpsimd
        def _(pool):
            def ln_rstd(n):
                pool.wait_ge(mv_done, 1 + n * GT + GT)
                pool.nop(nofuse=True)
                pool.wait_ge(norm_ready, 1 + n * GT)
                pool.nop(nofuse=True)
                pool.tensor_scalar(veps[:], mv[:, :, 1], EPS, None, ALU.add).then_inc(veps_done, 1)
                pool.wait_ge(veps_done, n + 2)
                pool.tensor_tensor(rstd[:], veps[:], half[:].to_broadcast([P, GT]), ALU.pow).then_inc(rstd_ready, 1)

            def pool_unit(k, g, last=False):
                if not last:
                    ln_rstd(2 * k + 1)
                n2 = 2 * k + 2 - last
                ln_rstd(n2)
                if True:
                    pool.wait_ge(norm_ready, 1 + n2 * GT + GT)
                    pool.tensor_tensor(xg(g), xg(g), b2_bc[:].unsqueeze(1).to_broadcast([P, GT, DM]), ALU.add).then_inc(b2_done, 1)

            pool.memset(half[:], -0.5).then_inc(veps_done, 1)
            pool.memset(ident[:], 0.0).then_inc(ident_step, 1)
            pool.memset(runmask[:], 1.0).then_inc(run_step, 1)
            pool.wait_ge(ident_step, 1)
            pool.affine_select(out=ident[:], in_=ident[:], compare_op=ALU.not_equal, fill=1.0, base=0,
                               pattern=[[-1, P]], channel_multiplier=1).then_inc(ident_ready, 1)
            pool.wait_ge(run_step, 1)
            pool.memset(runmask[:, :, 0:1], 0.0).then_inc(run_step, 1)
            pool.wait_ge(idx_ready, 1)
            for s in range(NSEQ):
                pool.indirect_dma_start(x[:, s, :], None, emb, bass.IndirectOffsetOnAxis(ap=idx[:, s:s + 1], axis=0))\
                    .then_inc(gathered[s // GT], 16)
            with pool.Fori(0, L) as l:
                pool.wait_ge(ld_par, l * 32 + 32)
                pool.wait_ge(gelu_done, 1 + l * (2 * NF * NG) + 2)
                pool.nop(nofuse=True)
                pool.tensor_copy(col[:], st_cols[:]).then_inc(par_ready, 1)
                pool.wait_ge(b2_done, 1 + l * NG)
                pool.nop(nofuse=True)
                pool.tensor_copy(b2_bc[:], st_b2[:]).then_inc(par_ready, 1)
                pool.wait_ge(par_ready, 1 + l * 2 + 2)
                ln_rstd(l * (2 * NG))
                with pool.Fori(0, NG - 1) as g:
                    pool_unit(l * NG + g, g)
                pool_unit(l * NG + NG - 1, NG - 1, last=True)

        @block.scalar
        def _(act):
            def evac(n, k, w, dst, halves=(0, 1)):
                for h in halves:
                    act.wait_ge(tr_done, 1 + n * 2 + h + 1)
                    if w == 0:
                        act.wait_ge(y_done, 1 + k * 2)
                    else:
                        act.wait_ge(up_done, 1 + k * NF)
                    act.wait_ge(lo_done, 1 + n * 2)
                    sc, bi = col[:, 4 * w + h:4 * w + h + 1], col[:, 4 * w + 2 + h:4 * w + 3 + h]
                    act.activation(dst[:, HI, h, :], TR[h][:], ACT.Identity, scale=sc, bias=bi).then_inc(evac_done, 1)
                    act.activation(full[:, h, :], TR[h][:], ACT.Identity, scale=sc, bias=bi).then_inc(evac_done, 1)

            def ssm_act(k, s, par, last=False):
                if s in (5, 6) and not last:
                    evac(2 * k + 1, k + 1, 0, h1, (s - 5,))
                elif s == 1:
                    act.wait_ge(scan_done, 1 + k + 1)
                    act.wait_ge(y_done, 1 + k * 2)
                    act.activation(hs_w[:, HI, :], hs[:], ACT.Copy).then_inc(hshi_done, 1)
                elif s == 7:
                    evac(2 * k + 2 - last, k, 1, h2[par])

            def gelu(k, f):
                m = f % 2
                act.wait_ge(up_done, 1 + k * NF + f + 1 + NF)
                act.wait_ge(down_done, 1 + k * NF + f)
                act.wait_ge(glo_done, 1 + k * NF + f)
                act.activation(g_w[:, m, HI, :], MID[m][:], ACT.Gelu, bias=col[:, 8 + f:9 + f]).then_inc(gelu_done, 1)
                act.activation(gfull[:, m, :], MID[m][:], ACT.Gelu, bias=col[:, 8 + f:9 + f]).then_inc(gelu_done, 1)

            act.sem_inc(gelu_done, 2)
            act.wait_ge(ld_const, 80)
            act.activation(a_sig[:], a_col[:], ACT.Sigmoid).then_inc(asig_ready, 1)
            act.wait_ge(asig_ready, 1)
            act.activation(a_col[:, 0:1], a_sig[:, 0:1], ACT.Gelu).then_inc(asig_ready, 1)
            with act.Fori(0, L) as l:
                act.wait_ge(ld_ssm, l * 80 + 80)
                act.wait_ge(y_done, 1 + l * (2 * NG))
                act.activation(d_w[:, HI], st_d[:], ACT.Copy).then_inc(whi_done, 1)
                act.activation(b_w[:, HI], st_b[:].rearrange("p h i s -> p h (i s)"), ACT.Copy).then_inc(whi_done, 1)
                act.activation(c_w[0:S, :], st_c[0:S, :], ACT.Copy).then_inc(whi_done, 1)
                act.activation(c_t[S:P, :], st_c[S:P, :], ACT.Copy).then_inc(whi_done, 1)
                act.wait_ge(down_done, 1 + l * (NG * NF) + 1)
                act.wait_ge(ld_w1, l * 16 + 16)
                act.activation(w1_w[:, HI], st_w1[:], ACT.Copy).then_inc(whi_done, 1)
                act.wait_ge(ld_w2, l * 16 + 16)
                act.activation(w2_w[:, HI], st_w2[:], ACT.Copy).then_inc(whi_done, 1)
                act.wait_ge(par_ready, 1 + l * 2 + 2)
                evac(l * (2 * NG), l * NG, 0, h1)
                for s in range(9):
                    ssm_act(l * NG, s, 0)
                def unit(k, par, last=False):
                    for f in range(9):
                        if f < NF:
                            gelu(k - 1, f)
                        ssm_act(k, f, par, last)
                with act.Fori(0, (NG - 2) // 2) as i:
                    unit(l * NG + i * 2 + 1, 1)
                    unit(l * NG + i * 2 + 2, 0)
                unit(l * NG + NG - 1, 1, last=True)
                for f in range(NF):
                    gelu(l * NG + NG - 1, f)

        @block.vector
        def _(dve):
            def ln_stats(n, g, ready, count):
                dve.wait_ge(ready, count)
                dve.wait_ge(mv_done, 1 + n * GT)
                dve.nop(nofuse=True)
                for t in range(GT):
                    dve.bn_stats(stats[:, t, :], x[:, bass.ds(g * GT + t, 1), :]).then_inc(bn_done, 1)
                dve.wait_ge(bn_done, n * GT + GT)
                dve.nop(nofuse=True)
                dve.wait_ge(norm_ready, 1 + n * GT)
                dve.nop(nofuse=True)
                for t in range(GT):
                    dve.bn_aggr(mv[:, t, :], stats[:, t, :]).then_inc(mv_done, 1)

            def ln_norm(n, g):
                dve.wait_ge(rstd_ready, n + 1)
                dve.wait_ge(tr_done, 1 + n * 2)
                for t in range(GT):
                    dve.tensor_scalar(hn[:, t, :], x[:, bass.ds(g * GT + t, 1), :], mv[:, t, 0:1], rstd[:, t:t + 1],
                                      ALU.subtract, ALU.mult).then_inc(norm_ready, 1)

            def lows(n, dst, halves=(0, 1)):
                for h in halves:
                    dve.wait_ge(evac_done, 1 + n * 4 + 2 * h + 2)
                    dve.tensor_tensor(dst[:, LO, h, :], full[:, h, :], dst[:, HI, h, :].bitcast(F32), ALU.subtract)\
                        .then_inc(lo_done, 1)

            def ssm_dve(k, g, s, par, last=False):
                n1, n2 = 2 * k + 1, 2 * k + 2 - last
                if s == 1:
                    dve.wait_ge(u_done, k + 1)
                    dve.wait_ge(hshi_done, 1 + k)
                    dve.wait_ge(hslo_done, 1 + k)
                    dve.tensor_tensor_scan(hs[:], decay[:].rearrange("p g t -> p (g t)"), UY[0][:], 0.0, ALU.mult, ALU.add)\
                        .then_inc(scan_done, 1)
                    dve.wait_ge(hshi_done, 1 + k + 1)
                    dve.tensor_tensor(hs_w[:, LO, :], hs[:], hs_w[:, HI, :].bitcast(F32), ALU.subtract).then_inc(hslo_done, 1)
                if s == 2 and not last:
                    ln_stats(n1, g + 1, x_ready, 2 * k + 4)
                if s == 3:
                    x_update(k, g, 0)
                    if not last:
                        ln_norm(n1, g + 1)
                if s == 4:
                    x_update(k, g, 1)
                    ln_stats(n2, g, xupd_done, 1 + 2 * k + 2)
                if s == 5:
                    if not last:
                        lows(n1, h1, (0,))
                    ln_norm(n2, g)
                if s == 6 and not last:
                    lows(n1, h1, (1,))
                if s == 7:
                    lows(n2, h2[par])

            def x_update(k, g, j):
                dve.wait_ge(y_done, 1 + k * 2 + j + 1)
                xx = x[:, bass.ds(g * GT + 2 * j, 2), :]
                dve.tensor_tensor(xx, xx, UY[j][:].rearrange("p (a d) -> p a d", a=2), ALU.add).then_inc(xupd_done, 1)

            def glo(k, f):
                m = f % 2
                dve.wait_ge(gelu_done, 1 + 2 * (k * NF + f) + 4)
                dve.tensor_tensor(g_w[:, m, LO, :], gfull[:, m, :], g_w[:, m, HI, :].bitcast(F32), ALU.subtract)\
                    .then_inc(glo_done, 1)

            def mlp_add(k, g):
                dve.wait_ge(down_done, 1 + k * NF + NF + 1)
                dve.wait_ge(b2_done, 1 + k + 1)
                for j in range(2):
                    xx = x[:, bass.ds(g * GT + 2 * j, 2), :]
                    dve.tensor_tensor(xx, xx, ACC[j][:].rearrange("p (a d) -> p a d", a=2), ALU.add).then_inc(x_ready, 1)

            dve.sem_inc(glo_done, 1)
            dve.wait_ge(ld_ids, 16)
            dve.tensor_copy(idf[:], ids_sb[:]).then_inc(ids_step, 1)
            dve.wait_ge(ids_step, 1)
            dve.tensor_scalar(idneg[:], idf[:], 0.0, float(V), ALU.is_lt, ALU.mult).then_inc(ids_step, 1)
            dve.wait_ge(ids_step, 2)
            dve.tensor_tensor(idneg[:], idneg[:], idf[:], ALU.add).then_inc(ids_step, 1)
            dve.wait_ge(ids_step, 3)
            dve.tensor_scalar(idx[:], idneg[:], 0.0, float(V - 1), ALU.max, ALU.min).then_inc(idx_ready, 1)
            dve.wait_ge(ld_const, 80)
            for g in range(NG):
                dve.wait_ge(gathered[g], 16 * GT)
                for j in range(2):
                    xx = x[:, g * GT + 2 * j:g * GT + 2 * j + 2, :]
                    dve.tensor_tensor(xx, xx, pos_sb[:].unsqueeze(1).to_broadcast([P, 2, DM]), ALU.add).then_inc(x_ready, 1)
            dve.wait_ge(asig_ready, 2)
            dve.wait_ge(run_step, 2)
            with dve.Fori(0, L) as l:
                dve.wait_ge(scan_done, 1 + l * NG)
                dve.tensor_scalar(decay[:], runmask[:], a_sig[:, bass.ds(l, 1)], None, ALU.mult).then_inc(decay_ready, 1)
                dve.wait_ge(decay_ready, l + 1)
                ln_stats(l * (2 * NG), 0, x_ready, l * (2 * NG) + 2)
                ln_norm(l * (2 * NG), 0)
                dve.wait_ge(whi_done, l * 6 + 4)
                dve.tensor_tensor(d_w[:, LO], st_d[:], d_w[:, HI].bitcast(F32), ALU.subtract).then_inc(wlo_done, 1)
                dve.tensor_tensor(b_w[:, LO], st_b[:].rearrange("p h i s -> p h (i s)"), b_w[:, HI].bitcast(F32), ALU.subtract)
                dve.tensor_tensor(c_w[S:P, :], st_c[S:P, :], c_t[S:P, :].bitcast(F32), ALU.subtract).then_inc(wlo_done, 1)
                lows(l * (2 * NG), h1)
                for s in range(9):
                    ssm_dve(l * NG, 0, s, 0)
                    if s == 2:
                        dve.wait_ge(whi_done, l * 6 + 5)
                        dve.tensor_tensor(w1_w[:, LO], st_w1[:], w1_w[:, HI].bitcast(F32), ALU.subtract).then_inc(wlo_done, 1)
                    if s == 4:
                        dve.wait_ge(whi_done, l * 6 + 6)
                        dve.tensor_tensor(w2_w[:, LO], st_w2[:], w2_w[:, HI].bitcast(F32), ALU.subtract).then_inc(wlo_done, 1)
                def unit(k, g, par, last=False):
                    for f in range(9):
                        if f < NF:
                            glo(k - 1, f)
                        ssm_dve(k, g, f, par, last)
                    mlp_add(k - 1, g - 1)
                with dve.Fori(0, (NG - 2) // 2) as i:
                    unit(l * NG + i * 2 + 1, i * 2 + 1, 1)
                    unit(l * NG + i * 2 + 2, i * 2 + 2, 0)
                unit(l * NG + NG - 1, NG - 1, 1, last=True)
                for f in range(NF):
                    glo(l * NG + NG - 1, f)
                mlp_add(l * NG + NG - 1, NG - 1)

        @block.tensor
        def _(pe):
            def transposes(n):
                pe.wait_ge(norm_ready, 1 + n * GT + GT)
                pe.wait_ge(evac_done, 1 + n * 4)
                for h in range(2):
                    for t in range(GT):
                        last = pe.transpose(TR[h][:, t * P:(t + 1) * P], hn[:, t, h * P:(h + 1) * P], ident[:])
                    last.then_inc(tr_done, 1)

            def ssm_pe(k, s, first=False, last=False):
                if s == 0:
                    n1 = 2 * k - 1 + first
                    pe.wait_ge(lo_done, 1 + n1 * 2 + 2)
                    pe.wait_ge(xupd_done, 1 + k * 2)
                    for i, (h, (a, b)) in enumerate([(h, p) for h in range(2) for p in PASSES]):
                        last = pe.matmul(UY[0][:], b_w[:, a, h, :], h1[:, b, h, :], start=(i == 0), stop=(i == 5))
                    last.then_inc(u_done, 1)
                if s in (2, 3):
                    j = s - 2
                    pe.wait_ge(hslo_done, 1 + k + 1)
                    for t in range(2 * j, 2 * j + 2):
                        o = UY[j][:, (t % 2) * DM:(t % 2 + 1) * DM]
                        tok = slice(t * P, (t + 1) * P)
                        pe.matmul(o, hs_w[:, HI, tok], c_w[:], start=True, stop=False)
                        pe.matmul(o, hs_w[:, LO, tok], c_w[:], start=False, stop=False)
                        for i, (h, (a, b)) in enumerate([(h, p) for h in range(2) for p in PASSES]):
                            last_mm = pe.matmul(o, h1[:, a, h, tok], d_w[:, b, h, :], start=False, stop=(i == 5))
                    last_mm.then_inc(y_done, 1)

            def transposes_pe(k, s, last=False):
                if s == 5 and not last:
                    transposes(2 * k + 1)
                if s == 7:
                    transposes(2 * k + 2 - last)

            def up(k, f, par, last=False):
                m = f % 2
                if f == 0:
                    n2 = 2 * k + 2 - last
                    pe.wait_ge(lo_done, 1 + n2 * 2 + 2)
                pe.wait_ge(gelu_done, 1 + 2 * (k * NF + f))
                fs = slice(f * P, (f + 1) * P)
                for i, (h, (a, b)) in enumerate([(h, p) for h in range(2) for p in PASSES]):
                    last = pe.matmul(MID[m][:], w1_w[:, a, h, fs], h2[par][:, b, h, :], start=(i == 0), stop=(i == 5))
                last.then_inc(up_done, 1)

            def down(k, f):
                m = f % 2
                if f == 0:
                    pe.wait_ge(x_ready, 2 * k + 2 * NG)
                pe.wait_ge(glo_done, 1 + k * NF + f + 2)
                for t in range(GT):
                    o = ACC[t // 2][:, (t % 2) * DM:(t % 2 + 1) * DM]
                    tok = slice(t * P, (t + 1) * P)
                    for i, (a, b) in enumerate(PASSES):
                        last = pe.matmul(o, g_w[:, m, a, tok], w2_w[:, b, f, :], start=(f == 0 and i == 0 and t % 2 == 0),
                                         stop=(f == NF - 1 and i == 2), skip_group_check=True)
                last.then_inc(down_done, 1)

            pe.sem_inc(up_done, NF)
            pe.sem_inc(down_done, 1)
            pe.wait_ge(ident_ready, 1)
            with pe.Fori(0, L) as l:
                transposes(l * (2 * NG))
                pe.wait_ge(wlo_done, 1 + l * 4 + 2)
                for s in range(9):
                    transposes_pe(l * NG, s)
                    ssm_pe(l * NG, s, first=True)
                pe.wait_ge(wlo_done, 1 + l * 4 + 4)
                pe.nop(nofuse=True)

                def unit(k, par, last=False):
                    for f in range(9):
                        if f < NF:
                            up(k - 1, f, 1 - par)
                        transposes_pe(k, f, last=last)
                        if f >= 1:
                            down(k - 1, f - 1)
                        ssm_pe(k, f, last=last)
                with pe.Fori(0, (NG - 2) // 2) as i:
                    unit(l * NG + i * 2 + 1, 1)
                    unit(l * NG + i * 2 + 2, 0)
                unit(l * NG + NG - 1, 1, last=True)
                for f in range(9):
                    if f < NF:
                        up(l * NG + NG - 1, f, 1, last=True)
                    if f >= 1:
                        down(l * NG + NG - 1, f - 1)


def attention(nc, sems, x, ident, half, lnf_sb, wqkv, wbm, wo, conv, norm_w, scr_g, scr_b, scr_t):
    NSEQ, DM = x.shape[1], x.shape[2]
    GT = 4
    NG = NSEQ // GT
    GN = GT * P
    NH2 = DM // P
    HD = 64
    NHD = DM // HD
    NQ = GT * NHD
    C = 32
    NC = P // C
    NCH = 3 * NH2
    NB = NG // 2

    with ExitStack() as ctx:
        def sb(name, shape, dt=F32):
            return ctx.enter_context(nc.sbuf_tensor(name, shape, dt))

        def sem(name):
            sems.append(nc.alloc_semaphore(name=name))
            return sems[-1]

        bk = [ctx.enter_context(nc.psum_tensor(f"bk{i}", [P, 512], F32)) for i in range(8)]
        TR, QKV, TOK, VT, BACK = bk[0:2], bk[2:4], bk[4:6], bk[6], bk[7]
        OT = (VT, BACK)
        CONV = (QKV[0], QKV[1], BACK)

        st_bm = sb("st_bm", [P, NH2, 2 * NHD])
        qkv_w = sb("qkv_w", [P, 2, NH2, 3 * DM], F32R)
        bm_w = sb("bm_w", [P, 2, NH2, P], F32R)
        bm_z = sb("bm_z", [P, 2, NH2, P])
        wo_w = sb("wo_w", [P, 2, NH2, DM], F32R)
        cw = sb("cw", [P, NCH, 4])
        nw = sb("nw", [P, 1])
        causal = sb("causal", [P, 2, P])
        strict = sb("strict", [P, C, C])
        tcm_f = sb("tcm", [P, (C + 1) * C])
        tcm = tcm_f[:, 0:C * C].rearrange("p (i j) -> p i j", j=C)

        stats = sb("stats2", [P, GT, 6])
        mv = sb("mv2", [P, GT, 2])
        veps = sb("veps2", [P, GT])
        rstd = sb("rstd2", [P, GT])
        hn = sb("hn2", [P, GT, DM])
        a_w = sb("a_w", [P, 2, NH2, GN], F32R)
        bmT = sb("bmT", [2 * NHD, GN])
        bm = sb("bm", [P, 2 * GT, 2 * NHD])
        cv = sb("cv", [P, 3, GN])
        sg = sb("sg", [P, 3, GN])
        qkv_t = sb("qkv_t", [P, NCH, GN])
        sq = sb("sq", [P, 2, GN])
        ss = sb("ss", [P, GT, 2 * NHD])
        sse = sb("sse", [P, GT, 2 * NHD])
        rs = sb("rs", [P, GT, 2 * NHD])
        qkn = sb("qkn", [P, 2, GN])
        qk_w = sb("qk_w", [P, 2, GT, 4, P], F16)
        v = sb("v", [P, 2 * GT, DM])
        graw = sb("graw", [P, NQ, P])
        st_qkv = graw[:].rearrange("p q t -> p (q t)")[:, 0:NH2 * 3 * DM].rearrange("p (h c) -> p h c", h=NH2)
        g_w = sb("g_w2", [P, 2, 2, NQ, P], F16)
        kq = sb("kq", [P, 2, 2, P])
        kq_w = sb("kq_w", [P, 2, 2, NQ, P], F16)
        gcm = sb("gcm", [P, C, C])
        bcm = sb("bcm", [P, C])
        acm_f = sb("acm", [P, (C + 1) * C])
        acm = acm_f[:, 0:C * C].rearrange("p (i j) -> p i j", j=C)
        prod = graw[:].rearrange("p q t -> p (q t)")
        xm = sb("xm", [P, 16, 16])
        scm = sb("scm", [P, C, C])
        t_w = sb("t_w", [P, C, 2, C], F16)
        tt = sb("tt", [P, 2 * NQ, 2, C], F16)
        r = sb("r", [P, NQ, HD])
        st_wo = r[:].rearrange("p q d -> p (q d)")[:, 0:NH2 * DM].rearrange("p (h c) -> p h c", h=NH2)
        r_w = sb("r_w", [P, 2, NQ, HD], F16)
        u_w = sb("u_w", [P, 2, NQ, HD], F16)
        om = qkv_t[:, 0:2, :].rearrange("p c n -> p (c n)").rearrange("p (t d) -> p t d", t=GT)
        vm = qkv_t[:, 2:4, :].rearrange("p c n -> p (c n)").rearrange("p (t d) -> p t d", t=GT)
        omix = sb("omix", [P, GT, NHD])
        full = sb("full2", [P, NH2, GN])

        names = """ld_w whi wlo masks bmz m_bn m_mv m_veps m_rstd m_norm fin1 fin2 tr_done a_hi a_lo
        bmT_done bm_sig bm_tr bm_done beta_out qkv_done tap0 conv_done sig_done silu_done tok_done v_tr v_done
        sq_done ss_done sse_done rs_done qkn_done back_done qk_hi qk_lo gk_done graw_done kq_done kq_hi kq_lo
        g_hi g_lo g_out gcm_in ps_r a_step t_hi t_lo t_out tt_in ps1 r_done r_hi r_lo ps2 u_hi u_lo o_done
        om1 vm1 omix1 osq oss osse ors o3 otr o_hi o_full o_lo wo_done x_out""".split()
        S = {n: sem("a_" + n) for n in names}

        xg = lambda g: x[:, bass.ds(g * GT, GT), :]
        primed = """a_lo a_step beta_out bm_tr g_out gcm_in gk_done kq_lo o_done o_lo om1 ors otr ps2 ps_r qk_lo
        qkn_done qkv_done rs_done silu_done t_hi tok_done tr_done u_lo v_tr vm1 wo_done x_out""".split()
        block = ctx.enter_context(nc.Block())

        @block.sync
        def _(sp):
            for n in primed:
                sp.sem_inc(S[n], 1)
            sp.dma_start(st_qkv, wqkv.rearrange("(h p) c -> p h c", p=P)).then_inc(S["ld_w"], 16)
            sp.dma_start(st_bm[:], wbm.rearrange("(h p) c -> p h c", p=P)).then_inc(S["ld_w"], 16)
            sp.dma_start(st_wo, wo.rearrange("(h p) c -> p h c", p=P)).then_inc(S["ld_w"], 16)
            sp.dma_start(cw[:], conv.rearrange("(c p) k -> p c k", p=P)).then_inc(S["ld_w"], 16)
            sp.dma_start(nw[:], norm_w).then_inc(S["ld_w"], 16)
            scr_b_v = scr_b.rearrange("(b s h) t -> h b s t", b=2, h=NHD)
            with sp.Fori(0, NB) as b:
                for gi in range(2):
                    m = b * 2 + gi
                    sp.wait_ge(S["bm_sig"], m + 1)
                    sp.wait_ge(S["gcm_in"], 1 + b * 32)
                    sp.dma_start(scr_b_v[:, gi], bmT[0:NHD, :].rearrange("h (s t) -> h s t", s=GT)).then_inc(S["beta_out"], 16)
                    sp.wait_ge(S["graw_done"], m * 8 + 8)
                    for n in range(NC):
                        src = graw[C * n:C * n + C, :, C * n:C * n + C]
                        dst = scr_g.rearrange("(g q n) i j -> g n i q j", g=2, n=NC)[gi, n]
                        sp.dma_start(dst, src).then_inc(S["g_out"], 16)
                sp.wait_ge(S["g_out"], 1 + b * 128 + 128)
                sp.nop(nofuse=True)
                sp.wait_ge(S["beta_out"], 1 + b * 32 + 32)
                sp.wait_ge(S["a_step"], 1 + b * 3)
                sp.dma_start(gcm[:], scr_g).then_inc(S["gcm_in"], 16)
                sp.dma_start(bcm[:], scr_b.rearrange("q (n i) -> (q n) i", n=NC)).then_inc(S["gcm_in"], 16)
                sp.wait_ge(S["t_lo"], b + 1)
                sp.dma_start(scr_t, t_w[:].rearrange("p j s i -> p j (s i)")).then_inc(S["t_out"], 16)
                sp.wait_ge(S["t_out"], b * 16 + 16)
                sp.nop(nofuse=True)
                sp.wait_ge(S["u_lo"], 1 + b * 16)
                for n in range(NC):
                    sp.dma_start(tt[C * n:C * n + C].rearrange("j q s i -> j q (s i)"),
                                 scr_t.rearrange("(q n) j x -> n j q x", n=NC)[n]).then_inc(S["tt_in"], 16)

        @block.gpsimd
        def _(pool):
            def rstd_of(n):
                pool.wait_ge(S["m_mv"], n * GT + GT)
                pool.nop(nofuse=True)
                pool.wait_ge(S["m_norm"], n * GT)
                pool.nop(nofuse=True)
                pool.tensor_scalar(veps[:], mv[:, :, 1], EPS, None, ALU.add).then_inc(S["m_veps"], 1)
                pool.wait_ge(S["m_veps"], n + 1)
                pool.tensor_tensor(rstd[:], veps[:], half[:].to_broadcast([P, GT]), ALU.pow).then_inc(S["m_rstd"], 1)

            pool.memset(bm_z[:], 0.0).then_inc(S["bmz"], 1)
            pool.memset(causal[:], 1.0).then_inc(S["masks"], 1)
            pool.memset(strict[:], -1.0).then_inc(S["masks"], 1)
            pool.memset(tcm, 0.0).then_inc(S["masks"], 1)
            pool.wait_ge(S["masks"], 3)
            pool.affine_select(out=causal[:], in_=causal[:], compare_op=ALU.is_ge, fill=0.0, base=0,
                               pattern=[[0, 2], [1, P]], channel_multiplier=-1).then_inc(S["masks"], 1)
            pool.affine_select(out=strict[:], in_=strict[:], compare_op=ALU.is_gt, fill=0.0, base=0,
                               pattern=[[1, C], [-1, C]], channel_multiplier=0).then_inc(S["masks"], 1)
            pool.affine_select(out=tcm, in_=tcm, compare_op=ALU.not_equal, fill=1.0, base=0,
                               pattern=[[1, C], [-1, C]], channel_multiplier=0).then_inc(S["masks"], 1)
            def batch(b, final=False):
                pool.wait_ge(S["x_out"], 1 + b * 4)
                for gi in range(2):
                    m = b * 2 + gi
                    ahead = not (final and gi == 1)
                    for c in range(NCH):
                        pool.wait_ge(S["sig_done"], m * NCH + c + 1)
                        pool.wait_ge(S["tok_done"], 1 + m * 4)
                        pool.wait_ge(S["v_tr"], 1 + m * 2)
                        pool.tensor_tensor(qkv_t[:, c, :], cv[:, c % 3, :], sg[:, c % 3, :], ALU.mult).then_inc(S["silu_done"], 1)
                    for t in range(GT):
                        pool.wait_ge(S["ss_done"], m * GT + t + 1)
                        pool.nop(nofuse=True)
                        pool.wait_ge(S["rs_done"], 1 + m * GT + t)
                        pool.nop(nofuse=True)
                        pool.tensor_scalar(sse[:, t, :], ss[:, t, :], L2_EPS, None, ALU.add).then_inc(S["sse_done"], 1)
                        pool.wait_ge(S["sse_done"], m * GT + t + 1)
                        pool.wait_ge(S["qkn_done"], 1 + m * GT)
                        pool.tensor_tensor(rs[:, t, :], sse[:, t, :], half[:].to_broadcast([P, 2 * NHD]), ALU.pow).then_inc(S["rs_done"], 1)
                        if ahead and t == 0:
                            rstd_of(2 * m + 2)
                    for j in range(8):
                        q2 = slice(4 * (j // 2) + j % 2, 4 * (j // 2) + 4, 2)
                        pool.wait_ge(S["kq_hi"], m * 8 + j + 1)
                        pool.tensor_tensor(kq_w[:, gi, LO, q2, :], kq[:, j % 2], kq_w[:, gi, HI, q2, :], ALU.subtract).then_inc(S["kq_lo"], 1)
                        pool.wait_ge(S["g_hi"], m * 8 + j + 1)
                        pool.tensor_tensor(g_w[:, gi, LO, q2, :], graw[:, q2, :], g_w[:, gi, HI, q2, :], ALU.subtract).then_inc(S["g_lo"], 1)
                    if ahead:
                        rstd_of(2 * m + 3)
                for gi in range(2):
                    m = b * 2 + gi
                    pool.wait_ge(S["omix1"], m + 1)
                    pool.wait_ge(S["otr"], 1 + m * 2)
                    pool.tensor_tensor(vm.rearrange("p t (h d) -> p t h d", h=NHD), v[:, gi * GT:gi * GT + GT, :].rearrange("p t (h d) -> p t h d", h=NHD),
                                       omix[:].unsqueeze(3).to_broadcast([P, GT, NHD, HD]), ALU.mult).then_inc(S["vm1"], 1)
                    pool.wait_ge(S["oss"], m + 1)
                    pool.nop(nofuse=True)
                    pool.tensor_scalar(sse[:, :, 0:NHD], ss[:, :, 0:NHD], 1.0 / HD, EPS, ALU.mult, ALU.add).then_inc(S["osse"], 1)
                    pool.wait_ge(S["osse"], m + 1)
                    pool.tensor_tensor(rs[:, :, 0:NHD], sse[:, :, 0:NHD], half[:].unsqueeze(2).to_broadcast([P, GT, NHD]), ALU.pow).then_inc(S["ors"], 1)

            rstd_of(0)
            rstd_of(1)
            with pool.Fori(0, NB - 1) as b:
                batch(b)
            batch(NB - 1, final=True)

        @block.scalar
        def _(act):
            def hi_qk(m, t):
                act.wait_ge(S["back_done"], m * GT + t + 1)
                act.wait_ge(S["gk_done"], 1 + m * 8)
                act.activation(qk_w[:, HI, t], BACK[:].rearrange("p (c t) -> p c t", c=4), ACT.Copy).then_inc(S["qk_hi"], 1)

            act.wait_ge(S["ld_w"], 80)
            act.activation(qkv_w[:, HI], st_qkv, ACT.Copy).then_inc(S["whi"], 1)
            act.wait_ge(S["bmz"], 2)
            act.activation(bm_w[:, HI], bm_z[:, 0], ACT.Copy).then_inc(S["whi"], 1)
            act.activation(wo_w[:, HI], st_wo, ACT.Copy).then_inc(S["whi"], 1)
            act.wait_ge(S["wlo"], 3)
            act.activation(sg[:, 0, 0:4], cw[:, 0, :], ACT.Sigmoid).then_inc(S["whi"], 1)
            act.wait_ge(S["whi"], 4)
            with act.Fori(0, NB) as b:
                act.wait_ge(S["x_out"], 1 + b * 4)
                for gi in range(2):
                    m = b * 2 + gi
                    for h in range(2):
                        act.wait_ge(S["tr_done"], 1 + m * 2 + h + 1)
                        act.wait_ge(S["qkv_done"], 1 + m * NCH)
                        act.activation(a_w[:, HI, h, :], TR[h][:], ACT.Copy).then_inc(S["a_hi"], 1)
                    for c in range(NCH + 1):
                        n = m * NCH + c
                        if c < NCH:
                            act.wait_ge(S["qkv_done"], 1 + n + 1)
                            act.wait_ge(S["silu_done"], 1 + (n - 2 if c >= 3 else m * NCH))
                            act.activation(cv[:, c % 3, :], CONV[c % 3][:], ACT.Copy, scale=cw[:, c, 3:4]).then_inc(S["tap0"], 1)
                        if c >= 1:
                            d = (c - 1) % 3
                            act.wait_ge(S["conv_done"], n * 3)
                            act.activation(sg[:, d, :], cv[:, d, :], ACT.Sigmoid).then_inc(S["sig_done"], 1)
                        if c == 5:
                            act.wait_ge(S["bmT_done"], m + 1)
                            act.wait_ge(S["bm_tr"], 1 + m)
                            act.wait_ge(S["beta_out"], 1 + m * 16)
                            act.activation(bmT[:], TR[0][0:2 * NHD, :], ACT.Sigmoid).then_inc(S["bm_sig"], 1)
                    act.wait_ge(S["bm_tr"], 1 + m + 1)
                    act.activation(bm[:, gi * GT:gi * GT + GT, :], VT[:, 0:GT * 2 * NHD].rearrange("p (t c) -> p t c", t=GT), ACT.Copy).then_inc(S["bm_done"], 1)
                    for t in range(GT):
                        act.wait_ge(S["tok_done"], 1 + m * 4 + t + 1)
                        if t >= 2:
                            act.wait_ge(S["ss_done"], m * GT + t - 1)
                        act.activation(sq[:, t % 2, :], TOK[t % 2][:], ACT.Square).then_inc(S["sq_done"], 1)
                        if t % 2 == 1:
                            act.wait_ge(S["v_tr"], 1 + m * 2 + t // 2 + 1)
                            act.activation(v[:, gi * GT + t - 1:gi * GT + t + 1, :], VT[:].rearrange("p (t d) -> p t d", t=2), ACT.Copy).then_inc(S["v_done"], 1)
                        if t >= 1:
                            hi_qk(m, t - 1)
                    hi_qk(m, GT - 1)
                    for j in range(8):
                        q2 = slice(4 * (j // 2) + j % 2, 4 * (j // 2) + 4, 2)
                        gb = QKV[j % 2][:].rearrange("p (h c t) -> p h c t", h=2, c=2)
                        act.wait_ge(S["gk_done"], 1 + m * 8 + j + 1)
                        act.wait_ge(S["g_out"], 1 + m * 64)
                        act.activation(graw[:, q2, :], gb[:, :, 1, :], ACT.Copy).then_inc(S["graw_done"], 1)
                        act.wait_ge(S["kq_done"], m * 8 + j + 1)
                        act.activation(kq_w[:, gi, HI, q2, :], kq[:, j % 2], ACT.Copy).then_inc(S["kq_hi"], 1)
                        act.wait_ge(S["graw_done"], m * 8 + j + 1)
                        act.activation(g_w[:, gi, HI, q2, :], graw[:, q2, :], ACT.Copy).then_inc(S["g_hi"], 1)
                act.wait_ge(S["a_step"], 1 + b * 3 + 3)
                act.activation(t_w[:, :, 0, :], scm[:], ACT.Copy).then_inc(S["t_hi"], 1)
                def chunk(gi, n, beside=None):
                    m = b * 2 + gi
                    rows = slice(C * n, C * n + C)
                    for j in range(2):
                        q8 = slice(8 * j, 8 * j + 8)
                        if n == 0:
                            act.wait_ge(S["v_done"], m * 2 + 2)
                            act.wait_ge(S["ps2"], 1 + m * 8)
                            act.activation(r_w[rows, HI, q8, :], v[rows, gi * GT + 2 * j:gi * GT + 2 * j + 2, :].rearrange("p t (h d) -> p (t h) d", h=NHD), ACT.Copy).then_inc(S["r_hi"], 1)
                        else:
                            act.wait_ge(S["r_done"], m * 6 + (n - 1) * 2 + j + 1)
                            act.activation(r_w[rows, HI, q8, :], r[rows, q8, :], ACT.Copy).then_inc(S["r_hi"], 1)
                    for j in range(2):
                        q8 = slice(8 * j, 8 * j + 8)
                        act.wait_ge(S["ps2"], 1 + m * 8 + n * 2 + j + 1)
                        act.wait_ge(S["o_done"], 1 + m * 2)
                        act.activation(u_w[rows, HI, q8, :], QKV[j][rows, :].rearrange("p (q d) -> p q d", q=8), ACT.Copy).then_inc(S["u_hi"], 1)

                def squares(m):
                    act.wait_ge(S["om1"], 1 + m * 4 + 4)
                    act.wait_ge(S["o_lo"], 1 + m * 2)
                    act.activation(full[:], om.rearrange("p t d -> p (t d)").rearrange("p (h n) -> p h n", h=2), ACT.Square).then_inc(S["osq"], 1)

                def split(m):
                    for h in range(2):
                        act.wait_ge(S["otr"], 1 + m * 2 + h + 1)
                        act.wait_ge(S["oss"], m + 1)
                        act.wait_ge(S["wo_done"], 1 + m * 2)
                        act.activation(a_w[:, HI, h, :], OT[h][:], ACT.Copy, scale=nw[:]).then_inc(S["o_hi"], 1)
                        act.activation(full[:, h, :], OT[h][:], ACT.Copy, scale=nw[:]).then_inc(S["o_full"], 1)

                for n in range(NC):
                    chunk(0, n)
                for n in range(NC):
                    chunk(1, n)
                    if n == 1:
                        squares(2 * b)
                split(2 * b)
                squares(2 * b + 1)
                split(2 * b + 1)

        @block.vector
        def _(dve):
            def lo_qk(m, t):
                dve.wait_ge(S["qk_hi"], m * GT + t + 1)
                dve.tensor_tensor(qk_w[:, LO, t], BACK[:].rearrange("p (c t) -> p c t", c=4), qk_w[:, HI, t], ALU.subtract).then_inc(S["qk_lo"], 1)

            def stats_of(n, g):
                dve.wait_ge(S["m_mv"], n * GT)
                dve.nop(nofuse=True)
                for t in range(GT):
                    dve.bn_stats(stats[:, t, :], x[:, bass.ds(g * GT + t, 1), :]).then_inc(S["m_bn"], 1)
                dve.wait_ge(S["m_bn"], n * GT + GT)
                dve.nop(nofuse=True)
                dve.wait_ge(S["m_norm"], n * GT)
                dve.nop(nofuse=True)
                for t in range(GT):
                    dve.bn_aggr(mv[:, t, :], stats[:, t, :]).then_inc(S["m_mv"], 1)

            dve.wait_ge(S["ld_w"], 80)
            dve.wait_ge(S["bmz"], 1)
            dve.tensor_copy(bm_z[:, 0, :, 0:2 * NHD], st_bm[:]).then_inc(S["bmz"], 1)
            dve.wait_ge(S["whi"], 3)
            dve.tensor_tensor(qkv_w[:, LO], st_qkv, qkv_w[:, HI].bitcast(F32), ALU.subtract).then_inc(S["wlo"], 1)
            dve.tensor_tensor(bm_w[:, LO], bm_z[:, 0], bm_w[:, HI].bitcast(F32), ALU.subtract).then_inc(S["wlo"], 1)
            dve.tensor_tensor(wo_w[:, LO], st_wo, wo_w[:, HI].bitcast(F32), ALU.subtract).then_inc(S["wlo"], 1)
            dve.wait_ge(S["masks"], 6)
            def norm_stats(m):
                stats_of(2 * m, m)

            def norm_apply(m):
                dve.wait_ge(S["m_rstd"], 2 * m + 1)
                for t in range(GT):
                    xx = x[:, bass.ds(m * GT + t, 1), :]
                    dve.tensor_scalar(xx, xx, mv[:, t, 0:1], rstd[:, t:t + 1], ALU.subtract, ALU.mult).then_inc(S["m_norm"], 1)

            def norm_scale(m):
                dve.wait_ge(S["m_norm"], 2 * m * GT + GT)
                dve.tensor_tensor(xg(m), xg(m), lnf_sb[:, 0:1, :].to_broadcast([P, GT, DM]), ALU.mult).then_inc(S["fin1"], 1)

            def norm_shift(m):
                dve.wait_ge(S["fin1"], m + 1)
                dve.tensor_tensor(xg(m), xg(m), lnf_sb[:, 1:2, :].to_broadcast([P, GT, DM]), ALU.add).then_inc(S["fin2"], 1)

            def attn_stats(m):
                dve.wait_ge(S["fin2"], m + 1)
                stats_of(2 * m + 1, m)

            def batch(b, final=False):
                for gi in range(2):
                    m = b * 2 + gi
                    ahead = not (final and gi == 1)
                    dve.wait_ge(S["m_rstd"], 2 * m + 2)
                    dve.wait_ge(S["tr_done"], 1 + m * 2)
                    dve.wait_ge(S["otr"], 1 + b * 4)
                    for t in range(GT):
                        dve.tensor_scalar(hn[:, t, :], x[:, bass.ds(m * GT + t, 1), :], mv[:, t, 0:1], rstd[:, t:t + 1], ALU.subtract, ALU.mult)\
                            .then_inc(S["m_norm"], 1)
                    for h in range(2):
                        dve.wait_ge(S["a_hi"], m * 2 + h + 1)
                        dve.tensor_tensor(a_w[:, LO, h, :], TR[h][:], a_w[:, HI, h, :].bitcast(F32), ALU.subtract).then_inc(S["a_lo"], 1)
                    for c in range(NCH):
                        n = m * NCH + c
                        dve.wait_ge(S["tap0"], n + 1)
                        src = CONV[c % 3][:].rearrange("p (s t) -> p s t", s=GT)
                        dst = cv[:, c % 3, :].rearrange("p (s t) -> p s t", s=GT)
                        for k in range(1, 4):
                            if k > 1:
                                dve.wait_ge(S["conv_done"], n * 3 + k - 1)
                            dve.scalar_tensor_tensor(dst[:, :, k:P], src[:, :, 0:P - k], cw[:, c, 3 - k:4 - k], dst[:, :, k:P], ALU.mult, ALU.add)\
                                .then_inc(S["conv_done"], 1)
                    for t in range(GT):
                        dve.wait_ge(S["sq_done"], m * GT + t + 1)
                        if t == 0:
                            dve.wait_ge(S["ors"], 1 + b * 2)
                        dve.tensor_reduce(ss[:, t, :], sq[:, t % 2, :].rearrange("p (h d) -> p h d", d=HD), AX.X, ALU.add).then_inc(S["ss_done"], 1)
                        dve.wait_ge(S["rs_done"], 1 + m * GT + t + 1)
                        if t >= 2:
                            dve.wait_ge(S["back_done"], m * GT + t - 1)
                        dve.tensor_tensor(qkn[:, t % 2, :].rearrange("p (h d) -> p h d", d=HD), TOK[t % 2][:].rearrange("p (h d) -> p h d", d=HD),
                                          rs[:, t, :].unsqueeze(2).to_broadcast([P, 2 * NHD, HD]), ALU.mult).then_inc(S["qkn_done"], 1)
                        if t >= 1:
                            lo_qk(m, t - 1)
                        if ahead:
                            (norm_stats, norm_apply, norm_scale, norm_shift)[t](m + 1)
                    lo_qk(m, GT - 1)
                    if ahead:
                        attn_stats(m + 1)
                    for j in range(8):
                        gb = QKV[j % 2][:].rearrange("p (h c t) -> p h c t", h=2, c=2)
                        dve.wait_ge(S["graw_done"], m * 8 + j + 1)
                        if j >= 2:
                            dve.wait_ge(S["kq_lo"], 1 + m * 8 + j - 1)
                        else:
                            dve.wait_ge(S["kq_lo"], 1 + m * 8)
                        dve.tensor_tensor(kq[:, j % 2], gb[:, :, 0, :], causal[:], ALU.mult).then_inc(S["kq_done"], 1)
                dve.wait_ge(S["gcm_in"], 1 + b * 32 + 32)
                dve.tensor_tensor(acm, gcm[:], bcm[:].unsqueeze(2).to_broadcast([P, C, C]), ALU.mult).then_inc(S["a_step"], 1)
                dve.wait_ge(S["a_step"], 1 + b * 3 + 1)
                dve.tensor_tensor(acm, acm, strict[:], ALU.mult).then_inc(S["a_step"], 1)
                dve.wait_ge(S["a_step"], 1 + b * 3 + 2)
                dve.wait_ge(S["g_lo"], b * 16 + 16)
                diag = lambda f: f.rearrange("p (d x) -> p d x", d=4)[:, :, 0:8 * C].rearrange("p d (i j) -> p d i j", j=C)
                acm_d, tcm_d = diag(acm_f[:]), diag(tcm_f[:])
                for i in range(1, 8):
                    pr = prod[:, 0:4 * i * i].rearrange("p (d k j) -> p d k j", d=4, j=i)
                    base = b * 30 + 2 * (i - 1)
                    dve.wait_ge(S["ps_r"], 1 + base)
                    dve.tensor_tensor(pr, acm_d[:, :, i, 0:i].unsqueeze(2).to_broadcast([P, 4, i, i]),
                                      tcm_d[:, :, 0:i, 0:i].rearrange("p d j k -> p d k j"), ALU.mult).then_inc(S["ps_r"], 1)
                    dve.wait_ge(S["ps_r"], 1 + base + 1)
                    dve.tensor_reduce(tcm_d[:, :, i, 0:i], pr, AX.X, ALU.add).then_inc(S["ps_r"], 1)

                def product(out, left, right, count, first=0):
                    ni, nj, nk = left.shape[1], left.shape[2], right.shape[2]
                    pr = prod[:, first:first + ni * nk * nj].rearrange("p (i k j) -> p i k j", i=ni, j=nj)
                    dve.wait_ge(S["ps_r"], 1 + count)
                    dve.tensor_tensor(pr, left.unsqueeze(2).to_broadcast([P, ni, nk, nj]),
                                      right.rearrange("p j k -> p k j").unsqueeze(1).to_broadcast([P, ni, nk, nj]), ALU.mult).then_inc(S["ps_r"], 1)
                    dve.wait_ge(S["ps_r"], 1 + count + 1)
                    dve.tensor_reduce(out, pr, AX.X, ALU.add).then_inc(S["ps_r"], 1)

                r0 = b * 30 + 14
                for e in range(2):
                    o, q, r8 = 16 * e, 16 * e + 8, 16 * e + 16
                    product(xm[:, 8 * e:8 * e + 8, 0:8], acm[:, q:r8, o:q], tcm[:, o:q, o:q], r0 + 4 * e)
                    product(tcm[:, q:r8, o:q], tcm[:, q:r8, q:r8], xm[:, 8 * e:8 * e + 8, 0:8], r0 + 4 * e + 2)
                r1 = r0 + 8
                product(xm[:, :, 0:8], acm[:, 16:32, 0:16], tcm[:, 0:16, 0:8], r1)
                product(xm[:, :, 8:16], acm[:, 16:32, 8:16], tcm[:, 8:16, 8:16], r1 + 2)
                product(tcm[:, 16:24, 0:16], tcm[:, 16:24, 16:24], xm[:, 0:8, :], r1 + 4)
                product(tcm[:, 24:32, 0:16], tcm[:, 24:32, 16:32], xm[:, :, :], r1 + 6)
                dve.wait_ge(S["ps_r"], 1 + b * 30 + 30)
                dve.wait_ge(S["t_hi"], 1 + b)
                dve.tensor_tensor(scm[:], tcm.rearrange("p i j -> p j i"), bcm[:].unsqueeze(2).to_broadcast([P, C, C]), ALU.mult).then_inc(S["a_step"], 1)
                dve.wait_ge(S["a_step"], 1 + b * 3 + 3)
                dve.wait_ge(S["t_hi"], 1 + b + 1)
                dve.tensor_tensor(t_w[:, :, 1, :], scm[:], t_w[:, :, 0, :], ALU.subtract).then_inc(S["t_lo"], 1)
                def chunk(gi, n, beside=()):
                    m = b * 2 + gi
                    vq = v[:, gi * GT:gi * GT + GT, :].rearrange("p t (h d) -> p (t h) d", h=NHD)
                    rows = slice(C * n, C * n + C)
                    for j in range(2):
                        q8 = slice(8 * j, 8 * j + 8)
                        if n > 0:
                            dve.wait_ge(S["ps1"], m * 6 + (n - 1) * 2 + j + 1)
                            dve.tensor_tensor(r[rows, q8, :], vq[rows, q8, :], TR[j][rows, :].rearrange("p (q d) -> p q d", q=8), ALU.subtract).then_inc(S["r_done"], 1)
                    for j in range(2):
                        q8 = slice(8 * j, 8 * j + 8)
                        dve.wait_ge(S["r_hi"], m * 8 + 2 * n + j + 1)
                        dve.tensor_tensor(r_w[rows, LO, q8, :], (vq if n == 0 else r)[rows, q8, :], r_w[rows, HI, q8, :], ALU.subtract).then_inc(S["r_lo"], 1)
                    for work in beside[0:1]:
                        work()
                    for j in range(2):
                        q8 = slice(8 * j, 8 * j + 8)
                        dve.wait_ge(S["u_hi"], m * 8 + 2 * n + j + 1)
                        dve.tensor_tensor(u_w[rows, LO, q8, :], QKV[j][rows, :].rearrange("p (q d) -> p q d", q=8), u_w[rows, HI, q8, :], ALU.subtract).then_inc(S["u_lo"], 1)
                    for work in beside[1:2]:
                        work()

                def one_minus_mix(gi):
                    m = b * 2 + gi
                    dve.wait_ge(S["vm1"], 1 + m)
                    dve.tensor_scalar(omix[:], bm[:, gi * GT:gi * GT + GT, NHD:2 * NHD], -1.0, 1.0, ALU.mult, ALU.add).then_inc(S["omix1"], 1)

                def mixed(gi, j):
                    m = b * 2 + gi
                    mix = bm[:, gi * GT:gi * GT + GT, NHD:2 * NHD]
                    dve.wait_ge(S["o_done"], 1 + m * 2 + j + 1)
                    dve.wait_ge(S["otr"], 1 + m * 2)
                    dve.tensor_tensor(om[:, 2 * j:2 * j + 2, :].rearrange("p t (h d) -> p t h d", h=NHD), TOK[j][:].rearrange("p (t h d) -> p t h d", t=2, h=NHD),
                                      mix[:, 2 * j:2 * j + 2].unsqueeze(3).to_broadcast([P, 2, NHD, HD]), ALU.mult).then_inc(S["om1"], 1)

                def add_v(gi):
                    m = b * 2 + gi
                    dve.wait_ge(S["vm1"], 1 + m + 1)
                    dve.wait_ge(S["om1"], 1 + m * 4 + 2)
                    dve.tensor_tensor(om, om, vm, ALU.add).then_inc(S["om1"], 2)

                def sum_squares(gi):
                    m = b * 2 + gi
                    dve.wait_ge(S["osq"], m + 1)
                    dve.tensor_reduce(ss[:, :, 0:NHD], full[:].rearrange("p a n -> p (a n)").rearrange("p (t h d) -> p t h d", t=GT, h=NHD), AX.X, ALU.add).then_inc(S["oss"], 1)

                def scaled(gi):
                    m = b * 2 + gi
                    dve.wait_ge(S["ors"], 1 + m + 1)
                    dve.tensor_tensor(om.rearrange("p t (h d) -> p t h d", h=NHD), om.rearrange("p t (h d) -> p t h d", h=NHD),
                                      rs[:, :, 0:NHD].unsqueeze(3).to_broadcast([P, GT, NHD, HD]), ALU.mult).then_inc(S["o3"], 1)

                def low_parts(gi):
                    m = b * 2 + gi
                    for h in range(2):
                        dve.wait_ge(S["o_full"], m * 2 + h + 1)
                        dve.tensor_tensor(a_w[:, LO, h, :], full[:, h, :], a_w[:, HI, h, :].bitcast(F32), ALU.subtract).then_inc(S["o_lo"], 1)

                def add_out(gi):
                    m = b * 2 + gi
                    for j in range(2):
                        dve.wait_ge(S["wo_done"], 1 + m * 2 + j + 1)
                        xx = x[:, bass.ds(m * GT + 2 * j, 2), :]
                        dve.tensor_tensor(xx, xx, OT[j][:].rearrange("p (a d) -> p a d", a=2), ALU.add).then_inc(S["x_out"], 1)

                for n in range(NC):
                    chunk(0, n)
                chunk(1, 0, (lambda: one_minus_mix(0), lambda: mixed(0, 0)))
                chunk(1, 1, (lambda: mixed(0, 1), lambda: add_v(0)))
                chunk(1, 2, (lambda: sum_squares(0), lambda: None))
                chunk(1, 3, (lambda: scaled(0), lambda: None))
                low_parts(0)
                one_minus_mix(1)
                mixed(1, 0)
                mixed(1, 1)
                add_out(0)
                add_v(1)
                sum_squares(1)
                scaled(1)
                low_parts(1)
                add_out(1)

            norm_stats(0)
            norm_apply(0)
            norm_scale(0)
            norm_shift(0)
            attn_stats(0)
            with dve.Fori(0, NB - 1) as b:
                batch(b)
            batch(NB - 1, final=True)

        @block.tensor
        def _(pe):
            def back(m, t):
                pe.wait_ge(S["qkn_done"], 1 + m * GT + t + 1)
                pe.wait_ge(S["qk_lo"], 1 + m * GT + t)
                for c in range(4):
                    last = pe.transpose(BACK[:, c * P:(c + 1) * P], qkn[:, t % 2, c * P:(c + 1) * P], ident[:])
                last.then_inc(S["back_done"], 1)

            hp = [(h, p) for h in range(2) for p in PASSES]
            pe.wait_ge(S["wlo"], 3)
            with pe.Fori(0, NB) as b:
                pe.wait_ge(S["x_out"], 1 + b * 4)
                for gi in range(2):
                    m = b * 2 + gi
                    pe.wait_ge(S["m_norm"], (2 * m + 2) * GT)
                    pe.wait_ge(S["a_lo"], 1 + m * 2)
                    pe.wait_ge(S["o_lo"], 1 + b * 4)
                    for h in range(2):
                        for t in range(GT):
                            last = pe.transpose(TR[h][:, t * P:(t + 1) * P], hn[:, t, h * P:(h + 1) * P], ident[:])
                        last.then_inc(S["tr_done"], 1)
                    pe.wait_ge(S["a_lo"], 1 + m * 2 + 2)
                    for c in range(NCH):
                        n = m * NCH + c
                        if c >= 3:
                            pe.wait_ge(S["conv_done"], (n - 2) * 3)
                        elif c == 2:
                            pe.wait_ge(S["qk_lo"], 1 + m * GT)
                        for i, (h, (p, q)) in enumerate(hp):
                            last = pe.matmul(CONV[c % 3][:], qkv_w[:, p, h, c * P:(c + 1) * P], a_w[:, q, h, :], start=(i == 0), stop=(i == 5))
                        last.then_inc(S["qkv_done"], 1)
                        if c == 3:
                            for i, (h, (p, q)) in enumerate(hp):
                                last = pe.matmul(TR[0][:], bm_w[:, p, h, :], a_w[:, q, h, :], start=(i == 0), stop=(i == 5))
                            last.then_inc(S["bmT_done"], 1)
                    pe.wait_ge(S["bm_sig"], m + 1)
                    pe.nop(nofuse=True)
                    for t in range(GT):
                        last = pe.transpose(VT[:, t * 2 * NHD:(t + 1) * 2 * NHD], bmT[:, t * P:(t + 1) * P], ident[0:2 * NHD, 0:2 * NHD])
                    last.then_inc(S["bm_tr"], 1)
                    pe.wait_ge(S["bm_done"], m + 1)
                    for t in range(GT):
                        pe.wait_ge(S["silu_done"], 1 + (m * NCH + (4 if t == 0 else 6)))
                        if t >= 2:
                            pe.wait_ge(S["qkn_done"], 1 + m * GT + t - 1)
                        for c in range(4):
                            last = pe.transpose(TOK[t % 2][:, c * P:(c + 1) * P], qkv_t[:, c, t * P:(t + 1) * P], ident[:])
                        last.then_inc(S["tok_done"], 1)
                        pe.wait_ge(S["silu_done"], 1 + m * NCH + 6)
                        if t == 2:
                            pe.wait_ge(S["v_done"], m * 2 + 1)
                        for c in range(2):
                            last = pe.transpose(VT[:, (t % 2) * DM + c * P:(t % 2) * DM + (c + 1) * P], qkv_t[:, 4 + c, t * P:(t + 1) * P], ident[:])
                        if t % 2 == 1:
                            last.then_inc(S["v_tr"], 1)
                        if t >= 1:
                            back(m, t - 1)
                    back(m, GT - 1)
                    for j in range(8):
                        t = j // 2
                        pe.wait_ge(S["qk_lo"], 1 + m * GT + t + 1)
                        if j >= 2:
                            pe.wait_ge(S["kq_done"], m * 8 + j - 1)
                        for hh in range(2):
                            hd = j % 2 + 2 * hh
                            rows = slice((hd % 2) * HD, (hd % 2) * HD + HD)
                            for i, (p, q) in enumerate(PASSES):
                                o = QKV[j % 2][:, hh * 256:(hh + 1) * 256].rearrange("p (c t) -> p c t", c=2)
                                last = pe.matmul(o, qk_w[rows, p, t, 2 + hd // 2, :], qk_w[rows, q, t, hd // 2::2, :], start=(i == 0), stop=(i == 2))
                        last.then_inc(S["gk_done"], 1)
                pe.wait_ge(S["tt_in"], b * 64 + 64)
                pe.wait_ge(S["kq_lo"], 1 + b * 16 + 16)
                pe.nop(nofuse=True)
                pe.wait_ge(S["g_lo"], b * 16 + 16)

                def chunk(gi, n):
                    m = b * 2 + gi
                    rows = slice(C * n, C * n + C)
                    if n > 0:
                        for j in range(2):
                            pe.wait_ge(S["u_lo"], 1 + m * 8 + (n - 1) * 2 + j + 1)
                            pe.nop(nofuse=True)
                            for q in range(8 * j, 8 * j + 8):
                                for i, (p, s) in enumerate(PASSES):
                                    last = pe.matmul(TR[j][rows, (q % 8) * HD:(q % 8 + 1) * HD], g_w[0:C * n, gi, p, q, rows], u_w[0:C * n, s, q, :],
                                                     start=(i == 0), stop=(i == 2))
                            last.then_inc(S["ps1"], 1)
                    for j in range(2):
                        pe.wait_ge(S["r_lo"], m * 8 + 2 * n + j + 1)
                        pe.nop(nofuse=True)
                        for q in range(8 * j, 8 * j + 8):
                            for i, (p, s) in enumerate(PASSES):
                                last = pe.matmul(QKV[j][rows, (q % 8) * HD:(q % 8 + 1) * HD], tt[rows, gi * NQ + q, p, :], r_w[rows, s, q, :],
                                                 start=(i == 0), stop=(i == 2))
                        last.then_inc(S["ps2"], 1)

                def outputs(gi):
                    m = b * 2 + gi
                    for j in range(2):
                        pe.wait_ge(S["u_lo"], 1 + m * 8 + 6 + j + 1)
                        pe.wait_ge(S["om1"], 1 + m * 4)
                        for q in range(8 * j, 8 * j + 8):
                            for i, (p, s) in enumerate(PASSES):
                                last = pe.matmul(TOK[j][:, (q % 8) * HD:(q % 8 + 1) * HD], kq_w[:, gi, p, q, :], u_w[:, s, q, :], start=(i == 0), stop=(i == 2))
                        last.then_inc(S["o_done"], 1)

                def turned(gi):
                    m = b * 2 + gi
                    pe.wait_ge(S["o3"], m + 1)
                    pe.wait_ge(S["x_out"], 1 + m * 2)
                    for h in range(2):
                        for t in range(GT):
                            last = pe.transpose(OT[h][:, t * P:(t + 1) * P], om[:, t, h * P:(h + 1) * P], ident[:])
                        last.then_inc(S["otr"], 1)

                def wo_product(gi):
                    m = b * 2 + gi
                    pe.wait_ge(S["o_lo"], 1 + m * 2 + 2)
                    for j in range(2):
                        for t in range(2 * j, 2 * j + 2):
                            tok = slice(t * P, (t + 1) * P)
                            for i, (h, (p, q)) in enumerate(hp):
                                last = pe.matmul(OT[j][:, (t % 2) * DM:(t % 2 + 1) * DM], a_w[:, p, h, tok], wo_w[:, q, h, :], start=(i == 0), stop=(i == 5))
                        last.then_inc(S["wo_done"], 1)

                for n in range(NC):
                    chunk(0, n)
                outputs(0)
                for n in range(NC):
                    chunk(1, n)
                turned(0)
                outputs(1)
                wo_product(0)
                turned(1)
                wo_product(1)


def slot_tiles(tokens, E, K=2):
    n = K * tokens // P + E
    return n + n % 2


def experts(nc, sems, x, ident, half, slots, y_d, wr, wgu, bias, wd, out):
    NSEQ, DM = x.shape[1], x.shape[2]
    GT = 4
    NG = NSEQ // GT
    GN = GT * P
    E = wr.shape[1]
    INTER = wd.shape[1]
    LIMIT, ALPHA = 7.0, 1.702
    NT = slot_tiles(NSEQ * P, E)
    NP = NT // 2
    TMAX = 2 * NSEQ
    assert INTER == P
    with ExitStack() as ctx:
        def sb(name, shape, dt=F32, where=ctx):
            return where.enter_context(nc.sbuf_tensor(name, shape, dt))

        bk = [ctx.enter_context(nc.psum_tensor(f"mk{i}", [P, 512], F32)) for i in range(8)]
        TRX, GU, AT, DN = bk[0:2], bk[2:4], bk[4:6], bk[6:8]
        LGT, LGB, WITHIN, TOTAL = GU[0], GU[1], AT[0], AT[1]
        m_all = sb("m_all", [P, NSEQ, DM])
        gu_w = sb("gu_w", [P, 2, E, 2, 2 * P], F32R)
        bias_w = sb("bias_w", [P, E, 2, DM], BF16)
        sel = sb("sel", [P, P], BF16)
        pos_i = sb("pos_i", [P, 2, NSEQ], I32)
        wt = sb("wt", [P, NSEQ, 2])
        te_i = sb("te_i", [P, NT], I32)
        r_w = sb("rt_w", [P, 2, 2, P], F32R)
        with ExitStack() as early:
            lg = sb("lg", [P, NSEQ, E], where=early)
            mx = sb("mx", [P, NSEQ, 8], where=early)
            ix = sb("ix", [P, NSEQ, 8], U32, where=early)
            ixf = sb("ixf", [P, NSEQ, 2], where=early)
            df = sb("df", [P, NSEQ, 2], where=early)
            oh = sb("oh", [P, 2, NSEQ, E], where=early)
            z = sb("z", [P, NSEQ, E], where=early)
            tot = sb("tot", [P, E, NSEQ], where=early)
            notfirst = sb("notfirst", [P, E, NSEQ], where=early)
            cum = sb("cum", [P, E, NSEQ], where=early)
            cnt = sb("cnt", [P, E], where=early)
            need = sb("need", [P, E], where=early)
            ends = sb("ends", [P, E], where=early)
            starts = sb("starts", [P, E], where=early)
            posf = sb("posf", [P, 2, NSEQ], where=early)
            tef = sb("tef", [P, NT], where=early)
            cmp = sb("cmp", [P, NT, E], where=early)
        dn_w = sb("dn_w", [P, 2, E, DM], F32R)
        with ExitStack() as early:
            m_w = sb("m_w", [P, 2, 2, GN], F32R, where=early)
            st = sb("st_e", [P, 2, 2, 2 * P], where=early)
            st_d = sb("st_ed", [P, 2, DM], where=early)
            st_b = sb("st_eb", [P, 2, 2, DM], where=early)
            lgT = sb("lgT", [E, GN], where=early)
            r_z = sb("rt_z", [P, 2, P], where=early)
            st_r = sb("st_r", [P, 2, E], where=early)
            zrow = sb("zrow", [P, DM], where=early)
            stats = sb("stats3", [P, NSEQ, 6], where=early)
            mv = sb("mv3", [P, NSEQ, 2], where=early)
            veps = sb("veps3", [P, NSEQ], where=early)
            rstd = sb("rstd3", [P, NSEQ], where=early)
            before = sb("before", [P, P], where=early)
            ones = sb("ones3", [P, P], where=early)
            iota_t = sb("iota_t", [P, NT], where=early)
        xs = sb("xs", [P, 2, 2, DM])
        xs_w = sb("xs_w", [P, 2, 2, 2, 2, P], F32R)
        gs = sb("gs3", [P, 2, 2, P])
        sg = sb("sg3", [P, 2, 2, P])
        us = sb("us3", [P, 2, 2, P])
        ac_w = sb("ac_w", [P, 2, 2, 2, P], F32R)
        y = sb("y3", [P, 2, 2, DM])

        names = """ld_r ld_e0 ld_e1 slots_zero consts r_hi r_lo stats_done mv_done veps_done rstd_done norm_done tr_done
        m_hi m_lo lgT_done lgT_out lgB_done lg_done max_done ix_done plan df_done wt_done counted
        tot_out pos_out te_out scattered w_hi w_lo b_hi b_r1 b_mid b_lo xs_in0 xs_in1 trx hix lox gu gsd usd sgd gld acd att hia loa
        dn yev y_out0 y_out1 added0 added1 out_done""".split()
        S = {n: sems.enter_context(nc.semaphore("e_" + n)) for n in names}
        gathered = [sems.enter_context(nc.semaphore(f"e_gathered{g}")) for g in range(NG)]
        primed = """lgB_done lgT_done""".split()
        block = ctx.enter_context(nc.Block())
        xs_v = slots.rearrange("(n a p) d -> n p a d", a=2, p=P)
        y_v = y_d.rearrange("(n a p) d -> n p a d", a=2, p=P)
        gu_d = wgu.rearrange("e (h p) c -> e p h c", p=P)
        BROWS = (0, 32, 64)

        def later(m):
            return not isinstance(m, int) or m >= 2

        def item(i, c):
            return 2 * i + c, i + c // 2, c % 2

        def steps(eng, step):
            for n in range(-1, 4):
                step(0, n, tr=True, mid=n >= 0, at=n >= 1, down=n >= 2)
            with eng.Fori(0, (NP - 6) // 2) as i:
                step(i, 4)
                step(i, 5)
            for n in range(NP - 2, NP + 2):
                step(0, n, tr=n < NP - 1, mid=n < NP, at=n < NP + 1)

        @block.sync
        def _(sp):
            for n in primed:
                sp.sem_inc(S[n], 1)
            sp.dma_start(st_r[:], wr.rearrange("(h p) e -> p h e", p=P)).then_inc(S["ld_r"], 16)
            sp.wait_ge(S["consts"], 2)
            sp.dma_start(slots.rearrange("(p a) d -> p a d", p=P), zrow[:].unsqueeze(1).to_broadcast([P, NT, DM])).then_inc(S["slots_zero"], 16)
            for e in range(E):
                b = e % 2
                if e >= 2:
                    sp.wait_ge(S["w_lo"], 2 * (e - 1))
                    sp.wait_ge(S["b_lo"], e - 1)
                ld = S["ld_e0"] if b == 0 else S["ld_e1"]
                sp.dma_start(st[:, b], gu_d[e]).then_inc(ld, 16)
                sp.dma_start(st_d[:, b], wd[e]).then_inc(ld, 16)
                for r in BROWS:
                    sp.dma_start(st_b[r:r + 1, b], bias[e:e + 1]).then_inc(ld, 16)

            def load(i, c):
                m, before_m, b = item(i, c)
                if later(m):
                    sp.wait_ge(S["trx"], m - 1)
                src = xs_v[m] if isinstance(m, int) else xs_v[bass.ds(m, 1)].rearrange("o p a d -> (o p) a d")
                sp.dma_start(xs[:, b], src).then_inc(S["xs_in0"] if b == 0 else S["xs_in1"], 16)

            def store(i, c):
                m, before_m, b = item(i, c)
                sp.wait_ge(S["yev"], m + 1)
                dst = y_v[m] if isinstance(m, int) else y_v[bass.ds(m, 1)].rearrange("o p a d -> (o p) a d")
                sp.dma_start(dst, y[:, b]).then_inc(S["y_out0"] if b == 0 else S["y_out1"], 16)

            LAG = 5
            sp.wait_ge(S["scattered"], 16 * 2 * NSEQ)
            sp.wait_ge(S["w_lo"], 2 * E)
            sp.wait_ge(S["b_lo"], E)
            for n in range(6):
                load(0, n)
                if n >= LAG:
                    store(0, n - LAG)
            with sp.Fori(0, (NP - 6) // 2) as i:
                for c in range(6, 8):
                    load(i, c)
                    store(i, c - LAG)
            for n in range(NP - LAG, NP):
                store(0, n)
            out_v = out.rearrange("b t d -> t b d")
            with sp.Fori(0, NG) as g:
                sp.wait_ge(S["added1"], (g + 1) * GT)
                sp.dma_start(out_v[:, bass.ds(g * GT, GT), :], x[:, bass.ds(g * GT, GT), :]).then_inc(S["out_done"], 16)
            sp.wait_ge(S["out_done"], 16 * NG)

        @block.gpsimd
        def _(pool):
            pool.memset(zrow[:], 0.0).then_inc(S["consts"], 1)
            pool.memset(st_b[:], 0.0).then_inc(S["consts"], 1)
            pool.memset(r_z[:], 0.0).then_inc(S["consts"], 1)
            pool.iota(iota_t[:], [[1, NT]], base=0, channel_multiplier=0, allow_small_or_imprecise_dtypes=True).then_inc(S["consts"], 1)
            pool.memset(ones[:], 1.0).then_inc(S["consts"], 1)
            pool.memset(notfirst[:], 1.0).then_inc(S["consts"], 1)
            pool.memset(sel[:], 0.0).then_inc(S["consts"], 1)
            pool.wait_ge(S["consts"], 7)
            pool.affine_select(out=before[:], in_=ones[:], compare_op=ALU.is_gt, fill=0.0, base=0, pattern=[[1, P]], channel_multiplier=-1)\
                .then_inc(S["consts"], 1)
            pool.memset(notfirst[:, :, 0:1], 0.0).then_inc(S["consts"], 1)
            pool.wait_ge(S["mv_done"], NSEQ)
            pool.tensor_scalar(veps[:], mv[:, :, 1], EPS, None, ALU.add).then_inc(S["veps_done"], 1)
            pool.wait_ge(S["veps_done"], 1)
            pool.tensor_tensor(rstd[:], veps[:], half[:].to_broadcast([P, NSEQ]), ALU.pow).then_inc(S["rstd_done"], 1)
            pool.wait_ge(S["pos_out"], 1)
            pool.wait_ge(S["norm_done"], NSEQ)
            pool.wait_ge(S["slots_zero"], 16)
            for t in range(NSEQ):
                for k in range(2):
                    pool.indirect_dma_start(slots, bass.IndirectOffsetOnAxis(ap=pos_i[:, k, t:t + 1], axis=0), m_all[:, t, :], None)\
                        .then_inc(S["scattered"], 16)

            def gate(i, c):
                m, _, b = item(i, c)
                pool.wait_ge(S["sgd"], m + 1)
                pool.wait_ge(S["gsd"], m + 1)
                pool.tensor_tensor(gs[:, b], gs[:, b], sg[:, b], ALU.mult).then_inc(S["gld"], 1)

            with pool.Fori(0, NP // 2) as i:
                gate(i, 0)
                gate(i, 1)
            pool.wait_ge(S["scattered"], 16 * 2 * NSEQ)
            pool.wait_ge(S["y_out0"], 16 * (NP // 2))
            pool.wait_ge(S["y_out1"], 16 * (NP // 2))
            for t in range(NSEQ):
                if t >= NSEQ // 2:
                    pool.wait_ge(S["added1"], t - NSEQ // 2 + 1)
                for k in range(2):
                    pool.indirect_dma_start(m_all[:, (2 * t + k) % NSEQ, :], None, y_d, bass.IndirectOffsetOnAxis(ap=pos_i[:, k, t:t + 1], axis=0))\
                        .then_inc(gathered[t // GT], 16)

        @block.scalar
        def _(act):
            act.wait_ge(S["r_lo"], 1)
            act.activation(r_w[:, HI], r_z[:], ACT.Copy).then_inc(S["r_hi"], 1)
            with act.Fori(0, NG) as g:
                act.wait_ge(S["lgT_done"], 1 + g)
                for h in range(2):
                    act.wait_ge(S["tr_done"], g * 2 + h + 1)
                    act.activation(m_w[:, HI, h, :], TRX[h][:], ACT.Copy).then_inc(S["m_hi"], 1)
                act.wait_ge(S["lgT_done"], 1 + g + 1)
                act.wait_ge(S["lgB_done"], 1 + g)
                act.activation(lgT[:], LGT[0:E, :], ACT.Copy).then_inc(S["lgT_out"], 1)
                act.wait_ge(S["lgB_done"], 1 + g + 1)
                act.activation(lg[:, bass.ds(g * GT, GT), :], LGB[:, 0:GT * E].rearrange("p (t e) -> p t e", t=GT), ACT.Copy).then_inc(S["lg_done"], 1)
            act.wait_ge(S["df_done"], 2)
            act.activation(wt[:], df[:], ACT.Sigmoid).then_inc(S["wt_done"], 1)
            act.wait_ge(S["counted"], 2)
            act.activation(tot[:], TOTAL[:].rearrange("p (t e) -> p e t", t=NSEQ), ACT.Copy).then_inc(S["tot_out"], 1)
            act.wait_ge(S["te_out"], 1)
            act.wait_ge(S["wt_done"], 1)
            for e in range(E):
                b = e % 2
                act.wait_ge(S["ld_e0"] if b == 0 else S["ld_e1"], 80 * (e // 2 + 1))
                act.activation(gu_w[:, HI, e], st[:, b], ACT.Copy).then_inc(S["w_hi"], 1)
                act.activation(dn_w[:, HI, e], st_d[:, b], ACT.Copy).then_inc(S["w_hi"], 1)
                act.activation(bias_w[:, e], st_b[:, b], ACT.Copy).then_inc(S["b_hi"], 1)
                act.wait_ge(S["b_r1"], e + 1)
                act.activation(bias_w[32:64, e], st_b[32:64, b], ACT.Copy).then_inc(S["b_mid"], 1)
                act.activation(bias_w[64:96, e], st_b[64:96, b], ACT.Copy).then_inc(S["b_mid"], 1)
            act.wait_ge(S["w_lo"], 2 * E)
            act.wait_ge(S["b_lo"], E)

            def step(i, n, tr=True, mid=True, at=True, down=True):
                if tr:
                    m, _, b = item(i, n + 1)
                    act.wait_ge(S["trx"], m + 1)
                    if later(m):
                        act.wait_ge(S["gu"], m - 1)
                    act.activation(xs_w[:, b, HI].rearrange("p a h s -> p (a h s)"), TRX[b][:], ACT.Copy).then_inc(S["hix"], 1)
                if mid:
                    m, _, b = item(i, n)
                    act.wait_ge(S["gsd"], m + 1)
                    if later(m):
                        act.wait_ge(S["gld"], m - 1)
                    act.activation(sg[:, b], gs[:, b], ACT.Sigmoid, scale=ALPHA).then_inc(S["sgd"], 1)
                if at:
                    m, _, b = item(i, n - 1)
                    act.wait_ge(S["att"], m + 1)
                    if later(m):
                        act.wait_ge(S["dn"], m - 1)
                    act.activation(ac_w[:, b, HI].rearrange("p a s -> p (a s)"), AT[b][:, 0:2 * P], ACT.Copy).then_inc(S["hia"], 1)
                if down:
                    m, before_m, b = item(i, n - 2)
                    act.wait_ge(S["dn"], m + 1)
                    if later(m):
                        act.wait_ge(S["y_out0"] if b == 0 else S["y_out1"], before_m * 16)
                    act.activation(y[:, b].rearrange("p a d -> p (a d)"), DN[b][:], ACT.Copy).then_inc(S["yev"], 1)

            steps(act, step)

        @block.vector
        def _(dve):
            with dve.Fori(0, NG) as g:
                for t in range(GT):
                    dve.bn_stats(stats[:, bass.ds(g * GT + t, 1), :], x[:, bass.ds(g * GT + t, 1), :]).then_inc(S["stats_done"], 1)
            dve.wait_ge(S["stats_done"], NSEQ)
            for t in range(NSEQ):
                dve.bn_aggr(mv[:, t, :], stats[:, t, :]).then_inc(S["mv_done"], 1)
            dve.wait_ge(S["consts"], 9)
            for r in BROWS:
                dve.memset(sel[r:r + 1, :], 1.0).then_inc(S["consts"], 1)
            dve.wait_ge(S["ld_r"], 16)
            dve.wait_ge(S["consts"], 3)
            dve.tensor_copy(r_z[:, :, 0:E], st_r[:]).then_inc(S["r_lo"], 1)
            dve.wait_ge(S["r_hi"], 1)
            dve.tensor_tensor(r_w[:, LO], r_z[:], r_w[:, HI].bitcast(F32), ALU.subtract).then_inc(S["r_lo"], 1)
            dve.wait_ge(S["rstd_done"], 1)

            def norm(t):
                dve.tensor_scalar(m_all[:, t, :], x[:, t, :], mv[:, t, 0:1], rstd[:, t:t + 1], ALU.subtract, ALU.mult).then_inc(S["norm_done"], 1)

            def top2(g):
                dve.wait_ge(S["lg_done"], g + 1)
                for t in range(g * GT, g * GT + GT):
                    dve.max(mx[:, t, :], lg[:, t, :]).then_inc(S["max_done"], 1)
                dve.wait_ge(S["max_done"], g * GT + GT)
                for t in range(g * GT, g * GT + GT):
                    dve.max_index(ix[:, t, :], mx[:, t, :], lg[:, t, :]).then_inc(S["ix_done"], 1)

            for t in range(GT):
                norm(t)
            for g in range(NG):
                if g + 1 < NG:
                    for t in range(GT):
                        norm((g + 1) * GT + t)
                for h in range(2):
                    dve.wait_ge(S["m_hi"], g * 2 + h + 1)
                    dve.tensor_tensor(m_w[:, LO, h, :], TRX[h][:], m_w[:, HI, h, :].bitcast(F32), ALU.subtract).then_inc(S["m_lo"], 1)
                if g >= 1:
                    top2(g - 1)
            top2(NG - 1)
            dve.tensor_tensor(df[:, :, 0], mx[:, :, 0], mx[:, :, 1], ALU.subtract).then_inc(S["df_done"], 1)
            dve.tensor_tensor(df[:, :, 1], mx[:, :, 1], mx[:, :, 0], ALU.subtract).then_inc(S["df_done"], 1)
            dve.wait_ge(S["ix_done"], NSEQ)
            dve.tensor_copy(ixf[:], ix[:, :, 0:2]).then_inc(S["plan"], 1)
            dve.wait_ge(S["plan"], 1)
            dve.wait_ge(S["consts"], 4)
            for k in range(2):
                dve.tensor_tensor(oh[:, k], iota_t[:, 0:E].unsqueeze(1).to_broadcast([P, NSEQ, E]), ixf[:, :, k:k + 1].to_broadcast([P, NSEQ, E]), ALU.is_equal)\
                    .then_inc(S["plan"], 1)
            dve.wait_ge(S["plan"], 3)
            dve.tensor_tensor(z[:], oh[:, 0], oh[:, 1], ALU.add).then_inc(S["plan"], 1)
            dve.wait_ge(S["tot_out"], 1)
            dve.wait_ge(S["consts"], 9)
            dve.tensor_tensor_scan(cum[:].rearrange("p e t -> p (e t)"), notfirst[:].rearrange("p e t -> p (e t)"), tot[:].rearrange("p e t -> p (e t)"),
                                   0.0, ALU.mult, ALU.add).then_inc(S["plan"], 1)
            dve.wait_ge(S["plan"], 5)
            dve.tensor_scalar(cnt[:], cum[:, :, NSEQ - 1], 1.0 / P, None, ALU.mult).then_inc(S["plan"], 1)
            dve.tensor_tensor(tot[:], cum[:], tot[:], ALU.subtract).then_inc(S["plan"], 1)
            dve.wait_ge(S["plan"], 7)
            below = cmp[:].rearrange("p n e -> p (n e)")[:, 0:E * TMAX].rearrange("p (e n) -> p e n", n=TMAX)
            dve.tensor_tensor(below, iota_t[:, 0:TMAX].unsqueeze(1).to_broadcast([P, E, TMAX]), cnt[:].unsqueeze(2).to_broadcast([P, E, TMAX]), ALU.is_lt)\
                .then_inc(S["plan"], 1)
            dve.wait_ge(S["plan"], 8)
            dve.tensor_reduce(need[:], below, AX.X, ALU.add).then_inc(S["plan"], 1)
            dve.wait_ge(S["plan"], 9)
            dve.tensor_tensor_scan(ends[:], ones[:, 0:E], need[:], 0.0, ALU.mult, ALU.add).then_inc(S["plan"], 1)
            dve.wait_ge(S["plan"], 10)
            dve.tensor_tensor(starts[:], ends[:], need[:], ALU.subtract).then_inc(S["plan"], 1)
            dve.wait_ge(S["plan"], 11)
            dve.scalar_tensor_tensor(cum[:], starts[:].unsqueeze(2).to_broadcast([P, E, NSEQ]), float(P), tot[:], ALU.mult, ALU.add).then_inc(S["plan"], 1)
            dve.wait_ge(S["plan"], 12)
            dve.tensor_tensor(z[:], WITHIN[:].rearrange("p (t e) -> p t e", e=E), cum[:].rearrange("p e t -> p t e"), ALU.add).then_inc(S["plan"], 1)
            dve.wait_ge(S["plan"], 13)
            for k in range(2):
                dve.tensor_tensor(oh[:, k], oh[:, k], z[:], ALU.mult).then_inc(S["plan"], 1)
            dve.wait_ge(S["plan"], 15)
            for k in range(2):
                dve.tensor_reduce(posf[:, k, :], oh[:, k], AX.X, ALU.add).then_inc(S["plan"], 1)
            dve.wait_ge(S["plan"], 17)
            dve.tensor_copy(pos_i[:], posf[:]).then_inc(S["pos_out"], 1)
            dve.tensor_tensor(cmp[:], ends[:].unsqueeze(1).to_broadcast([P, NT, E]), iota_t[:].unsqueeze(2).to_broadcast([P, NT, E]), ALU.is_le)\
                .then_inc(S["plan"], 1)
            dve.wait_ge(S["plan"], 18)
            dve.tensor_reduce(tef[:], cmp[:], AX.X, ALU.add).then_inc(S["plan"], 1)
            dve.wait_ge(S["plan"], 19)
            dve.tensor_scalar(te_i[:], tef[:], float(E - 1), None, ALU.min).then_inc(S["te_out"], 1)
            for e in range(E):
                b = e % 2
                dve.wait_ge(S["w_hi"], 2 * e + 2)
                dve.tensor_tensor(gu_w[:, LO, e], st[:, b], gu_w[:, HI, e].bitcast(F32), ALU.subtract).then_inc(S["w_lo"], 1)
                dve.tensor_tensor(dn_w[:, LO, e], st_d[:, b], dn_w[:, HI, e].bitcast(F32), ALU.subtract).then_inc(S["w_lo"], 1)
                dve.wait_ge(S["b_hi"], e + 1)
                dve.tensor_tensor(st_b[:, b], st_b[:, b], bias_w[:, e], ALU.subtract).then_inc(S["b_r1"], 1)
                dve.wait_ge(S["b_mid"], 2 * e + 2)
                dve.tensor_tensor(bias_w[64:96, e], st_b[64:96, b], bias_w[64:96, e], ALU.subtract).then_inc(S["b_lo"], 1)
            dve.wait_ge(S["w_lo"], 2 * E)
            dve.wait_ge(S["b_lo"], E)

            def step(i, n, tr=True, mid=True, at=True, down=True):
                if tr:
                    m, _, b = item(i, n + 1)
                    dve.wait_ge(S["hix"], m + 1)
                    dve.tensor_tensor(xs_w[:, b, LO].rearrange("p a h s -> p (a h s)"), TRX[b][:], xs_w[:, b, HI].bitcast(F32).rearrange("p a h s -> p (a h s)"),
                                      ALU.subtract).then_inc(S["lox"], 1)
                if mid:
                    m, _, b = item(i, n)
                    gu_p = GU[b][:].rearrange("p (a c) -> p a c", a=2)
                    dve.wait_ge(S["gu"], m + 1)
                    dve.tensor_scalar(gs[:, b], gu_p[:, :, 0:P], LIMIT, None, ALU.min).then_inc(S["gsd"], 1)
                    if later(m):
                        dve.wait_ge(S["att"], m - 1)
                    dve.tensor_scalar(us[:, b], gu_p[:, :, P:2 * P], LIMIT, -LIMIT, ALU.min, ALU.max).then_inc(S["usd"], 1)
                if at:
                    m, _, b = item(i, n - 1)
                    dve.wait_ge(S["hia"], m + 1)
                    dve.tensor_tensor(ac_w[:, b, LO].rearrange("p a s -> p (a s)"), AT[b][:, 0:2 * P], ac_w[:, b, HI].bitcast(F32).rearrange("p a s -> p (a s)"),
                                      ALU.subtract).then_inc(S["loa"], 1)
                if mid:
                    m, _, b = item(i, n)
                    dve.wait_ge(S["gld"], m + 1)
                    dve.wait_ge(S["usd"], m + 1)
                    dve.scalar_tensor_tensor(us[:, b], us[:, b], 1.0, gs[:, b], ALU.add, ALU.mult).then_inc(S["acd"], 1)

            steps(dve, step)
            for g in range(NG):
                dve.wait_ge(gathered[g], 16 * 2 * GT)
                for k in range(2):
                    if k == 1:
                        dve.wait_ge(S["added0"], g * GT + GT)
                    for t in range(g * GT, g * GT + GT):
                        dve.scalar_tensor_tensor(x[:, t, :], m_all[:, (2 * t + k) % NSEQ, :], wt[:, t, k:k + 1], x[:, t, :], ALU.mult, ALU.add)\
                            .then_inc(S[f"added{k}"], 1)

        @block.tensor
        def _(pe):
            hp = [(h, p) for h in range(2) for p in PASSES]
            pe.wait_ge(S["r_lo"], 2)
            def transposes(g):
                pe.wait_ge(S["norm_done"], g * GT + GT)
                if g >= 1:
                    pe.wait_ge(S["m_lo"], g * 2)
                for h in range(2):
                    for t in range(GT):
                        last = pe.transpose(TRX[h][:, t * P:(t + 1) * P], m_all[:, g * GT + t, h * P:(h + 1) * P], ident[:])
                    last.then_inc(S["tr_done"], 1)

            transposes(0)
            for g in range(NG):
                pe.wait_ge(S["m_lo"], g * 2 + 2)
                if g >= 1:
                    pe.wait_ge(S["lgT_out"], g)
                for i, (h, (a, b)) in enumerate(hp):
                    last = pe.matmul(LGT[:], r_w[:, a, h, :], m_w[:, b, h, :], start=(i == 0), stop=(i == 5))
                last.then_inc(S["lgT_done"], 1)
                if g + 1 < NG:
                    transposes(g + 1)
                pe.wait_ge(S["lgT_out"], g + 1)
                if g >= 1:
                    pe.wait_ge(S["lg_done"], g)
                for t in range(GT):
                    last = pe.transpose(LGB[:, t * E:(t + 1) * E], lgT[:, t * P:(t + 1) * P], ident[0:E, 0:E])
                last.then_inc(S["lgB_done"], 1)
            pe.wait_ge(S["plan"], 4)
            pe.wait_ge(S["consts"], 8)
            pe.matmul(TOTAL[:], ones[:], z[:].rearrange("p t e -> p (t e)"), start=True, stop=True).then_inc(S["counted"], 1)
            pe.matmul(WITHIN[:], before[:], z[:].rearrange("p t e -> p (t e)"), start=True, stop=True).then_inc(S["counted"], 1)
            pe.wait_ge(S["te_out"], 1)
            pe.wait_ge(S["w_lo"], 2 * E)
            pe.wait_ge(S["b_lo"], E)
            pe.wait_ge(S["consts"], 12)

            loaded = []

            def load_experts(tile, count):
                return list(nc.values_load_multi_w_load_instructions(te_i[0:1, bass.ds(tile, count)], engines=[mybir.EngineType.PE],
                                                                     min_val=0, max_val=E - 1)[1])

            def step(i, n, tr=True, mid=True, at=True, down=True):
                if isinstance(i, int):
                    first, last_m = (n - 2 if down else n), (n if mid else n - 2)
                    loaded.clear()
                    if last_m >= 0:
                        loaded.extend(load_experts(2 * first, 2 * (last_m - first + 1)))
                    e_down, e_mid = loaded[0:2], loaded[-2:]
                elif n % 2 == 0:
                    loaded[:] = load_experts(2 * item(i, n - 2)[0], 8)
                    e_down, e_mid = loaded[0:2], loaded[4:6]
                else:
                    e_down, e_mid = loaded[2:4], loaded[6:8]
                if tr:
                    m, before_m, b = item(i, n + 1)
                    pe.wait_ge(S["xs_in0"] if b == 0 else S["xs_in1"], 16 * before_m + 16)
                    if later(m):
                        pe.wait_ge(S["lox"], m - 1)
                    for a in range(2):
                        for h in range(2):
                            last = pe.transpose(TRX[b][:, (2 * a + h) * P:(2 * a + h + 1) * P], xs[:, b, a, h * P:(h + 1) * P], ident[:])
                    last.then_inc(S["trx"], 1)
                if mid:
                    m, _, b = item(i, n)
                    pe.wait_ge(S["lox"], m + 1)
                    if later(m):
                        pe.wait_ge(S["gsd"], m - 1)
                        pe.wait_ge(S["usd"], m - 1)
                    for a in range(2):
                        e = e_mid[a]
                        gu_a = GU[b][:, a * 2 * P:(a + 1) * 2 * P]
                        for j, (h, (p, q)) in enumerate(hp):
                            pe.matmul(gu_a, xs_w[:, b, p, a, h, :], gu_w[:, q, bass.ds(e, 1), h, :].rearrange("p o c -> p (o c)"), start=(j == 0), stop=False)
                        last = pe.matmul(gu_a, sel[0:96, :], bias_w[0:96, bass.ds(e, 1), 0, :].rearrange("p o c -> p (o c)"), start=False, stop=True)
                    last.then_inc(S["gu"], 1)
                if at:
                    m, _, b = item(i, n - 1)
                    pe.wait_ge(S["acd"], m + 1)
                    if later(m):
                        pe.wait_ge(S["loa"], m - 1)
                    for a in range(2):
                        last = pe.transpose(AT[b][:, a * P:(a + 1) * P], us[:, b, a, :], ident[:])
                    last.then_inc(S["att"], 1)
                if down:
                    m, _, b = item(i, n - 2)
                    pe.wait_ge(S["loa"], m + 1)
                    if later(m):
                        pe.wait_ge(S["yev"], m - 1)
                    for a in range(2):
                        e = e_down[a]
                        dn_a = DN[b][:, a * DM:(a + 1) * DM]
                        for j, (p, q) in enumerate(PASSES):
                            pe.matmul(dn_a, ac_w[:, b, p, a, :], dn_w[:, q, bass.ds(e, 1), :].rearrange("p o c -> p (o c)"), start=(j == 0), stop=False)
                        last = pe.matmul(dn_a, sel[0:96, :], bias_w[0:96, bass.ds(e, 1), 1, :].rearrange("p o c -> p (o c)"), start=False, stop=True)
                    last.then_inc(S["dn"], 1)

            steps(pe, step)


def program(nc, ids, emb, pos, A_diag, Bw, Cw, Dw, w1, w2, b2, cols, lnf, wqkv, wbm, wo, conv, norm_w, wr, wgu, bias, wd, out):
    NSEQ, DM = ids.shape[1], emb.shape[1]
    scr_g = nc.dram_tensor("scr_g", (P, 32, 32), F32, kind="Internal").ap()
    scr_b = nc.dram_tensor("scr_b", (32, P), F32, kind="Internal").ap()
    scr_t = nc.dram_tensor("scr_t", (P, 32, 64), F16, kind="Internal").ap()
    SLOTS = P * slot_tiles(NSEQ * P, wr.shape[1])
    slots = nc.dram_tensor("slots", (SLOTS, DM), F32, kind="Internal").ap()
    slot_out = nc.dram_tensor("slot_out", (SLOTS, DM), F32, kind="Internal").ap()
    with ExitStack() as ctx:
        x = ctx.enter_context(nc.sbuf_tensor("x", [P, NSEQ, DM], F32))
        ident = ctx.enter_context(nc.sbuf_tensor("ident", [P, P], F32))
        half = ctx.enter_context(nc.sbuf_tensor("half", [P, 1], F32))
        lnf_sb = ctx.enter_context(nc.sbuf_tensor("lnf_sb", [P, 2, DM], F32))
        def give_back(phase_sems):
            nc.all_engine_barrier()
            nc.clear_and_free_semaphores(phase_sems)
            nc.all_engine_barrier()

        phase_sems = []
        tower(nc, phase_sems, x, ident, half, lnf_sb, ids, emb, pos, A_diag, Bw, Cw, Dw, w1, w2, b2, cols, lnf)
        give_back(phase_sems)
        phase_sems = []
        attention(nc, phase_sems, x, ident, half, lnf_sb, wqkv, wbm, wo, conv, norm_w, scr_g, scr_b, scr_t)
        give_back(phase_sems)
        experts(nc, ctx, x, ident, half, slots, slot_out, wr, wgu, bias, wd, out)


def kernel(**inputs):
    import numpy as np
    import concourse.bacc as bacc
    from concourse.bass_utils import run_bass_kernel_spmd as run

    a = {k: np.asarray(v) for k, v in inputs.items()}
    tok, attn, ffn = "L0_tok_", "L0_attn_", "L0_ffn_"

    def columns(v):
        return v.reshape(v.shape[0], -1, P).transpose(0, 2, 1)

    gate_up, gate_up_bias = a[ffn + "gate_up_proj"], a[ffn + "gate_up_proj_bias"]
    arrays = {
        "ids": a["x"].T, "emb": a[tok + "emb"], "pos": a[tok + "pos_emb"], "A_diag": a[tok + "A_diag"].T,
        "Bw": a[tok + "B"], "Cw": a[tok + "C"], "Dw": a[tok + "D"], "w1": a[tok + "w1"], "w2": a[tok + "w2"], "b2": a[tok + "b2"],
        "cols": np.concatenate([columns(a[tok + n]) for n in ("ln1_s", "ln1_b", "ln2_s", "ln2_b", "b1")], axis=2),
        "lnf": np.stack([a[tok + "lnf_s"], a[tok + "lnf_b"]]),
        "wqkv": np.concatenate([a[attn + n].T for n in ("Wq", "Wk", "Wv")], axis=1),
        "wbm": np.concatenate([a[attn + "Wb"].T, a[attn + "Wmix"].T], axis=1),
        "wo": a[attn + "Wo"].T,
        "conv": np.concatenate([a[attn + n] for n in ("conv_q", "conv_k", "conv_v")]),
        "norm_w": np.concatenate([a[attn + "norm_w"]] * 2)[:, None],
        "wr": a[ffn + "router_weight"],
        "wgu": np.concatenate([gate_up[:, :, 0::2], gate_up[:, :, 1::2]], axis=2),
        "bias": np.stack([np.concatenate([gate_up_bias[:, 0::2], gate_up_bias[:, 1::2]], axis=1), a[ffn + "down_proj_bias"]], axis=1),
        "wd": a[ffn + "down_proj"],
    }
    arrays = {k: np.ascontiguousarray(v) for k, v in arrays.items()}
    nc = bacc.Bacc("TRN2", target_bir_lowering=False, num_devices=1)
    aps = {k: nc.dram_tensor(k, v.shape, mybir.dt.from_np(v.dtype), kind="ExternalInput").ap() for k, v in arrays.items()}
    shape = (a["x"].shape[0], a["x"].shape[1], a[tok + "emb"].shape[1])
    aps["out"] = nc.dram_tensor("out", shape, F32, kind="ExternalOutput").ap()
    program(nc, **aps)
    return run(nc, [arrays], core_ids=[0]).results[0]["out"]
```

```python
from contextlib import ExitStack

import concourse.bass as bass
from concourse import mybir

ALU = mybir.AluOpType
ACT = mybir.ActivationFunctionType
F32 = mybir.dt.float32
F32R = mybir.dt.float32r
F16 = mybir.dt.float16
BF16 = mybir.dt.bfloat16
I32 = mybir.dt.int32
U32 = mybir.dt.uint32
AX = mybir.AxisListType

P = 128
HI, LO = 0, 1
PASSES = ((HI, HI), (HI, LO), (LO, HI))
EPS = 1e-5
L2_EPS = 1e-6


def tower(nc, sems, x, ident, half, lnf_sb, ids, emb, pos, A_diag, Bw, Cw, Dw, w1, w2, b2, cols, lnf):
    V, DM = emb.shape
    NSEQ, T = ids.shape[1], P
    S, L = A_diag.shape
    FF = w1.shape[2]
    GT = 4
    NG = NSEQ // GT
    GN = GT * P
    NH2 = DM // P
    NF = FF // P
    NCOL = cols.shape[2]
    assert GN == 512 and NH2 == 2 and 2 * S == P and NG == 8 and NF == 8

    with ExitStack() as ctx:
        def sb(name, shape, dt=F32):
            return ctx.enter_context(nc.sbuf_tensor(name, shape, dt))

        def sem(name):
            sems.append(nc.alloc_semaphore(name=name))
            return sems[-1]

        def bank(name):
            return ctx.enter_context(nc.psum_tensor(name, [P, 512], F32))

        ids_sb = sb("ids_sb", [P, NSEQ], I32)
        idf = sb("idf", [P, NSEQ])
        idneg = sb("idneg", [P, NSEQ])
        idx = sb("idx", [P, NSEQ], I32)
        pos_sb = sb("pos_sb", [P, DM])
        a_col = sb("a_col", [P, L])
        a_sig = sb("a_sig", [P, L])
        runmask = sb("runmask", [P, GT, T])
        decay = sb("decay", [P, GT, T])
        st_d = sb("st_d", [P, NH2, DM])
        st_b = sb("st_b", [P, NH2, 2, S])
        st_c = sb("st_c", [P, DM])
        st_w1 = sb("st_w1", [P, NH2, FF])
        st_w2 = sb("st_w2", [P, NF, DM])
        d_w = sb("d_w", [P, 2, NH2, DM], F32R)
        b_w = sb("b_w", [P, 2, NH2, P], F32R)
        c_w = sb("c_w", [P, DM], F32R)
        c_t = sb("c_t", [P, DM], F32R)
        w1_w = sb("w1_w", [P, 2, NH2, FF], F32R)
        w2_w = sb("w2_w", [P, 2, NF, DM], F32R)
        b2_bc = sb("b2_bc", [P, L, DM])
        col = sb("col", [P, L * NCOL])
        stats = sb("stats", [P, GT, 6])
        mv = sb("mv", [P, GT, 2])
        veps = sb("veps", [P, GT])
        rstd = sb("rstd", [P, GT])
        hn = sb("hn", [P, GT, DM])
        full = sb("full", [P, NH2, GN])
        h1 = sb("h1", [P, 2, NH2, GN], F32R)
        h2 = [sb(f"h2_{i}", [P, 2, NH2, GN], F32R) for i in range(2)]
        hs = sb("hs", [P, GN])
        hs_w = sb("hs_w", [P, 2, GN], F32R)
        gfull = sb("gfull", [P, 2, GN])
        g_w = sb("g_w", [P, 2, 2, GN], F32R)

        TR = [bank(f"TR{i}") for i in range(2)]
        MID = [bank(f"MID{i}") for i in range(2)]
        ACC = [bank(f"ACC{i}") for i in range(2)]
        UY = [bank(f"UY{i}") for i in range(2)]

        ld_ids = sem("ld_ids")
        ld_const = sem("ld_const")
        ids_step = sem("ids_step")
        idx_ready = sem("idx_ready")
        gathered = [sem(f"gathered{g}") for g in range(NG)]
        ident_step = sem("ident_step")
        ident_ready = sem("ident_ready")
        run_step = sem("run_step")
        asig_ready = sem("asig_ready")
        decay_ready = sem("decay_ready")
        ld_ssm = sem("ld_ssm")
        ld_w1 = sem("ld_w1")
        ld_w2 = sem("ld_w2")
        ssmhi_done = sem("ssmhi_done")
        ssmlo_done = sem("ssmlo_done")
        w1hi_done = sem("w1hi_done")
        w1lo_done = sem("w1lo_done")
        w2hi_done = sem("w2hi_done")
        w2lo_done = sem("w2lo_done")
        bn_done = sem("bn_done")
        mv_done = sem("mv_done")
        veps_done = sem("veps_done")
        rstd_ready = sem("rstd_ready")
        norm_ready = sem("norm_ready")
        tr_done = sem("tr_done")
        evac_done = sem("evac_done")
        lo_done = sem("lo_done")
        u_done = sem("u_done")
        scan_done = sem("scan_done")
        hshi_done = sem("hshi_done")
        hslo_done = sem("hslo_done")
        y_done = sem("y_done")
        xupd_done = sem("xupd_done")
        b2_done = sem("b2_done")
        up_done = sem("up_done")
        gelu_done = sem("gelu_done")
        glo_done = sem("glo_done")
        down_done = sem("down_done")
        x_ready = sem("x_ready")

        w1_d = w1.rearrange("l (h p) f -> l p h f", p=P)
        w2_d = w2.rearrange("l (f p) d -> l p f d", p=P)
        d_d = Dw.rearrange("l (h p) e -> l p h e", p=P)
        b_d = Bw.rearrange("l (h p) s -> l p h s", p=P)

        def at(ap, l):
            return ap[bass.ds(l, 1)].rearrange("o p h f -> (o p) h f")

        def xg(g):
            return x[:, bass.ds(g * GT, GT), :]

        primed = (down_done, gelu_done, glo_done)
        block = ctx.enter_context(nc.Block())

        @block.sync
        def _(sp):
            for s in primed:
                sp.sem_inc(s, 1)
            sp.dma_start(ids_sb[:], ids).then_inc(ld_ids, 16)
            sp.dma_start(pos_sb[:], pos[0:P, :]).then_inc(ld_const, 16)
            for i in range(2):
                sp.dma_start(a_col[S * i:S * i + S, :], A_diag).then_inc(ld_const, 16)
                sp.dma_start(lnf_sb[:, i, :], lnf[i:i + 1, :].partition_broadcast(P)).then_inc(ld_const, 16)
            sp.dma_start(col[:].rearrange("p (l c) -> p l c", l=L), cols.rearrange("l p c -> p l c")).then_inc(ld_const, 16)
            for l in range(L):
                sp.dma_start(b2_bc[:, l, :], b2[l:l + 1, :].partition_broadcast(P)).then_inc(ld_const, 16)

            def load(l):
                if not isinstance(l, int):
                    sp.wait_ge(ssmlo_done, l * 3)
                sp.dma_start(st_d[:], at(d_d, l)).then_inc(ld_ssm, 16)
                for i in range(2):
                    sp.dma_start(st_b[:, :, i, :], at(b_d, l)).then_inc(ld_ssm, 16)
                    sp.dma_start(st_c[S * i:S * i + S, :], Cw[bass.ds(l, 1)].rearrange("o s d -> (o s) d")).then_inc(ld_ssm, 16)
                if not isinstance(l, int):
                    sp.wait_ge(w1lo_done, l * NF)
                sp.dma_start(st_w1[:], at(w1_d, l)).then_inc(ld_w1, 16)
                if not isinstance(l, int):
                    sp.wait_ge(w2lo_done, l * NF)
                sp.dma_start(st_w2[:], at(w2_d, l)).then_inc(ld_w2, 16)

            load(0)
            with sp.Fori(1, L) as l:
                load(l)

        @block.gpsimd
        def _(pool):
            def ln_rstd(n):
                pool.wait_ge(mv_done, n * GT + GT)
                pool.nop(nofuse=True)
                pool.wait_ge(norm_ready, n * GT)
                pool.nop(nofuse=True)
                pool.tensor_scalar(veps[:], mv[:, :, 1], EPS, None, ALU.add).then_inc(veps_done, 1)
                pool.wait_ge(veps_done, n + 2)
                pool.tensor_tensor(rstd[:], veps[:], half[:].to_broadcast([P, GT]), ALU.pow).then_inc(rstd_ready, 1)

            def pool_unit(l, g, last=False, head=False):
                k = l * NG + g
                if not last and not head:
                    ln_rstd(2 * k + 1)
                n2 = 2 * k + 2 - last
                ln_rstd(n2)
                pool.wait_ge(norm_ready, n2 * GT + GT)
                b2_l = b2_bc[:, l, :].unsqueeze(1) if isinstance(l, int) else b2_bc[:, bass.ds(l, 1), :]
                pool.tensor_tensor(xg(g), xg(g), b2_l.to_broadcast([P, GT, DM]), ALU.add).then_inc(b2_done, 1)

            pool.memset(half[:], -0.5).then_inc(veps_done, 1)
            pool.memset(ident[:], 0.0).then_inc(ident_step, 1)
            pool.memset(runmask[:], 1.0).then_inc(run_step, 1)
            pool.wait_ge(ident_step, 1)
            pool.affine_select(out=ident[:], in_=ident[:], compare_op=ALU.not_equal, fill=1.0, base=0,
                               pattern=[[-1, P]], channel_multiplier=1).then_inc(ident_ready, 1)
            pool.wait_ge(run_step, 1)
            pool.memset(runmask[:, :, 0:1], 0.0).then_inc(run_step, 1)
            pool.wait_ge(idx_ready, 1)

            def gather(groups):
                for s in range(GT * groups.start, GT * groups.stop):
                    pool.indirect_dma_start(x[:, s, :], None, emb, bass.IndirectOffsetOnAxis(ap=idx[:, s:s + 1], axis=0))\
                        .then_inc(gathered[s // GT], 16)

            gather(range(0, 2))
            ln_rstd(0)
            gather(range(2, 3))
            ln_rstd(1)
            gather(range(3, 5))
            pool.wait_ge(ld_const, 16 * (6 + L))
            pool_unit(0, 0, head=True)
            gather(range(5, NG))
            with pool.Fori(1, NG) as g:
                pool_unit(0, g)
            with pool.Fori(1, L - 1) as l:
                with pool.Fori(0, NG) as g:
                    pool_unit(l, g)
            with pool.Fori(0, NG - 1) as g:
                pool_unit(L - 1, g)
            pool_unit(L - 1, NG - 1, last=True)

        @block.scalar
        def _(act):
            def column(l, i):
                return col[:, bass.ds(l * NCOL + i, 1)]

            def evac(n, k, w, dst, l, halves=(0, 1)):
                for h in halves:
                    act.wait_ge(tr_done, n * 2 + h + 1)
                    act.nop(nofuse=True)
                    if w == 0:
                        act.wait_ge(y_done, k * 2)
                        act.nop(nofuse=True)
                    else:
                        act.wait_ge(up_done, k * NF)
                        act.nop(nofuse=True)
                    act.wait_ge(lo_done, n * 2)
                    act.nop(nofuse=True)
                    sc, bi = column(l, 4 * w + h), column(l, 4 * w + 2 + h)
                    act.activation(dst[:, HI, h, :], TR[h][:], ACT.Identity, scale=sc, bias=bi).then_inc(evac_done, 1)
                    act.activation(full[:, h, :], TR[h][:], ACT.Identity, scale=sc, bias=bi).then_inc(evac_done, 1)

            def ssm_act(k, s, par, l, last=False, turn=False):
                if s in (5, 6) and not last:
                    evac(2 * k + 1, k + 1, 0, h1, l + turn, (s - 5,))
                elif s == 1:
                    act.wait_ge(scan_done, k + 1)
                    act.wait_ge(y_done, k * 2)
                    act.activation(hs_w[:, HI, :], hs[:], ACT.Copy).then_inc(hshi_done, 1)
                elif s == 7:
                    evac(2 * k + 2 - last, k, 1, h2[par], l)
                elif s == 4 and turn:
                    ssm_weights(l + 1)

            def ssm_weights(l):
                act.wait_ge(ld_ssm, l * 80 + 80)
                if not (isinstance(l, int) and l == 0):
                    act.wait_ge(y_done, l * (2 * NG))
                act.activation(d_w[:, HI], st_d[:], ACT.Copy).then_inc(ssmhi_done, 1)
                act.activation(b_w[:, HI], st_b[:].rearrange("p h i s -> p h (i s)"), ACT.Copy).then_inc(ssmhi_done, 1)
                act.activation(c_w[0:S, :], st_c[0:S, :], ACT.Copy).then_inc(ssmhi_done, 1)
                act.activation(c_t[S:P, :], st_c[S:P, :], ACT.Copy).then_inc(ssmhi_done, 1)

            def w1_chunk(l, f):
                fs = slice(f * P, (f + 1) * P)
                act.wait_ge(ld_w1, l * 16 + 16)
                act.wait_ge(up_done, l * (NG * NF) + f + 1)
                act.activation(w1_w[:, HI, :, fs], st_w1[:, :, fs], ACT.Copy).then_inc(w1hi_done, 1)

            def w2_chunk(l, f):
                act.wait_ge(ld_w2, l * 16 + 16)
                if not (isinstance(l, int) and l == 0):
                    act.wait_ge(down_done, 1 + l * (NG * NF) - NF + f + 2)
                act.activation(w2_w[:, HI, f, :], st_w2[:, f, :], ACT.Copy).then_inc(w2hi_done, 1)

            def gelu(k, f, l):
                m = f % 2
                act.wait_ge(up_done, k * NF + f + 1 + NF)
                act.nop(nofuse=True)
                act.wait_ge(down_done, 1 + k * NF + f)
                act.nop(nofuse=True)
                act.wait_ge(glo_done, 1 + k * NF + f)
                act.nop(nofuse=True)
                act.activation(g_w[:, m, HI, :], MID[m][:], ACT.Gelu, bias=column(l, 8 + f)).then_inc(gelu_done, 1)
                act.activation(gfull[:, m, :], MID[m][:], ACT.Gelu, bias=column(l, 8 + f)).then_inc(gelu_done, 1)

            act.sem_inc(gelu_done, 2)
            act.wait_ge(ld_const, 16 * (6 + L))
            act.activation(a_sig[:], a_col[:], ACT.Sigmoid).then_inc(asig_ready, 1)
            act.wait_ge(asig_ready, 1)
            act.activation(a_col[:, 0:1], a_sig[:, 0:1], ACT.Gelu).then_inc(asig_ready, 1)
            ssm_weights(0)
            evac(0, 0, 0, h1, 0)
            for s in range(9):
                ssm_act(0, s, 0, 0)
                if s < NF:
                    w1_chunk(0, s)
                    w2_chunk(0, s)

            def unit(l, g, last=False, turn=False):
                k, par = (l * NG + g[0], g[1])
                for f in range(9):
                    if f < NF:
                        gelu(k - 1, f, l)
                    ssm_act(k, f, par, l, last, turn)

            def layer(l, last=False):
                with act.Fori(0, (NG - 2) // 2) as i:
                    unit(l, (i * 2 + 1, 1))
                    unit(l, (i * 2 + 2, 0))
                unit(l, (NG - 1, 1), last=last, turn=not last)

            with act.Fori(0, L - 1) as l:
                layer(l)
                k = l * NG + NG
                for f in range(9):
                    if f < NF:
                        gelu(k - 1, f, l)
                    ssm_act(k, f, 0, l + 1)
                    if f < NF:
                        w1_chunk(l + 1, f)
                    if f >= 2:
                        w2_chunk(l + 1, f - 2)
                w2_chunk(l + 1, NF - 1)
            layer(L - 1, last=True)
            for f in range(NF):
                gelu(L * NG - 1, f, L - 1)

        @block.vector
        def _(dve):
            def ln_stats(n, g, ready, count):
                dve.wait_ge(ready, count)
                dve.wait_ge(mv_done, n * GT)
                dve.nop(nofuse=True)
                for t in range(GT):
                    dve.bn_stats(stats[:, t, :], x[:, bass.ds(g * GT + t, 1), :]).then_inc(bn_done, 1)
                dve.wait_ge(bn_done, n * GT + GT)
                dve.nop(nofuse=True)
                dve.wait_ge(norm_ready, n * GT)
                dve.nop(nofuse=True)
                for t in range(GT):
                    dve.bn_aggr(mv[:, t, :], stats[:, t, :]).then_inc(mv_done, 1)

            def ln_norm(n, g):
                dve.wait_ge(rstd_ready, n + 1)
                dve.wait_ge(tr_done, n * 2)
                for t in range(GT):
                    dve.tensor_scalar(hn[:, t, :], x[:, bass.ds(g * GT + t, 1), :], mv[:, t, 0:1], rstd[:, t:t + 1],
                                      ALU.subtract, ALU.mult).then_inc(norm_ready, 1)

            def lows(n, dst, halves=(0, 1)):
                for h in halves:
                    dve.wait_ge(evac_done, n * 4 + 2 * h + 2)
                    dve.tensor_tensor(dst[:, LO, h, :], full[:, h, :], dst[:, HI, h, :].bitcast(F32), ALU.subtract)\
                        .then_inc(lo_done, 1)

            def ssm_dve(k, l, g, s, par, last=False, turn=False):
                n1, n2 = 2 * k + 1, 2 * k + 2 - last
                g_next = 0 if turn else g + 1
                if s == 1:
                    dve.wait_ge(u_done, k + 1)
                    dve.wait_ge(hshi_done, k)
                    dve.wait_ge(hslo_done, k)
                    dve.tensor_tensor_scan(hs[:], decay[:].rearrange("p g t -> p (g t)"), UY[0][:], 0.0, ALU.mult, ALU.add)\
                        .then_inc(scan_done, 1)
                    dve.wait_ge(hshi_done, k + 1)
                    dve.tensor_tensor(hs_w[:, LO, :], hs[:], hs_w[:, HI, :].bitcast(F32), ALU.subtract).then_inc(hslo_done, 1)
                if s == 2 and not last:
                    ln_stats(n1, g_next, x_ready, 2 * k + 4)
                if s == 3:
                    x_update(k, g, 0)
                    if not last:
                        ln_norm(n1, g_next)
                if s == 4:
                    x_update(k, g, 1)
                    ln_stats(n2, g, xupd_done, 2 * k + 2)
                if s == 5:
                    if not last:
                        lows(n1, h1, (0,))
                    ln_norm(n2, g)
                if s == 6 and not last:
                    lows(n1, h1, (1,))
                if s == 6 and turn:
                    ssm_weights(l + 1)
                if s == 7:
                    lows(n2, h2[par])

            def ssm_weights(l):
                if not (isinstance(l, int) and l == 0):
                    dve.wait_ge(scan_done, l * NG)
                a_l = a_sig[:, l:l + 1] if isinstance(l, int) else a_sig[:, bass.ds(l, 1)]
                dve.tensor_scalar(decay[:], runmask[:], a_l, None, ALU.mult).then_inc(decay_ready, 1)
                dve.wait_ge(ssmhi_done, l * 4 + 4)
                dve.tensor_tensor(d_w[:, LO], st_d[:], d_w[:, HI].bitcast(F32), ALU.subtract).then_inc(ssmlo_done, 1)
                dve.tensor_tensor(b_w[:, LO], st_b[:].rearrange("p h i s -> p h (i s)"), b_w[:, HI].bitcast(F32), ALU.subtract).then_inc(ssmlo_done, 1)
                dve.tensor_tensor(c_w[S:P, :], st_c[S:P, :], c_t[S:P, :].bitcast(F32), ALU.subtract).then_inc(ssmlo_done, 1)
                dve.wait_ge(decay_ready, l + 1)

            def w1_chunk(l, f):
                fs = slice(f * P, (f + 1) * P)
                dve.wait_ge(w1hi_done, l * NF + f + 1)
                dve.tensor_tensor(w1_w[:, LO, :, fs], st_w1[:, :, fs], w1_w[:, HI, :, fs].bitcast(F32), ALU.subtract).then_inc(w1lo_done, 1)

            def w2_chunk(l, f):
                dve.wait_ge(w2hi_done, l * NF + f + 1)
                dve.tensor_tensor(w2_w[:, LO, f, :], st_w2[:, f, :], w2_w[:, HI, f, :].bitcast(F32), ALU.subtract).then_inc(w2lo_done, 1)

            def x_update(k, g, j):
                dve.wait_ge(y_done, k * 2 + j + 1)
                xx = x[:, bass.ds(g * GT + 2 * j, 2), :]
                dve.tensor_tensor(xx, xx, UY[j][:].rearrange("p (a d) -> p a d", a=2), ALU.add).then_inc(xupd_done, 1)

            def glo(k, f):
                m = f % 2
                dve.wait_ge(gelu_done, 1 + 2 * (k * NF + f) + 4)
                dve.tensor_tensor(g_w[:, m, LO, :], gfull[:, m, :], g_w[:, m, HI, :].bitcast(F32), ALU.subtract)\
                    .then_inc(glo_done, 1)

            def mlp_add(k, g):
                dve.wait_ge(down_done, 1 + k * NF + NF + 1)
                dve.wait_ge(b2_done, k + 1)
                for j in range(2):
                    xx = x[:, bass.ds(g * GT + 2 * j, 2), :]
                    dve.tensor_tensor(xx, xx, ACC[j][:].rearrange("p (a d) -> p a d", a=2), ALU.add).then_inc(x_ready, 1)

            dve.sem_inc(glo_done, 1)
            dve.wait_ge(ld_ids, 16)
            dve.tensor_copy(idf[:], ids_sb[:]).then_inc(ids_step, 1)
            dve.wait_ge(ids_step, 1)
            dve.tensor_scalar(idneg[:], idf[:], 0.0, float(V), ALU.is_lt, ALU.mult).then_inc(ids_step, 1)
            dve.wait_ge(ids_step, 2)
            dve.tensor_tensor(idneg[:], idneg[:], idf[:], ALU.add).then_inc(ids_step, 1)
            dve.wait_ge(ids_step, 3)
            dve.tensor_scalar(idx[:], idneg[:], 0.0, float(V - 1), ALU.max, ALU.min).then_inc(idx_ready, 1)
            dve.wait_ge(ld_const, 16 * (6 + L))

            def embed(g):
                dve.wait_ge(gathered[g], 16 * GT)
                for j in range(2):
                    xx = x[:, g * GT + 2 * j:g * GT + 2 * j + 2, :]
                    dve.tensor_tensor(xx, xx, pos_sb[:].unsqueeze(1).to_broadcast([P, 2, DM]), ALU.add).then_inc(x_ready, 1)

            embed(0)
            ln_stats(0, 0, x_ready, 2)
            ln_norm(0, 0)
            dve.wait_ge(asig_ready, 2)
            dve.wait_ge(run_step, 2)
            ssm_weights(0)
            lows(0, h1)
            for s in range(9):
                if s == 0:
                    embed(1)
                ssm_dve(0, 0, 0, s, 0)
                for g in {2: (2,), 3: (3,), 4: (4,), 6: (5,), 7: (6,), 8: (7,)}.get(s, ()):
                    embed(g)
                if s < NF:
                    w1_chunk(0, s)
                    w2_chunk(0, s)

            def unit(l, g, last=False, turn=False):
                g, par = g
                k = l * NG + g
                for f in range(9):
                    if f < NF:
                        glo(k - 1, f)
                    ssm_dve(k, l, g, f, par, last, turn)
                mlp_add(k - 1, g - 1)

            def layer(l, last=False):
                with dve.Fori(0, (NG - 2) // 2) as i:
                    unit(l, (i * 2 + 1, 1))
                    unit(l, (i * 2 + 2, 0))
                unit(l, (NG - 1, 1), last=last, turn=not last)

            with dve.Fori(0, L - 1) as l:
                layer(l)
                k = l * NG + NG
                for f in range(9):
                    if f < NF:
                        glo(k - 1, f)
                    ssm_dve(k, l + 1, 0, f, 0)
                    if f < NF:
                        w1_chunk(l + 1, f)
                    if f >= 2:
                        w2_chunk(l + 1, f - 2)
                w2_chunk(l + 1, NF - 1)
                mlp_add(k - 1, NG - 1)
            layer(L - 1, last=True)
            for f in range(NF):
                glo(L * NG - 1, f)
            mlp_add(L * NG - 1, NG - 1)

        @block.tensor
        def _(pe):
            def transposes(n):
                pe.wait_ge(norm_ready, n * GT + GT)
                pe.wait_ge(evac_done, n * 4)
                for h in range(2):
                    for t in range(GT):
                        last = pe.transpose(TR[h][:, t * P:(t + 1) * P], hn[:, t, h * P:(h + 1) * P], ident[:])
                    last.then_inc(tr_done, 1)

            def ssm_pe(k, s, l, first=False):
                if s == 0:
                    pe.wait_ge(ssmlo_done, l * 3 + 3)
                    n1 = 2 * k - 1 + first
                    pe.wait_ge(lo_done, n1 * 2 + 2)
                    pe.wait_ge(xupd_done, k * 2)
                    for i, (h, (a, b)) in enumerate([(h, p) for h in range(2) for p in PASSES]):
                        last = pe.matmul(UY[0][:], b_w[:, a, h, :], h1[:, b, h, :], start=(i == 0), stop=(i == 5))
                    last.then_inc(u_done, 1)
                if s in (2, 3):
                    j = s - 2
                    pe.wait_ge(hslo_done, k + 1)
                    for t in range(2 * j, 2 * j + 2):
                        o = UY[j][:, (t % 2) * DM:(t % 2 + 1) * DM]
                        tok = slice(t * P, (t + 1) * P)
                        pe.matmul(o, hs_w[:, HI, tok], c_w[:], start=True, stop=False)
                        pe.matmul(o, hs_w[:, LO, tok], c_w[:], start=False, stop=False)
                        for i, (h, (a, b)) in enumerate([(h, p) for h in range(2) for p in PASSES]):
                            last_mm = pe.matmul(o, h1[:, a, h, tok], d_w[:, b, h, :], start=False, stop=(i == 5))
                    last_mm.then_inc(y_done, 1)

            def transposes_pe(k, s, last=False):
                if s == 5 and not last:
                    transposes(2 * k + 1)
                if s == 7:
                    transposes(2 * k + 2 - last)

            def up(k, f, par, l, last=False):
                m = f % 2
                pe.wait_ge(w1lo_done, l * NF + f + 1)
                if f == 0:
                    n2 = 2 * k + 2 - last
                    pe.wait_ge(lo_done, n2 * 2 + 2)
                pe.wait_ge(gelu_done, 1 + 2 * (k * NF + f))
                fs = slice(f * P, (f + 1) * P)
                for i, (h, (a, b)) in enumerate([(h, p) for h in range(2) for p in PASSES]):
                    last = pe.matmul(MID[m][:], w1_w[:, a, h, fs], h2[par][:, b, h, :], start=(i == 0), stop=(i == 5))
                last.then_inc(up_done, 1)

            def down(k, f, l):
                m = f % 2
                pe.wait_ge(w2lo_done, l * NF + f + 1)
                if f == 0:
                    pe.wait_ge(x_ready, 2 * k + 2 * NG)
                pe.wait_ge(glo_done, 1 + k * NF + f + 2)
                for t in range(GT):
                    o = ACC[t // 2][:, (t % 2) * DM:(t % 2 + 1) * DM]
                    tok = slice(t * P, (t + 1) * P)
                    for i, (a, b) in enumerate(PASSES):
                        last = pe.matmul(o, g_w[:, m, a, tok], w2_w[:, b, f, :], start=(f == 0 and i == 0 and t % 2 == 0),
                                         stop=(f == NF - 1 and i == 2), skip_group_check=True)
                last.then_inc(down_done, 1)

            pe.sem_inc(up_done, NF)
            pe.sem_inc(down_done, 1)
            pe.wait_ge(ident_ready, 1)
            transposes(0)
            for s in range(9):
                transposes_pe(0, s)
                ssm_pe(0, s, 0, first=True)

            def unit(l, g, last=False):
                g, par = g
                k = l * NG + g
                for f in range(9):
                    if f < NF:
                        up(k - 1, f, 1 - par, l)
                    transposes_pe(k, f, last=last)
                    if f >= 1:
                        down(k - 1, f - 1, l)
                    ssm_pe(k, f, l)

            def layer(l, last=False):
                with pe.Fori(0, (NG - 2) // 2) as i:
                    unit(l, (i * 2 + 1, 1))
                    unit(l, (i * 2 + 2, 0))
                unit(l, (NG - 1, 1), last=last)

            with pe.Fori(0, L - 1) as l:
                layer(l)
                k = l * NG + NG
                for f in range(9):
                    if f < NF:
                        up(k - 1, f, 1, l)
                    transposes_pe(k, f)
                    if f >= 1:
                        down(k - 1, f - 1, l)
                    ssm_pe(k, f, l + 1)
            layer(L - 1, last=True)
            for f in range(9):
                if f < NF:
                    up(L * NG - 1, f, 1, L - 1, last=True)
                if f >= 1:
                    down(L * NG - 1, f - 1, L - 1)


def attention(nc, sems, x, ident, half, lnf_sb, wqkv, wbm, wo, conv, norm_w, scr_g, scr_b, scr_t):
    NSEQ, DM = x.shape[1], x.shape[2]
    GT = 4
    NG = NSEQ // GT
    GN = GT * P
    NH2 = DM // P
    HD = 64
    NHD = DM // HD
    NQ = GT * NHD
    C = 32
    NC = P // C
    NCH = 3 * NH2
    NB = NG // 2

    with ExitStack() as ctx:
        def sb(name, shape, dt=F32):
            return ctx.enter_context(nc.sbuf_tensor(name, shape, dt))

        def sem(name):
            sems.append(nc.alloc_semaphore(name=name))
            return sems[-1]

        bk = [ctx.enter_context(nc.psum_tensor(f"bk{i}", [P, 512], F32)) for i in range(8)]
        TR, QKV, TOK, VT, BACK = bk[0:2], bk[2:4], bk[4:6], bk[6], bk[7]
        OT = (VT, BACK)
        TOK4 = (TOK[0], TOK[1], QKV[0], QKV[1])
        CONV = (QKV[0], QKV[1], BACK)

        st_bm = sb("st_bm", [P, NH2, 2 * NHD])
        qkv_w = sb("qkv_w", [P, 2, NH2, 3 * DM], F32R)
        bm_w = sb("bm_w", [P, 2, NH2, P], F32R)
        bm_z = sb("bm_z", [P, 2, NH2, P])
        wo_w = sb("wo_w", [P, 2, NH2, DM], F32R)
        cw = sb("cw", [P, NCH, 4])
        nw = sb("nw", [P, 1])
        causal = sb("causal", [P, 2, P])
        strict = sb("strict", [P, C, C])
        tcm_f = sb("tcm", [P, (C + 1) * C])
        tcm = tcm_f[:, 0:C * C].rearrange("p (i j) -> p i j", j=C)

        stats = sb("stats2", [P, GT, 6])
        mv = sb("mv2", [P, GT, 2])
        veps = sb("veps2", [P, GT])
        rstd = sb("rstd2", [P, GT])
        hn = sb("hn2", [P, GT, DM])
        a_w = sb("a_w", [P, 2, NH2, GN], F32R)
        bmT = sb("bmT", [2 * NHD, GN])
        bm = sb("bm", [P, 2 * GT, 2 * NHD])
        cv = sb("cv", [P, 3, GN])
        sg = sb("sg", [P, 3, GN])
        qkv_t = sb("qkv_t", [P, NCH, GN])
        sq = sb("sq", [P, 2, GN])
        ss = sb("ss", [P, GT, 2 * NHD])
        sse = sb("sse", [P, GT, 2 * NHD])
        rs = sb("rs", [P, GT, 2 * NHD])
        qkn = sb("qkn", [P, 2, GN])
        qk_w = sb("qk_w", [P, 2, GT, 4, P], F16)
        v = sb("v", [P, 2 * GT, DM])
        graw = sb("graw", [P, NQ, P])
        st_qkv = graw[:].rearrange("p q t -> p (q t)")[:, 0:NH2 * 3 * DM].rearrange("p (h c) -> p h c", h=NH2)
        g_w = sb("g_w2", [P, 2, 2, NQ, P], F16)
        kq = sb("kq", [P, 2, 2, P])
        kq_w = sb("kq_w", [P, 2, 2, NQ, P], F16)
        gcm = sb("gcm", [P, C, C])
        bcm = sb("bcm", [P, C])
        acm_f = sb("acm", [P, (C + 1) * C])
        acm = acm_f[:, 0:C * C].rearrange("p (i j) -> p i j", j=C)
        prod = graw[:].rearrange("p q t -> p (q t)")
        xm = sb("xm", [P, 16, 16])
        scm = sb("scm", [P, C, C])
        t_w = sb("t_w", [P, C, 2, C], F16)
        tt = sb("tt", [P, 2 * NQ, 2, C], F16)
        r = sb("r", [P, NQ, HD])
        st_wo = r[:].rearrange("p q d -> p (q d)")[:, 0:NH2 * DM].rearrange("p (h c) -> p h c", h=NH2)
        r_w = sb("r_w", [P, 2, NQ, HD], F16)
        u_w = sb("u_w", [P, 2, NQ, HD], F16)
        om = graw[:, 0:NQ // 2, :].rearrange("p q n -> p (q n)").rearrange("p (t d) -> p t d", t=GT)
        vm = graw[:, NQ // 2:NQ, :].rearrange("p q n -> p (q n)").rearrange("p (t d) -> p t d", t=GT)
        omix = sb("omix", [P, GT, NHD])
        full = sb("full2", [P, NH2, GN])

        names = """ld_w whi wlo masks bmz m_bn m_mv m_veps m_rstd m_norm fin1 fin2 tr_done a_hi a_lo
        bmT_done bm_sig bm_tr bm_done beta_out qkv_done tap0 conv_done sig_done silu_done tok_done v_tr v_done
        sq_done ss_done sse_done rs_done qkn_done back_done qk_hi qk_lo gk_done graw_done kq_done kq_hi kq_lo
        g_hi g_lo g_out gcm_in ps_r a_step t_hi t_lo t_out tt_in ps1 r_done r_hi r_lo ps2 u_hi u_lo o_done
        om1 vm1 omix1 osq oss osse ors o3 otr o_hi o_full o_lo wo_done x_out""".split()
        S = {n: sem("a_" + n) for n in names}

        xg = lambda g: x[:, bass.ds(g * GT, GT), :]
        primed = """a_step g_out gcm_in gk_done kq_lo o_done o_lo om1 ors otr ps2 ps_r qk_lo qkn_done rs_done t_hi u_lo
        vm1 wo_done x_out""".split()
        block = ctx.enter_context(nc.Block())

        @block.sync
        def _(sp):
            for n in primed:
                sp.sem_inc(S[n], 1)
            sp.dma_start(st_qkv, wqkv.rearrange("(h p) c -> p h c", p=P)).then_inc(S["ld_w"], 16)
            sp.dma_start(st_bm[:], wbm.rearrange("(h p) c -> p h c", p=P)).then_inc(S["ld_w"], 16)
            sp.dma_start(st_wo, wo.rearrange("(h p) c -> p h c", p=P)).then_inc(S["ld_w"], 16)
            sp.dma_start(cw[:], conv.rearrange("(c p) k -> p c k", p=P)).then_inc(S["ld_w"], 16)
            sp.dma_start(nw[:], norm_w).then_inc(S["ld_w"], 16)
            scr_b_v = scr_b.rearrange("(b s h) t -> h b s t", b=2, h=NHD)
            with sp.Fori(0, NB) as b:
                for gi in range(2):
                    m = b * 2 + gi
                    sp.wait_ge(S["bm_sig"], m + 1)
                    sp.wait_ge(S["gcm_in"], 1 + b * 32)
                    sp.dma_start(scr_b_v[:, gi], bmT[0:NHD, :].rearrange("h (s t) -> h s t", s=GT)).then_inc(S["beta_out"], 16)
                    sp.wait_ge(S["graw_done"], m * 8 + 8)
                    for n in range(NC):
                        src = graw[C * n:C * n + C, :, C * n:C * n + C]
                        dst = scr_g.rearrange("(g q n) i j -> g n i q j", g=2, n=NC)[gi, n]
                        sp.dma_start(dst, src).then_inc(S["g_out"], 16)
                sp.wait_ge(S["g_out"], 1 + b * 128 + 128)
                sp.nop(nofuse=True)
                sp.wait_ge(S["beta_out"], b * 32 + 32)
                sp.wait_ge(S["a_step"], 1 + b * 3)
                sp.dma_start(gcm[:], scr_g).then_inc(S["gcm_in"], 16)
                sp.dma_start(bcm[:], scr_b.rearrange("q (n i) -> (q n) i", n=NC)).then_inc(S["gcm_in"], 16)
                sp.wait_ge(S["t_lo"], b + 1)
                sp.dma_start(scr_t, t_w[:].rearrange("p j s i -> p j (s i)")).then_inc(S["t_out"], 16)
                sp.wait_ge(S["t_out"], b * 16 + 16)
                sp.nop(nofuse=True)
                sp.wait_ge(S["u_lo"], 1 + b * 16)
                for n in range(NC):
                    sp.dma_start(tt[C * n:C * n + C].rearrange("j q s i -> j q (s i)"),
                                 scr_t.rearrange("(q n) j x -> n j q x", n=NC)[n]).then_inc(S["tt_in"], 16)

        @block.gpsimd
        def _(pool):
            def rstd_of(n):
                pool.wait_ge(S["m_mv"], n * GT + GT)
                pool.nop(nofuse=True)
                pool.wait_ge(S["m_norm"], n * GT)
                pool.nop(nofuse=True)
                pool.tensor_scalar(veps[:], mv[:, :, 1], EPS, None, ALU.add).then_inc(S["m_veps"], 1)
                pool.wait_ge(S["m_veps"], n + 1)
                pool.tensor_tensor(rstd[:], veps[:], half[:].to_broadcast([P, GT]), ALU.pow).then_inc(S["m_rstd"], 1)

            pool.memset(bm_z[:], 0.0).then_inc(S["bmz"], 1)
            rstd_of(0)
            rstd_of(1)
            pool.memset(causal[:], 1.0).then_inc(S["masks"], 1)
            pool.memset(strict[:], -1.0).then_inc(S["masks"], 1)
            pool.memset(tcm, 0.0).then_inc(S["masks"], 1)
            pool.wait_ge(S["masks"], 3)
            pool.affine_select(out=causal[:], in_=causal[:], compare_op=ALU.is_ge, fill=0.0, base=0,
                               pattern=[[0, 2], [1, P]], channel_multiplier=-1).then_inc(S["masks"], 1)
            pool.affine_select(out=strict[:], in_=strict[:], compare_op=ALU.is_gt, fill=0.0, base=0,
                               pattern=[[1, C], [-1, C]], channel_multiplier=0).then_inc(S["masks"], 1)
            pool.affine_select(out=tcm, in_=tcm, compare_op=ALU.not_equal, fill=1.0, base=0,
                               pattern=[[1, C], [-1, C]], channel_multiplier=0).then_inc(S["masks"], 1)
            def front(m):
                for c in range(NCH):
                    pool.wait_ge(S["sig_done"], m * NCH + c + 1)
                    pool.wait_ge(S["tok_done"], m * 4)
                    pool.wait_ge(S["v_tr"], m * 2)
                    pool.tensor_tensor(qkv_t[:, c, :], cv[:, c % 3, :], sg[:, c % 3, :], ALU.mult).then_inc(S["silu_done"], 1)

            def batch(b, final=False):
                pool.wait_ge(S["x_out"], 1 + b * 4)
                for gi in range(2):
                    m = b * 2 + gi
                    ahead = not (final and gi == 1)
                    if gi == 1:
                        front(m)
                    for t in range(GT):
                        pool.wait_ge(S["ss_done"], m * GT + t + 1)
                        pool.nop(nofuse=True)
                        pool.wait_ge(S["rs_done"], 1 + m * GT + t)
                        pool.nop(nofuse=True)
                        pool.tensor_scalar(sse[:, t, :], ss[:, t, :], L2_EPS, None, ALU.add).then_inc(S["sse_done"], 1)
                        pool.wait_ge(S["sse_done"], m * GT + t + 1)
                        pool.wait_ge(S["qkn_done"], 1 + m * GT)
                        pool.tensor_tensor(rs[:, t, :], sse[:, t, :], half[:].to_broadcast([P, 2 * NHD]), ALU.pow).then_inc(S["rs_done"], 1)
                    for j in range(8):
                        q2 = slice(4 * (j // 2) + j % 2, 4 * (j // 2) + 4, 2)
                        pool.wait_ge(S["kq_hi"], m * 8 + j + 1)
                        pool.tensor_tensor(kq_w[:, gi, LO, q2, :], kq[:, j % 2], kq_w[:, gi, HI, q2, :], ALU.subtract).then_inc(S["kq_lo"], 1)
                        pool.wait_ge(S["g_hi"], m * 8 + j + 1)
                        pool.tensor_tensor(g_w[:, gi, LO, q2, :], graw[:, q2, :], g_w[:, gi, HI, q2, :], ALU.subtract).then_inc(S["g_lo"], 1)
                        if ahead and j == 1:
                            rstd_of(2 * m + 2)
                    if ahead:
                        rstd_of(2 * m + 3)
                if not final:
                    front(b * 2 + 2)
                for gi in range(2):
                    m = b * 2 + gi
                    pool.wait_ge(S["omix1"], m + 1)
                    pool.wait_ge(S["otr"], 1 + m * 2)
                    pool.tensor_tensor(vm.rearrange("p t (h d) -> p t h d", h=NHD), v[:, gi * GT:gi * GT + GT, :].rearrange("p t (h d) -> p t h d", h=NHD),
                                       omix[:].unsqueeze(3).to_broadcast([P, GT, NHD, HD]), ALU.mult).then_inc(S["vm1"], 1)
                    pool.wait_ge(S["oss"], m + 1)
                    pool.nop(nofuse=True)
                    pool.tensor_scalar(sse[:, :, 0:NHD], ss[:, :, 0:NHD], 1.0 / HD, EPS, ALU.mult, ALU.add).then_inc(S["osse"], 1)
                    pool.wait_ge(S["osse"], m + 1)
                    pool.tensor_tensor(rs[:, :, 0:NHD], sse[:, :, 0:NHD], half[:].unsqueeze(2).to_broadcast([P, GT, NHD]), ALU.pow).then_inc(S["ors"], 1)

            front(0)
            with pool.Fori(0, NB - 1) as b:
                batch(b)
            batch(NB - 1, final=True)

        @block.scalar
        def _(act):
            def hi_qk(m, t):
                act.wait_ge(S["back_done"], m * GT + t + 1)
                act.wait_ge(S["gk_done"], 1 + m * 8)
                act.activation(qk_w[:, HI, t], BACK[:].rearrange("p (c t) -> p c t", c=4), ACT.Copy).then_inc(S["qk_hi"], 1)

            act.wait_ge(S["ld_w"], 80)
            act.activation(qkv_w[:, HI], st_qkv, ACT.Copy).then_inc(S["whi"], 1)
            act.wait_ge(S["bmz"], 2)
            act.activation(bm_w[:, HI], bm_z[:, 0], ACT.Copy).then_inc(S["whi"], 1)
            act.activation(wo_w[:, HI], st_wo, ACT.Copy).then_inc(S["whi"], 1)
            act.wait_ge(S["wlo"], 3)
            act.activation(sg[:, 0, 0:4], cw[:, 0, :], ACT.Sigmoid).then_inc(S["whi"], 1)
            act.wait_ge(S["whi"], 4)
            def front(m, beside=None):
                for h in range(2):
                    act.wait_ge(S["tr_done"], m * 2 + h + 1)
                    act.wait_ge(S["qkv_done"], m * NCH)
                    act.activation(a_w[:, HI, h, :], TR[h][:], ACT.Copy).then_inc(S["a_hi"], 1)
                for c in range(NCH + 1):
                    n = m * NCH + c
                    if c < NCH:
                        act.wait_ge(S["qkv_done"], n + 1)
                        act.wait_ge(S["silu_done"], n - 2 if c >= 3 else m * NCH)
                        act.activation(cv[:, c % 3, :], CONV[c % 3][:], ACT.Copy, scale=cw[:, c, 3:4]).then_inc(S["tap0"], 1)
                    if c >= 1:
                        d = (c - 1) % 3
                        act.wait_ge(S["conv_done"], n * 3)
                        act.activation(sg[:, d, :], cv[:, d, :], ACT.Sigmoid).then_inc(S["sig_done"], 1)
                    if c == 4 and beside:
                        beside()
                    if c == 5:
                        act.wait_ge(S["bmT_done"], m + 1)
                        act.wait_ge(S["bm_tr"], m)
                        act.wait_ge(S["beta_out"], m * 16)
                        act.activation(bmT[:], TR[0][0:2 * NHD, :], ACT.Sigmoid).then_inc(S["bm_sig"], 1)

            def batch(b, final=False):
                act.wait_ge(S["x_out"], 1 + b * 4)
                for gi in range(2):
                    m = b * 2 + gi
                    if gi == 1:
                        front(m)
                    act.wait_ge(S["bm_tr"], m + 1)
                    act.activation(bm[:, gi * GT:gi * GT + GT, :], VT[:, 0:GT * 2 * NHD].rearrange("p (t c) -> p t c", t=GT), ACT.Copy).then_inc(S["bm_done"], 1)
                    for t in range(GT):
                        act.wait_ge(S["tok_done"], m * 4 + t + 1)
                        if t >= 2:
                            act.wait_ge(S["ss_done"], m * GT + t - 1)
                        act.activation(sq[:, t % 2, :], TOK4[t][:], ACT.Square).then_inc(S["sq_done"], 1)
                        if t % 2 == 1:
                            act.wait_ge(S["v_tr"], m * 2 + t // 2 + 1)
                            act.activation(v[:, gi * GT + t - 1:gi * GT + t + 1, :], VT[:].rearrange("p (t d) -> p t d", t=2), ACT.Copy).then_inc(S["v_done"], 1)
                    for t in range(GT):
                        hi_qk(m, t)
                    for j in range(8):
                        q2 = slice(4 * (j // 2) + j % 2, 4 * (j // 2) + 4, 2)
                        gb = QKV[j % 2][:].rearrange("p (h c t) -> p h c t", h=2, c=2)
                        act.wait_ge(S["gk_done"], 1 + m * 8 + j + 1)
                        act.wait_ge(S["g_out"], 1 + m * 64)
                        act.activation(graw[:, q2, :], gb[:, :, 1, :], ACT.Copy).then_inc(S["graw_done"], 1)
                        act.wait_ge(S["kq_done"], m * 8 + j + 1)
                        act.activation(kq_w[:, gi, HI, q2, :], kq[:, j % 2], ACT.Copy).then_inc(S["kq_hi"], 1)
                        act.wait_ge(S["graw_done"], m * 8 + j + 1)
                        act.activation(g_w[:, gi, HI, q2, :], graw[:, q2, :], ACT.Copy).then_inc(S["g_hi"], 1)

                def inverse_hi():
                    act.wait_ge(S["a_step"], 1 + b * 3 + 3)
                    act.activation(t_w[:, :, 0, :], scm[:], ACT.Copy).then_inc(S["t_hi"], 1)

                if final:
                    inverse_hi()
                else:
                    front(b * 2 + 2, beside=inverse_hi)

                def chunk(gi, n, beside=None):
                    m = b * 2 + gi
                    rows = slice(C * n, C * n + C)
                    for j in range(2):
                        q8 = slice(8 * j, 8 * j + 8)
                        if n == 0:
                            act.wait_ge(S["v_done"], m * 2 + 2)
                            act.wait_ge(S["ps2"], 1 + m * 8)
                            act.activation(r_w[rows, HI, q8, :], v[rows, gi * GT + 2 * j:gi * GT + 2 * j + 2, :].rearrange("p t (h d) -> p (t h) d", h=NHD), ACT.Copy).then_inc(S["r_hi"], 1)
                        else:
                            act.wait_ge(S["r_done"], m * 6 + (n - 1) * 2 + j + 1)
                            act.activation(r_w[rows, HI, q8, :], r[rows, q8, :], ACT.Copy).then_inc(S["r_hi"], 1)
                    for j in range(2):
                        q8 = slice(8 * j, 8 * j + 8)
                        act.wait_ge(S["ps2"], 1 + m * 8 + n * 2 + j + 1)
                        act.wait_ge(S["o_done"], 1 + m * 2)
                        act.activation(u_w[rows, HI, q8, :], QKV[j][rows, :].rearrange("p (q d) -> p q d", q=8), ACT.Copy).then_inc(S["u_hi"], 1)

                def squares(m):
                    act.wait_ge(S["om1"], 1 + m * 4 + 4)
                    act.wait_ge(S["o_lo"], 1 + m * 2)
                    act.activation(full[:], om.rearrange("p t d -> p (t d)").rearrange("p (h n) -> p h n", h=2), ACT.Square).then_inc(S["osq"], 1)

                def split(m):
                    for h in range(2):
                        act.wait_ge(S["otr"], 1 + m * 2 + h + 1)
                        act.wait_ge(S["oss"], m + 1)
                        act.wait_ge(S["wo_done"], 1 + m * 2)
                        act.activation(a_w[:, HI, h, :], OT[h][:], ACT.Copy, scale=nw[:]).then_inc(S["o_hi"], 1)
                        act.activation(full[:, h, :], OT[h][:], ACT.Copy, scale=nw[:]).then_inc(S["o_full"], 1)

                for n in range(NC):
                    chunk(0, n)
                for n in range(NC):
                    chunk(1, n)
                    if n == 1:
                        squares(2 * b)
                split(2 * b)
                squares(2 * b + 1)
                split(2 * b + 1)

            front(0)
            with act.Fori(0, NB - 1) as b:
                batch(b)
            batch(NB - 1, final=True)

        @block.vector
        def _(dve):
            def lo_qk(m, t):
                dve.wait_ge(S["qk_hi"], m * GT + t + 1)
                dve.tensor_tensor(qk_w[:, LO, t], BACK[:].rearrange("p (c t) -> p c t", c=4), qk_w[:, HI, t], ALU.subtract).then_inc(S["qk_lo"], 1)

            def stats_of(n, g):
                dve.wait_ge(S["m_mv"], n * GT)
                dve.nop(nofuse=True)
                for t in range(GT):
                    dve.bn_stats(stats[:, t, :], x[:, bass.ds(g * GT + t, 1), :]).then_inc(S["m_bn"], 1)
                dve.wait_ge(S["m_bn"], n * GT + GT)
                dve.nop(nofuse=True)
                dve.wait_ge(S["m_norm"], n * GT)
                dve.nop(nofuse=True)
                for t in range(GT):
                    dve.bn_aggr(mv[:, t, :], stats[:, t, :]).then_inc(S["m_mv"], 1)

            def norm_stats(m):
                stats_of(2 * m, m)

            def norm_apply(m):
                dve.wait_ge(S["m_rstd"], 2 * m + 1)
                for t in range(GT):
                    xx = x[:, bass.ds(m * GT + t, 1), :]
                    dve.tensor_scalar(xx, xx, mv[:, t, 0:1], rstd[:, t:t + 1], ALU.subtract, ALU.mult).then_inc(S["m_norm"], 1)

            def norm_scale(m):
                dve.wait_ge(S["m_norm"], 2 * m * GT + GT)
                dve.tensor_tensor(xg(m), xg(m), lnf_sb[:, 0:1, :].to_broadcast([P, GT, DM]), ALU.mult).then_inc(S["fin1"], 1)

            def norm_shift(m):
                dve.wait_ge(S["fin1"], m + 1)
                dve.tensor_tensor(xg(m), xg(m), lnf_sb[:, 1:2, :].to_broadcast([P, GT, DM]), ALU.add).then_inc(S["fin2"], 1)

            def attn_stats(m):
                dve.wait_ge(S["fin2"], m + 1)
                stats_of(2 * m + 1, m)

            def front_norm(m):
                dve.wait_ge(S["m_rstd"], 2 * m + 2)
                dve.wait_ge(S["tr_done"], m * 2)
                for t in range(GT):
                    dve.tensor_scalar(hn[:, t, :], x[:, bass.ds(m * GT + t, 1), :], mv[:, t, 0:1], rstd[:, t:t + 1], ALU.subtract, ALU.mult)\
                        .then_inc(S["m_norm"], 1)

            def front_low(m):
                for h in range(2):
                    dve.wait_ge(S["a_hi"], m * 2 + h + 1)
                    dve.tensor_tensor(a_w[:, LO, h, :], TR[h][:], a_w[:, HI, h, :].bitcast(F32), ALU.subtract).then_inc(S["a_lo"], 1)

            def front_conv(m, c):
                n = m * NCH + c
                dve.wait_ge(S["tap0"], n + 1)
                src = CONV[c % 3][:].rearrange("p (s t) -> p s t", s=GT)
                dst = cv[:, c % 3, :].rearrange("p (s t) -> p s t", s=GT)
                for k in range(1, 4):
                    if k > 1:
                        dve.wait_ge(S["conv_done"], n * 3 + k - 1)
                    dve.scalar_tensor_tensor(dst[:, :, k:P], src[:, :, 0:P - k], cw[:, c, 3 - k:4 - k], dst[:, :, k:P], ALU.mult, ALU.add)\
                        .then_inc(S["conv_done"], 1)

            def batch(b, final=False):
                for gi in range(2):
                    m = b * 2 + gi
                    ahead = not (final and gi == 1)
                    if gi == 1:
                        front_norm(m)
                        front_low(m)
                        for c in range(NCH):
                            front_conv(m, c)
                    for t in range(GT):
                        dve.wait_ge(S["sq_done"], m * GT + t + 1)
                        if t == 0:
                            dve.wait_ge(S["ors"], 1 + b * 2)
                        dve.tensor_reduce(ss[:, t, :], sq[:, t % 2, :].rearrange("p (h d) -> p h d", d=HD), AX.X, ALU.add).then_inc(S["ss_done"], 1)
                    for t in range(GT):
                        dve.wait_ge(S["rs_done"], 1 + m * GT + t + 1)
                        if t >= 2:
                            dve.wait_ge(S["back_done"], m * GT + t - 1)
                        dve.tensor_tensor(qkn[:, t % 2, :].rearrange("p (h d) -> p h d", d=HD), TOK4[t][:].rearrange("p (h d) -> p h d", d=HD),
                                          rs[:, t, :].unsqueeze(2).to_broadcast([P, 2 * NHD, HD]), ALU.mult).then_inc(S["qkn_done"], 1)
                        if t >= 1:
                            lo_qk(m, t - 1)
                    lo_qk(m, GT - 1)
                    for j in range(8):
                        gb = QKV[j % 2][:].rearrange("p (h c t) -> p h c t", h=2, c=2)
                        dve.wait_ge(S["graw_done"], m * 8 + j + 1)
                        if j >= 2:
                            dve.wait_ge(S["kq_lo"], 1 + m * 8 + j - 1)
                        else:
                            dve.wait_ge(S["kq_lo"], 1 + m * 8)
                        dve.tensor_tensor(kq[:, j % 2], gb[:, :, 0, :], causal[:], ALU.mult).then_inc(S["kq_done"], 1)
                        if ahead and j % 2 == 1:
                            (norm_stats, norm_apply, norm_scale, norm_shift)[j // 2](m + 1)
                    if ahead:
                        attn_stats(m + 1)
                nxt = b * 2 + 2
                if not final:
                    front_norm(nxt)
                    front_low(nxt)
                    front_conv(nxt, 0)
                    front_conv(nxt, 1)
                dve.wait_ge(S["gcm_in"], 1 + b * 32 + 32)
                dve.tensor_tensor(acm, gcm[:], bcm[:].unsqueeze(2).to_broadcast([P, C, C]), ALU.mult).then_inc(S["a_step"], 1)
                dve.wait_ge(S["a_step"], 1 + b * 3 + 1)
                dve.tensor_tensor(acm, acm, strict[:], ALU.mult).then_inc(S["a_step"], 1)
                dve.wait_ge(S["a_step"], 1 + b * 3 + 2)
                dve.wait_ge(S["g_lo"], b * 16 + 16)
                diag = lambda f: f.rearrange("p (d x) -> p d x", d=4)[:, :, 0:8 * C].rearrange("p d (i j) -> p d i j", j=C)
                acm_d, tcm_d = diag(acm_f[:]), diag(tcm_f[:])
                for i in range(1, 8):
                    pr = prod[:, 0:4 * i * i].rearrange("p (d k j) -> p d k j", d=4, j=i)
                    base = b * 30 + 2 * (i - 1)
                    dve.wait_ge(S["ps_r"], 1 + base)
                    dve.tensor_tensor(pr, acm_d[:, :, i, 0:i].unsqueeze(2).to_broadcast([P, 4, i, i]),
                                      tcm_d[:, :, 0:i, 0:i].rearrange("p d j k -> p d k j"), ALU.mult).then_inc(S["ps_r"], 1)
                    dve.wait_ge(S["ps_r"], 1 + base + 1)
                    dve.tensor_reduce(tcm_d[:, :, i, 0:i], pr, AX.X, ALU.add).then_inc(S["ps_r"], 1)

                def product(out, left, right, count, first=0):
                    ni, nj, nk = left.shape[1], left.shape[2], right.shape[2]
                    pr = prod[:, first:first + ni * nk * nj].rearrange("p (i k j) -> p i k j", i=ni, j=nj)
                    dve.wait_ge(S["ps_r"], 1 + count)
                    dve.tensor_tensor(pr, left.unsqueeze(2).to_broadcast([P, ni, nk, nj]),
                                      right.rearrange("p j k -> p k j").unsqueeze(1).to_broadcast([P, ni, nk, nj]), ALU.mult).then_inc(S["ps_r"], 1)
                    dve.wait_ge(S["ps_r"], 1 + count + 1)
                    dve.tensor_reduce(out, pr, AX.X, ALU.add).then_inc(S["ps_r"], 1)

                if not final:
                    front_conv(nxt, 2)
                r0 = b * 30 + 14
                for e in range(2):
                    o, q, r8 = 16 * e, 16 * e + 8, 16 * e + 16
                    product(xm[:, 8 * e:8 * e + 8, 0:8], acm[:, q:r8, o:q], tcm[:, o:q, o:q], r0 + 4 * e)
                    product(tcm[:, q:r8, o:q], tcm[:, q:r8, q:r8], xm[:, 8 * e:8 * e + 8, 0:8], r0 + 4 * e + 2)
                if not final:
                    front_conv(nxt, 3)
                r1 = r0 + 8
                product(xm[:, :, 0:8], acm[:, 16:32, 0:16], tcm[:, 0:16, 0:8], r1)
                product(xm[:, :, 8:16], acm[:, 16:32, 8:16], tcm[:, 8:16, 8:16], r1 + 2)
                product(tcm[:, 16:24, 0:16], tcm[:, 16:24, 16:24], xm[:, 0:8, :], r1 + 4)
                product(tcm[:, 24:32, 0:16], tcm[:, 24:32, 16:32], xm[:, :, :], r1 + 6)
                dve.wait_ge(S["ps_r"], 1 + b * 30 + 30)
                dve.wait_ge(S["t_hi"], 1 + b)
                dve.tensor_tensor(scm[:], tcm.rearrange("p i j -> p j i"), bcm[:].unsqueeze(2).to_broadcast([P, C, C]), ALU.mult).then_inc(S["a_step"], 1)
                dve.wait_ge(S["a_step"], 1 + b * 3 + 3)
                dve.wait_ge(S["t_hi"], 1 + b + 1)
                dve.tensor_tensor(t_w[:, :, 1, :], scm[:], t_w[:, :, 0, :], ALU.subtract).then_inc(S["t_lo"], 1)
                if not final:
                    front_conv(nxt, 4)
                    front_conv(nxt, 5)
                def chunk(gi, n, beside=()):
                    m = b * 2 + gi
                    vq = v[:, gi * GT:gi * GT + GT, :].rearrange("p t (h d) -> p (t h) d", h=NHD)
                    rows = slice(C * n, C * n + C)
                    for j in range(2):
                        q8 = slice(8 * j, 8 * j + 8)
                        if n > 0:
                            dve.wait_ge(S["ps1"], m * 6 + (n - 1) * 2 + j + 1)
                            dve.tensor_tensor(r[rows, q8, :], vq[rows, q8, :], TR[j][rows, :].rearrange("p (q d) -> p q d", q=8), ALU.subtract).then_inc(S["r_done"], 1)
                    for j in range(2):
                        q8 = slice(8 * j, 8 * j + 8)
                        dve.wait_ge(S["r_hi"], m * 8 + 2 * n + j + 1)
                        dve.tensor_tensor(r_w[rows, LO, q8, :], (vq if n == 0 else r)[rows, q8, :], r_w[rows, HI, q8, :], ALU.subtract).then_inc(S["r_lo"], 1)
                    for work in beside[0:1]:
                        work()
                    for j in range(2):
                        q8 = slice(8 * j, 8 * j + 8)
                        dve.wait_ge(S["u_hi"], m * 8 + 2 * n + j + 1)
                        dve.tensor_tensor(u_w[rows, LO, q8, :], QKV[j][rows, :].rearrange("p (q d) -> p q d", q=8), u_w[rows, HI, q8, :], ALU.subtract).then_inc(S["u_lo"], 1)
                    for work in beside[1:2]:
                        work()

                def one_minus_mix(gi):
                    m = b * 2 + gi
                    dve.wait_ge(S["vm1"], 1 + m)
                    dve.tensor_scalar(omix[:], bm[:, gi * GT:gi * GT + GT, NHD:2 * NHD], -1.0, 1.0, ALU.mult, ALU.add).then_inc(S["omix1"], 1)

                def mixed(gi, j):
                    m = b * 2 + gi
                    mix = bm[:, gi * GT:gi * GT + GT, NHD:2 * NHD]
                    dve.wait_ge(S["o_done"], 1 + m * 2 + j + 1)
                    dve.wait_ge(S["otr"], 1 + m * 2)
                    dve.tensor_tensor(om[:, 2 * j:2 * j + 2, :].rearrange("p t (h d) -> p t h d", h=NHD), TOK[j][:].rearrange("p (t h d) -> p t h d", t=2, h=NHD),
                                      mix[:, 2 * j:2 * j + 2].unsqueeze(3).to_broadcast([P, 2, NHD, HD]), ALU.mult).then_inc(S["om1"], 1)

                def add_v(gi):
                    m = b * 2 + gi
                    dve.wait_ge(S["vm1"], 1 + m + 1)
                    dve.wait_ge(S["om1"], 1 + m * 4 + 2)
                    dve.tensor_tensor(om, om, vm, ALU.add).then_inc(S["om1"], 2)

                def sum_squares(gi):
                    m = b * 2 + gi
                    dve.wait_ge(S["osq"], m + 1)
                    dve.tensor_reduce(ss[:, :, 0:NHD], full[:].rearrange("p a n -> p (a n)").rearrange("p (t h d) -> p t h d", t=GT, h=NHD), AX.X, ALU.add).then_inc(S["oss"], 1)

                def scaled(gi):
                    m = b * 2 + gi
                    dve.wait_ge(S["ors"], 1 + m + 1)
                    dve.tensor_tensor(om.rearrange("p t (h d) -> p t h d", h=NHD), om.rearrange("p t (h d) -> p t h d", h=NHD),
                                      rs[:, :, 0:NHD].unsqueeze(3).to_broadcast([P, GT, NHD, HD]), ALU.mult).then_inc(S["o3"], 1)

                def low_parts(gi):
                    m = b * 2 + gi
                    for h in range(2):
                        dve.wait_ge(S["o_full"], m * 2 + h + 1)
                        dve.tensor_tensor(a_w[:, LO, h, :], full[:, h, :], a_w[:, HI, h, :].bitcast(F32), ALU.subtract).then_inc(S["o_lo"], 1)

                def add_out(gi):
                    m = b * 2 + gi
                    for j in range(2):
                        dve.wait_ge(S["wo_done"], 1 + m * 2 + j + 1)
                        xx = x[:, bass.ds(m * GT + 2 * j, 2), :]
                        dve.tensor_tensor(xx, xx, OT[j][:].rearrange("p (a d) -> p a d", a=2), ALU.add).then_inc(S["x_out"], 1)

                for n in range(NC):
                    chunk(0, n)
                chunk(1, 0, (lambda: one_minus_mix(0), lambda: mixed(0, 0)))
                chunk(1, 1, (lambda: mixed(0, 1), lambda: add_v(0)))
                chunk(1, 2, (lambda: sum_squares(0), lambda: None))
                chunk(1, 3, (lambda: scaled(0), lambda: None))
                low_parts(0)
                one_minus_mix(1)
                mixed(1, 0)
                mixed(1, 1)
                add_out(0)
                add_v(1)
                sum_squares(1)
                scaled(1)
                low_parts(1)
                add_out(1)

            norm_stats(0)
            norm_apply(0)
            norm_scale(0)
            norm_shift(0)
            attn_stats(0)
            dve.wait_ge(S["ld_w"], 80)
            dve.wait_ge(S["bmz"], 1)
            dve.tensor_copy(bm_z[:, 0, :, 0:2 * NHD], st_bm[:]).then_inc(S["bmz"], 1)
            dve.wait_ge(S["whi"], 3)
            dve.tensor_tensor(qkv_w[:, LO], st_qkv, qkv_w[:, HI].bitcast(F32), ALU.subtract).then_inc(S["wlo"], 1)
            dve.tensor_tensor(bm_w[:, LO], bm_z[:, 0], bm_w[:, HI].bitcast(F32), ALU.subtract).then_inc(S["wlo"], 1)
            dve.tensor_tensor(wo_w[:, LO], st_wo, wo_w[:, HI].bitcast(F32), ALU.subtract).then_inc(S["wlo"], 1)
            front_norm(0)
            front_low(0)
            for c in range(NCH):
                front_conv(0, c)
            dve.wait_ge(S["masks"], 6)
            with dve.Fori(0, NB - 1) as b:
                batch(b)
            batch(NB - 1, final=True)

        @block.tensor
        def _(pe):
            def back(m, t):
                pe.wait_ge(S["qkn_done"], 1 + m * GT + t + 1)
                pe.wait_ge(S["qk_lo"], 1 + m * GT + t)
                for c in range(4):
                    last = pe.transpose(BACK[:, c * P:(c + 1) * P], qkn[:, t % 2, c * P:(c + 1) * P], ident[:])
                last.then_inc(S["back_done"], 1)

            hp = [(h, p) for h in range(2) for p in PASSES]
            pe.wait_ge(S["wlo"], 3)
            def front(m):
                pe.wait_ge(S["m_norm"], (2 * m + 2) * GT)
                pe.wait_ge(S["a_lo"], m * 2)
                for h in range(2):
                    for t in range(GT):
                        last = pe.transpose(TR[h][:, t * P:(t + 1) * P], hn[:, t, h * P:(h + 1) * P], ident[:])
                    last.then_inc(S["tr_done"], 1)
                pe.wait_ge(S["a_lo"], m * 2 + 2)
                for c in range(NCH):
                    n = m * NCH + c
                    if c >= 3:
                        pe.wait_ge(S["conv_done"], (n - 2) * 3)
                    elif c == 2:
                        pe.wait_ge(S["qk_lo"], 1 + m * GT)
                    for i, (h, (p, q)) in enumerate(hp):
                        last = pe.matmul(CONV[c % 3][:], qkv_w[:, p, h, c * P:(c + 1) * P], a_w[:, q, h, :], start=(i == 0), stop=(i == 5))
                    last.then_inc(S["qkv_done"], 1)
                    if c == 3:
                        for i, (h, (p, q)) in enumerate(hp):
                            last = pe.matmul(TR[0][:], bm_w[:, p, h, :], a_w[:, q, h, :], start=(i == 0), stop=(i == 5))
                        last.then_inc(S["bmT_done"], 1)

            def batch(b, final=False):
                pe.wait_ge(S["x_out"], 1 + b * 4)
                for gi in range(2):
                    m = b * 2 + gi
                    if gi == 1:
                        front(m)
                    pe.wait_ge(S["bm_sig"], m + 1)
                    pe.nop(nofuse=True)
                    for t in range(GT):
                        last = pe.transpose(VT[:, t * 2 * NHD:(t + 1) * 2 * NHD], bmT[:, t * P:(t + 1) * P], ident[0:2 * NHD, 0:2 * NHD])
                    last.then_inc(S["bm_tr"], 1)
                    pe.wait_ge(S["bm_done"], m + 1)
                    for t in range(GT):
                        pe.wait_ge(S["silu_done"], m * NCH + (4 if t == 0 else 6))
                        for c in range(4):
                            last = pe.transpose(TOK4[t][:, c * P:(c + 1) * P], qkv_t[:, c, t * P:(t + 1) * P], ident[:])
                        last.then_inc(S["tok_done"], 1)
                        pe.wait_ge(S["silu_done"], m * NCH + 6)
                        if t == 2:
                            pe.wait_ge(S["v_done"], m * 2 + 1)
                        for c in range(2):
                            last = pe.transpose(VT[:, (t % 2) * DM + c * P:(t % 2) * DM + (c + 1) * P], qkv_t[:, 4 + c, t * P:(t + 1) * P], ident[:])
                        if t % 2 == 1:
                            last.then_inc(S["v_tr"], 1)
                    for t in range(GT):
                        back(m, t)
                    for j in range(8):
                        t = j // 2
                        pe.wait_ge(S["qk_lo"], 1 + m * GT + t + 1)
                        if j >= 2:
                            pe.wait_ge(S["kq_done"], m * 8 + j - 1)
                        for hh in range(2):
                            hd = j % 2 + 2 * hh
                            rows = slice((hd % 2) * HD, (hd % 2) * HD + HD)
                            for i, (p, q) in enumerate(PASSES):
                                o = QKV[j % 2][:, hh * 256:(hh + 1) * 256].rearrange("p (c t) -> p c t", c=2)
                                last = pe.matmul(o, qk_w[rows, p, t, 2 + hd // 2, :], qk_w[rows, q, t, hd // 2::2, :], start=(i == 0), stop=(i == 2))
                        last.then_inc(S["gk_done"], 1)
                if not final:
                    front(b * 2 + 2)
                pe.wait_ge(S["tt_in"], b * 64 + 64)
                pe.wait_ge(S["kq_lo"], 1 + b * 16 + 16)
                pe.nop(nofuse=True)
                pe.wait_ge(S["g_lo"], b * 16 + 16)

                def chunk(gi, n):
                    m = b * 2 + gi
                    rows = slice(C * n, C * n + C)
                    if n > 0:
                        for j in range(2):
                            pe.wait_ge(S["u_lo"], 1 + m * 8 + (n - 1) * 2 + j + 1)
                            pe.nop(nofuse=True)
                            for q in range(8 * j, 8 * j + 8):
                                for i, (p, s) in enumerate(PASSES):
                                    last = pe.matmul(TR[j][rows, (q % 8) * HD:(q % 8 + 1) * HD], g_w[0:C * n, gi, p, q, rows], u_w[0:C * n, s, q, :],
                                                     start=(i == 0), stop=(i == 2))
                            last.then_inc(S["ps1"], 1)
                    for j in range(2):
                        pe.wait_ge(S["r_lo"], m * 8 + 2 * n + j + 1)
                        pe.nop(nofuse=True)
                        for q in range(8 * j, 8 * j + 8):
                            for i, (p, s) in enumerate(PASSES):
                                last = pe.matmul(QKV[j][rows, (q % 8) * HD:(q % 8 + 1) * HD], tt[rows, gi * NQ + q, p, :], r_w[rows, s, q, :],
                                                 start=(i == 0), stop=(i == 2))
                        last.then_inc(S["ps2"], 1)

                def outputs(gi):
                    m = b * 2 + gi
                    for j in range(2):
                        pe.wait_ge(S["u_lo"], 1 + m * 8 + 6 + j + 1)
                        pe.wait_ge(S["om1"], 1 + m * 4)
                        for q in range(8 * j, 8 * j + 8):
                            for i, (p, s) in enumerate(PASSES):
                                last = pe.matmul(TOK[j][:, (q % 8) * HD:(q % 8 + 1) * HD], kq_w[:, gi, p, q, :], u_w[:, s, q, :], start=(i == 0), stop=(i == 2))
                        last.then_inc(S["o_done"], 1)

                def turned(gi):
                    m = b * 2 + gi
                    pe.wait_ge(S["o3"], m + 1)
                    pe.wait_ge(S["x_out"], 1 + m * 2)
                    for h in range(2):
                        for t in range(GT):
                            last = pe.transpose(OT[h][:, t * P:(t + 1) * P], om[:, t, h * P:(h + 1) * P], ident[:])
                        last.then_inc(S["otr"], 1)

                def wo_product(gi):
                    m = b * 2 + gi
                    pe.wait_ge(S["o_lo"], 1 + m * 2 + 2)
                    for j in range(2):
                        for t in range(2 * j, 2 * j + 2):
                            tok = slice(t * P, (t + 1) * P)
                            for i, (h, (p, q)) in enumerate(hp):
                                last = pe.matmul(OT[j][:, (t % 2) * DM:(t % 2 + 1) * DM], a_w[:, p, h, tok], wo_w[:, q, h, :], start=(i == 0), stop=(i == 5))
                        last.then_inc(S["wo_done"], 1)

                for n in range(NC):
                    chunk(0, n)
                outputs(0)
                for n in range(NC):
                    chunk(1, n)
                turned(0)
                outputs(1)
                wo_product(0)
                turned(1)
                wo_product(1)

            front(0)
            with pe.Fori(0, NB - 1) as b:
                batch(b)
            batch(NB - 1, final=True)


def slot_tiles(tokens, E, K=2):
    n = K * tokens // P + E
    return n + n % 2


def experts(nc, sems, x, ident, half, slots, y_d, wr, wgu, bias, wd, out):
    NSEQ, DM = x.shape[1], x.shape[2]
    GT = 4
    NG = NSEQ // GT
    GN = GT * P
    E = wr.shape[1]
    INTER = wd.shape[1]
    LIMIT, ALPHA = 7.0, 1.702
    NT = slot_tiles(NSEQ * P, E)
    NP = NT // 2
    TMAX = 2 * NSEQ
    assert INTER == P
    with ExitStack() as ctx:
        def sb(name, shape, dt=F32, where=ctx):
            return where.enter_context(nc.sbuf_tensor(name, shape, dt))

        bk = [ctx.enter_context(nc.psum_tensor(f"mk{i}", [P, 512], F32)) for i in range(8)]
        TRX, GU, AT, DN = bk[0:2], bk[2:4], bk[4:6], bk[6:8]
        LGT, LGB, WITHIN, TOTAL = GU[0], GU[1], AT[0], AT[1]
        m_all = sb("m_all", [P, NSEQ, DM])
        gu_w = sb("gu_w", [P, 2, E, 2, 2 * P], F32R)
        bias_w = sb("bias_w", [P, E, 2, DM], BF16)
        sel = sb("sel", [P, P], BF16)
        pos_i = sb("pos_i", [P, 2, NSEQ], I32)
        wt = sb("wt", [P, NSEQ, 2])
        te_i = sb("te_i", [P, NT], I32)
        r_w = sb("rt_w", [P, 2, 2, P], F32R)
        with ExitStack() as early:
            lg = sb("lg", [P, NSEQ, E], where=early)
            mx = sb("mx", [P, NSEQ, 8], where=early)
            ix = sb("ix", [P, NSEQ, 8], U32, where=early)
            ixf = sb("ixf", [P, NSEQ, 2], where=early)
            df = sb("df", [P, NSEQ, 2], where=early)
            oh = sb("oh", [P, 2, NSEQ, E], where=early)
            z = sb("z", [P, NSEQ, E], where=early)
            tot = sb("tot", [P, E, NSEQ], where=early)
            notfirst = sb("notfirst", [P, E, NSEQ], where=early)
            cum = sb("cum", [P, E, NSEQ], where=early)
            cnt = sb("cnt", [P, E], where=early)
            need = sb("need", [P, E], where=early)
            ends = sb("ends", [P, E], where=early)
            starts = sb("starts", [P, E], where=early)
            posf = sb("posf", [P, 2, NSEQ], where=early)
            tef = sb("tef", [P, NT], where=early)
            cmp = sb("cmp", [P, NT, E], where=early)
        dn_w = sb("dn_w", [P, 2, E, DM], F32R)
        with ExitStack() as early:
            m_w = sb("m_w", [P, 2, 2, GN], F32R, where=early)
            st = sb("st_e", [P, 2, 2, 2 * P], where=early)
            st_d = sb("st_ed", [P, 2, DM], where=early)
            st_b = sb("st_eb", [P, 2, 2, DM], where=early)
            lgT = sb("lgT", [E, GN], where=early)
            r_z = sb("rt_z", [P, 2, P], where=early)
            st_r = sb("st_r", [P, 2, E], where=early)
            zrow = sb("zrow", [P, DM], where=early)
            stats = sb("stats3", [P, NSEQ, 6], where=early)
            mv = sb("mv3", [P, NSEQ, 2], where=early)
            veps = sb("veps3", [P, NSEQ], where=early)
            rstd = sb("rstd3", [P, NSEQ], where=early)
            before = sb("before", [P, P], where=early)
            ones = sb("ones3", [P, P], where=early)
            iota_t = sb("iota_t", [P, NT], where=early)
        xs = sb("xs", [P, 2, 2, DM])
        xs_w = sb("xs_w", [P, 2, 2, 2, 2, P], F32R)
        gs = sb("gs3", [P, 2, 2, P])
        sg = sb("sg3", [P, 2, 2, P])
        us = sb("us3", [P, 2, 2, P])
        ac_w = sb("ac_w", [P, 2, 2, 2, P], F32R)
        y = sb("y3", [P, 2, 2, DM])

        names = """ld_r ld_e0 ld_e1 slots_zero consts r_hi r_lo stats_done mv_done veps_done rstd_done norm_done tr_done
        m_hi m_lo lgT_done lgT_out lgB_done lg_done max_done ix_done plan df_done wt_done counted
        tot_out pos_out te_out scattered w_hi w_lo b_hi b_r1 b_mid b_lo xs_in0 xs_in1 trx hix lox gu gsd usd sgd gld acd att hia loa
        dn yev y_out0 y_out1 added0 added1 out_done""".split()
        S = {n: sems.enter_context(nc.semaphore("e_" + n)) for n in names}
        gathered = [sems.enter_context(nc.semaphore(f"e_gathered{g}")) for g in range(NG)]
        primed = """""".split()
        block = ctx.enter_context(nc.Block())
        xs_v = slots.rearrange("(n a p) d -> n p a d", a=2, p=P)
        y_v = y_d.rearrange("(n a p) d -> n p a d", a=2, p=P)
        gu_d = wgu.rearrange("e (h p) c -> e p h c", p=P)
        BROWS = (0, 32, 64)

        def later(m):
            return not isinstance(m, int) or m >= 2

        def item(i, c):
            return 2 * i + c, i + c // 2, c % 2

        def steps(eng, step):
            for n in range(-1, 4):
                step(0, n, tr=True, mid=n >= 0, at=n >= 1, down=n >= 2)
            with eng.Fori(0, (NP - 6) // 2) as i:
                step(i, 4)
                step(i, 5)
            for n in range(NP - 2, NP + 2):
                step(0, n, tr=n < NP - 1, mid=n < NP, at=n < NP + 1)

        @block.sync
        def _(sp):
            for n in primed:
                sp.sem_inc(S[n], 1)
            sp.dma_start(st_r[:], wr.rearrange("(h p) e -> p h e", p=P)).then_inc(S["ld_r"], 16)
            sp.wait_ge(S["consts"], 2)
            sp.dma_start(slots.rearrange("(p a) d -> p a d", p=P), zrow[:].unsqueeze(1).to_broadcast([P, NT, DM])).then_inc(S["slots_zero"], 16)
            for e in range(E):
                b = e % 2
                if e >= 2:
                    sp.wait_ge(S["w_lo"], 2 * (e - 1))
                    sp.wait_ge(S["b_lo"], e - 1)
                ld = S["ld_e0"] if b == 0 else S["ld_e1"]
                sp.dma_start(st[:, b], gu_d[e]).then_inc(ld, 16)
                sp.dma_start(st_d[:, b], wd[e]).then_inc(ld, 16)
                for r in BROWS:
                    sp.dma_start(st_b[r:r + 1, b], bias[e:e + 1]).then_inc(ld, 16)

            def load(i, c):
                m, before_m, b = item(i, c)
                if later(m):
                    sp.wait_ge(S["trx"], m - 1)
                src = xs_v[m] if isinstance(m, int) else xs_v[bass.ds(m, 1)].rearrange("o p a d -> (o p) a d")
                sp.dma_start(xs[:, b], src).then_inc(S["xs_in0"] if b == 0 else S["xs_in1"], 16)

            def store(i, c):
                m, before_m, b = item(i, c)
                sp.wait_ge(S["yev"], m + 1)
                dst = y_v[m] if isinstance(m, int) else y_v[bass.ds(m, 1)].rearrange("o p a d -> (o p) a d")
                sp.dma_start(dst, y[:, b]).then_inc(S["y_out0"] if b == 0 else S["y_out1"], 16)

            LAG = 5
            sp.wait_ge(S["scattered"], 16 * 2 * NSEQ)
            sp.wait_ge(S["w_lo"], 2 * E)
            sp.wait_ge(S["b_lo"], E)
            for n in range(6):
                load(0, n)
                if n >= LAG:
                    store(0, n - LAG)
            with sp.Fori(0, (NP - 6) // 2) as i:
                for c in range(6, 8):
                    load(i, c)
                    store(i, c - LAG)
            for n in range(NP - LAG, NP):
                store(0, n)
            out_v = out.rearrange("b t d -> t b d")
            with sp.Fori(0, NG) as g:
                sp.wait_ge(S["added1"], (g + 1) * GT)
                sp.dma_start(out_v[:, bass.ds(g * GT, GT), :], x[:, bass.ds(g * GT, GT), :]).then_inc(S["out_done"], 16)
            sp.wait_ge(S["out_done"], 16 * NG)

        @block.gpsimd
        def _(pool):
            pool.memset(zrow[:], 0.0).then_inc(S["consts"], 1)
            pool.memset(st_b[:], 0.0).then_inc(S["consts"], 1)
            pool.memset(r_z[:], 0.0).then_inc(S["consts"], 1)
            pool.iota(iota_t[:], [[1, NT]], base=0, channel_multiplier=0, allow_small_or_imprecise_dtypes=True).then_inc(S["consts"], 1)
            pool.memset(ones[:], 1.0).then_inc(S["consts"], 1)
            pool.memset(notfirst[:], 1.0).then_inc(S["consts"], 1)
            pool.memset(sel[:], 0.0).then_inc(S["consts"], 1)
            pool.wait_ge(S["consts"], 7)
            pool.affine_select(out=before[:], in_=ones[:], compare_op=ALU.is_gt, fill=0.0, base=0, pattern=[[1, P]], channel_multiplier=-1)\
                .then_inc(S["consts"], 1)
            pool.memset(notfirst[:, :, 0:1], 0.0).then_inc(S["consts"], 1)
            for g in range(NG):
                tiles = slice(g * GT, g * GT + GT)
                pool.wait_ge(S["mv_done"], g * GT + GT)
                pool.tensor_scalar(veps[:, tiles], mv[:, tiles, 1], EPS, None, ALU.add).then_inc(S["veps_done"], 1)
                pool.wait_ge(S["veps_done"], g + 1)
                pool.tensor_tensor(rstd[:, tiles], veps[:, tiles], half[:].to_broadcast([P, GT]), ALU.pow).then_inc(S["rstd_done"], 1)
            pool.wait_ge(S["pos_out"], 1)
            pool.wait_ge(S["norm_done"], NSEQ)
            pool.wait_ge(S["slots_zero"], 16)
            for t in range(NSEQ):
                for k in range(2):
                    pool.indirect_dma_start(slots, bass.IndirectOffsetOnAxis(ap=pos_i[:, k, t:t + 1], axis=0), m_all[:, t, :], None)\
                        .then_inc(S["scattered"], 16)

            def gate(i, c):
                m, _, b = item(i, c)
                pool.wait_ge(S["sgd"], m + 1)
                pool.wait_ge(S["gsd"], m + 1)
                pool.tensor_tensor(gs[:, b], gs[:, b], sg[:, b], ALU.mult).then_inc(S["gld"], 1)

            with pool.Fori(0, NP // 2) as i:
                gate(i, 0)
                gate(i, 1)
            pool.wait_ge(S["scattered"], 16 * 2 * NSEQ)
            pool.wait_ge(S["y_out0"], 16 * (NP // 2))
            pool.wait_ge(S["y_out1"], 16 * (NP // 2))
            for t in range(NSEQ):
                if t >= NSEQ // 2:
                    pool.wait_ge(S["added1"], t - NSEQ // 2 + 1)
                for k in range(2):
                    pool.indirect_dma_start(m_all[:, (2 * t + k) % NSEQ, :], None, y_d, bass.IndirectOffsetOnAxis(ap=pos_i[:, k, t:t + 1], axis=0))\
                        .then_inc(gathered[t // GT], 16)

        @block.scalar
        def _(act):
            act.wait_ge(S["r_lo"], 1)
            act.activation(r_w[:, HI], r_z[:], ACT.Copy).then_inc(S["r_hi"], 1)

            def m_parts(g):
                if not isinstance(g, int):
                    act.wait_ge(S["lgT_done"], g)
                for h in range(2):
                    act.wait_ge(S["tr_done"], g * 2 + h + 1)
                    act.activation(m_w[:, HI, h, :], TRX[h][:], ACT.Copy).then_inc(S["m_hi"], 1)

            def logits_out(g):
                act.wait_ge(S["lgB_done"], g + 1)
                act.activation(lg[:, bass.ds(g * GT, GT), :], LGB[:, 0:GT * E].rearrange("p (t e) -> p t e", t=GT), ACT.Copy).then_inc(S["lg_done"], 1)

            m_parts(0)
            act.wait_ge(S["lgT_done"], 1)
            act.activation(lgT[:], LGT[0:E, :], ACT.Copy).then_inc(S["lgT_out"], 1)
            with act.Fori(1, NG) as g:
                m_parts(g)
                logits_out(g - 1)
                act.wait_ge(S["lgT_done"], g + 1)
                act.activation(lgT[:], LGT[0:E, :], ACT.Copy).then_inc(S["lgT_out"], 1)
            logits_out(NG - 1)
            act.wait_ge(S["df_done"], 2)
            act.activation(wt[:], df[:], ACT.Sigmoid).then_inc(S["wt_done"], 1)
            act.wait_ge(S["counted"], 2)
            act.activation(tot[:], TOTAL[:].rearrange("p (t e) -> p e t", t=NSEQ), ACT.Copy).then_inc(S["tot_out"], 1)
            act.wait_ge(S["te_out"], 1)
            act.wait_ge(S["wt_done"], 1)
            for e in range(E):
                b = e % 2
                act.wait_ge(S["ld_e0"] if b == 0 else S["ld_e1"], 80 * (e // 2 + 1))
                act.activation(gu_w[:, HI, e], st[:, b], ACT.Copy).then_inc(S["w_hi"], 1)
                act.activation(dn_w[:, HI, e], st_d[:, b], ACT.Copy).then_inc(S["w_hi"], 1)
                act.activation(bias_w[:, e], st_b[:, b], ACT.Copy).then_inc(S["b_hi"], 1)
                act.wait_ge(S["b_r1"], e + 1)
                act.activation(bias_w[32:64, e], st_b[32:64, b], ACT.Copy).then_inc(S["b_mid"], 1)
                act.activation(bias_w[64:96, e], st_b[64:96, b], ACT.Copy).then_inc(S["b_mid"], 1)
            act.wait_ge(S["w_lo"], 2 * E)
            act.wait_ge(S["b_lo"], E)

            def step(i, n, tr=True, mid=True, at=True, down=True):
                if tr:
                    m, _, b = item(i, n + 1)
                    act.wait_ge(S["trx"], m + 1)
                    if later(m):
                        act.wait_ge(S["gu"], m - 1)
                    act.activation(xs_w[:, b, HI].rearrange("p a h s -> p (a h s)"), TRX[b][:], ACT.Copy).then_inc(S["hix"], 1)
                if mid:
                    m, _, b = item(i, n)
                    act.wait_ge(S["gsd"], m + 1)
                    if later(m):
                        act.wait_ge(S["gld"], m - 1)
                    act.activation(sg[:, b], gs[:, b], ACT.Sigmoid, scale=ALPHA).then_inc(S["sgd"], 1)
                if at:
                    m, _, b = item(i, n - 1)
                    act.wait_ge(S["att"], m + 1)
                    if later(m):
                        act.wait_ge(S["dn"], m - 1)
                    act.activation(ac_w[:, b, HI].rearrange("p a s -> p (a s)"), AT[b][:, 0:2 * P], ACT.Copy).then_inc(S["hia"], 1)
                if down:
                    m, before_m, b = item(i, n - 2)
                    act.wait_ge(S["dn"], m + 1)
                    if later(m):
                        act.wait_ge(S["y_out0"] if b == 0 else S["y_out1"], before_m * 16)
                    act.activation(y[:, b].rearrange("p a d -> p (a d)"), DN[b][:], ACT.Copy).then_inc(S["yev"], 1)

            steps(act, step)

        @block.vector
        def _(dve):
            def norm_stats(g):
                for t in range(g * GT, g * GT + GT):
                    dve.bn_stats(stats[:, t, :], x[:, t, :]).then_inc(S["stats_done"], 1)
                dve.wait_ge(S["stats_done"], g * GT + GT)
                for t in range(g * GT, g * GT + GT):
                    dve.bn_aggr(mv[:, t, :], stats[:, t, :]).then_inc(S["mv_done"], 1)

            norm_stats(0)
            norm_stats(1)
            dve.wait_ge(S["consts"], 9)
            for r in BROWS:
                dve.memset(sel[r:r + 1, :], 1.0).then_inc(S["consts"], 1)
            dve.wait_ge(S["ld_r"], 16)
            dve.wait_ge(S["consts"], 3)
            dve.tensor_copy(r_z[:, :, 0:E], st_r[:]).then_inc(S["r_lo"], 1)
            dve.wait_ge(S["r_hi"], 1)
            dve.tensor_tensor(r_w[:, LO], r_z[:], r_w[:, HI].bitcast(F32), ALU.subtract).then_inc(S["r_lo"], 1)

            def norm(t):
                dve.tensor_scalar(m_all[:, t, :], x[:, t, :], mv[:, t, 0:1], rstd[:, t:t + 1], ALU.subtract, ALU.mult).then_inc(S["norm_done"], 1)

            def top2(g):
                dve.wait_ge(S["lg_done"], g + 1)
                for t in range(g * GT, g * GT + GT):
                    dve.max(mx[:, t, :], lg[:, t, :]).then_inc(S["max_done"], 1)
                dve.wait_ge(S["max_done"], g * GT + GT)
                for t in range(g * GT, g * GT + GT):
                    dve.max_index(ix[:, t, :], mx[:, t, :], lg[:, t, :]).then_inc(S["ix_done"], 1)

            dve.wait_ge(S["rstd_done"], 1)
            for t in range(GT):
                norm(t)
            for g in range(NG):
                if g + 1 < NG:
                    dve.wait_ge(S["rstd_done"], g + 2)
                    for t in range(GT):
                        norm((g + 1) * GT + t)
                if g + 2 < NG:
                    norm_stats(g + 2)
                for h in range(2):
                    dve.wait_ge(S["m_hi"], g * 2 + h + 1)
                    dve.tensor_tensor(m_w[:, LO, h, :], TRX[h][:], m_w[:, HI, h, :].bitcast(F32), ALU.subtract).then_inc(S["m_lo"], 1)
                if g >= 1:
                    top2(g - 1)
            top2(NG - 1)
            dve.tensor_tensor(df[:, :, 0], mx[:, :, 0], mx[:, :, 1], ALU.subtract).then_inc(S["df_done"], 1)
            dve.tensor_tensor(df[:, :, 1], mx[:, :, 1], mx[:, :, 0], ALU.subtract).then_inc(S["df_done"], 1)
            dve.wait_ge(S["ix_done"], NSEQ)
            dve.tensor_copy(ixf[:], ix[:, :, 0:2]).then_inc(S["plan"], 1)
            dve.wait_ge(S["plan"], 1)
            dve.wait_ge(S["consts"], 4)
            for k in range(2):
                dve.tensor_tensor(oh[:, k], iota_t[:, 0:E].unsqueeze(1).to_broadcast([P, NSEQ, E]), ixf[:, :, k:k + 1].to_broadcast([P, NSEQ, E]), ALU.is_equal)\
                    .then_inc(S["plan"], 1)
            dve.wait_ge(S["plan"], 3)
            dve.tensor_tensor(z[:], oh[:, 0], oh[:, 1], ALU.add).then_inc(S["plan"], 1)
            dve.wait_ge(S["tot_out"], 1)
            dve.wait_ge(S["consts"], 9)
            dve.tensor_tensor_scan(cum[:].rearrange("p e t -> p (e t)"), notfirst[:].rearrange("p e t -> p (e t)"), tot[:].rearrange("p e t -> p (e t)"),
                                   0.0, ALU.mult, ALU.add).then_inc(S["plan"], 1)
            dve.wait_ge(S["plan"], 5)
            dve.tensor_scalar(cnt[:], cum[:, :, NSEQ - 1], 1.0 / P, None, ALU.mult).then_inc(S["plan"], 1)
            dve.tensor_tensor(tot[:], cum[:], tot[:], ALU.subtract).then_inc(S["plan"], 1)
            dve.wait_ge(S["plan"], 7)
            below = cmp[:].rearrange("p n e -> p (n e)")[:, 0:E * TMAX].rearrange("p (e n) -> p e n", n=TMAX)
            dve.tensor_tensor(below, iota_t[:, 0:TMAX].unsqueeze(1).to_broadcast([P, E, TMAX]), cnt[:].unsqueeze(2).to_broadcast([P, E, TMAX]), ALU.is_lt)\
                .then_inc(S["plan"], 1)
            dve.wait_ge(S["plan"], 8)
            dve.tensor_reduce(need[:], below, AX.X, ALU.add).then_inc(S["plan"], 1)
            dve.wait_ge(S["plan"], 9)
            dve.tensor_tensor_scan(ends[:], ones[:, 0:E], need[:], 0.0, ALU.mult, ALU.add).then_inc(S["plan"], 1)
            dve.wait_ge(S["plan"], 10)
            dve.tensor_tensor(starts[:], ends[:], need[:], ALU.subtract).then_inc(S["plan"], 1)
            dve.wait_ge(S["plan"], 11)
            dve.scalar_tensor_tensor(cum[:], starts[:].unsqueeze(2).to_broadcast([P, E, NSEQ]), float(P), tot[:], ALU.mult, ALU.add).then_inc(S["plan"], 1)
            dve.wait_ge(S["plan"], 12)
            dve.tensor_tensor(z[:], WITHIN[:].rearrange("p (t e) -> p t e", e=E), cum[:].rearrange("p e t -> p t e"), ALU.add).then_inc(S["plan"], 1)
            dve.wait_ge(S["plan"], 13)
            for k in range(2):
                dve.tensor_tensor(oh[:, k], oh[:, k], z[:], ALU.mult).then_inc(S["plan"], 1)
            dve.wait_ge(S["plan"], 15)
            for k in range(2):
                dve.tensor_reduce(posf[:, k, :], oh[:, k], AX.X, ALU.add).then_inc(S["plan"], 1)
            dve.wait_ge(S["plan"], 17)
            dve.tensor_copy(pos_i[:], posf[:]).then_inc(S["pos_out"], 1)
            dve.tensor_tensor(cmp[:], ends[:].unsqueeze(1).to_broadcast([P, NT, E]), iota_t[:].unsqueeze(2).to_broadcast([P, NT, E]), ALU.is_le)\
                .then_inc(S["plan"], 1)
            dve.wait_ge(S["plan"], 18)
            dve.tensor_reduce(tef[:], cmp[:], AX.X, ALU.add).then_inc(S["plan"], 1)
            dve.wait_ge(S["plan"], 19)
            dve.tensor_scalar(te_i[:], tef[:], float(E - 1), None, ALU.min).then_inc(S["te_out"], 1)
            for e in range(E):
                b = e % 2
                dve.wait_ge(S["w_hi"], 2 * e + 2)
                dve.tensor_tensor(gu_w[:, LO, e], st[:, b], gu_w[:, HI, e].bitcast(F32), ALU.subtract).then_inc(S["w_lo"], 1)
                dve.tensor_tensor(dn_w[:, LO, e], st_d[:, b], dn_w[:, HI, e].bitcast(F32), ALU.subtract).then_inc(S["w_lo"], 1)
                dve.wait_ge(S["b_hi"], e + 1)
                dve.tensor_tensor(st_b[:, b], st_b[:, b], bias_w[:, e], ALU.subtract).then_inc(S["b_r1"], 1)
                dve.wait_ge(S["b_mid"], 2 * e + 2)
                dve.tensor_tensor(bias_w[64:96, e], st_b[64:96, b], bias_w[64:96, e], ALU.subtract).then_inc(S["b_lo"], 1)
            dve.wait_ge(S["w_lo"], 2 * E)
            dve.wait_ge(S["b_lo"], E)

            def step(i, n, tr=True, mid=True, at=True, down=True):
                if tr:
                    m, _, b = item(i, n + 1)
                    dve.wait_ge(S["hix"], m + 1)
                    dve.tensor_tensor(xs_w[:, b, LO].rearrange("p a h s -> p (a h s)"), TRX[b][:], xs_w[:, b, HI].bitcast(F32).rearrange("p a h s -> p (a h s)"),
                                      ALU.subtract).then_inc(S["lox"], 1)
                if mid:
                    m, _, b = item(i, n)
                    gu_p = GU[b][:].rearrange("p (a c) -> p a c", a=2)
                    dve.wait_ge(S["gu"], m + 1)
                    dve.tensor_scalar(gs[:, b], gu_p[:, :, 0:P], LIMIT, None, ALU.min).then_inc(S["gsd"], 1)
                    if later(m):
                        dve.wait_ge(S["att"], m - 1)
                    dve.tensor_scalar(us[:, b], gu_p[:, :, P:2 * P], LIMIT, -LIMIT, ALU.min, ALU.max).then_inc(S["usd"], 1)
                if at:
                    m, _, b = item(i, n - 1)
                    dve.wait_ge(S["hia"], m + 1)
                    dve.tensor_tensor(ac_w[:, b, LO].rearrange("p a s -> p (a s)"), AT[b][:, 0:2 * P], ac_w[:, b, HI].bitcast(F32).rearrange("p a s -> p (a s)"),
                                      ALU.subtract).then_inc(S["loa"], 1)
                if mid:
                    m, _, b = item(i, n)
                    dve.wait_ge(S["gld"], m + 1)
                    dve.wait_ge(S["usd"], m + 1)
                    dve.scalar_tensor_tensor(us[:, b], us[:, b], 1.0, gs[:, b], ALU.add, ALU.mult).then_inc(S["acd"], 1)

            steps(dve, step)
            for g in range(NG):
                dve.wait_ge(gathered[g], 16 * 2 * GT)
                for k in range(2):
                    if k == 1:
                        dve.wait_ge(S["added0"], g * GT + GT)
                    for t in range(g * GT, g * GT + GT):
                        dve.scalar_tensor_tensor(x[:, t, :], m_all[:, (2 * t + k) % NSEQ, :], wt[:, t, k:k + 1], x[:, t, :], ALU.mult, ALU.add)\
                            .then_inc(S[f"added{k}"], 1)

        @block.tensor
        def _(pe):
            hp = [(h, p) for h in range(2) for p in PASSES]
            pe.wait_ge(S["r_lo"], 2)
            def transposes(g):
                pe.wait_ge(S["norm_done"], g * GT + GT)
                if g >= 1:
                    pe.wait_ge(S["m_lo"], g * 2)
                for h in range(2):
                    for t in range(GT):
                        last = pe.transpose(TRX[h][:, t * P:(t + 1) * P], m_all[:, g * GT + t, h * P:(h + 1) * P], ident[:])
                    last.then_inc(S["tr_done"], 1)

            transposes(0)
            for g in range(NG):
                pe.wait_ge(S["m_lo"], g * 2 + 2)
                if g >= 1:
                    pe.wait_ge(S["lgT_out"], g)
                for i, (h, (a, b)) in enumerate(hp):
                    last = pe.matmul(LGT[:], r_w[:, a, h, :], m_w[:, b, h, :], start=(i == 0), stop=(i == 5))
                last.then_inc(S["lgT_done"], 1)
                if g + 1 < NG:
                    transposes(g + 1)
                pe.wait_ge(S["lgT_out"], g + 1)
                if g >= 1:
                    pe.wait_ge(S["lg_done"], g)
                for t in range(GT):
                    last = pe.transpose(LGB[:, t * E:(t + 1) * E], lgT[:, t * P:(t + 1) * P], ident[0:E, 0:E])
                last.then_inc(S["lgB_done"], 1)
            pe.wait_ge(S["plan"], 4)
            pe.wait_ge(S["consts"], 8)
            pe.matmul(TOTAL[:], ones[:], z[:].rearrange("p t e -> p (t e)"), start=True, stop=True).then_inc(S["counted"], 1)
            pe.matmul(WITHIN[:], before[:], z[:].rearrange("p t e -> p (t e)"), start=True, stop=True).then_inc(S["counted"], 1)
            pe.wait_ge(S["te_out"], 1)
            pe.wait_ge(S["w_lo"], 2 * E)
            pe.wait_ge(S["b_lo"], E)
            pe.wait_ge(S["consts"], 12)

            loaded = []

            def load_experts(tile, count):
                return list(nc.values_load_multi_w_load_instructions(te_i[0:1, bass.ds(tile, count)], engines=[mybir.EngineType.PE],
                                                                     min_val=0, max_val=E - 1)[1])

            def step(i, n, tr=True, mid=True, at=True, down=True):
                if isinstance(i, int):
                    first, last_m = (n - 2 if down else n), (n if mid else n - 2)
                    loaded.clear()
                    if last_m >= 0:
                        loaded.extend(load_experts(2 * first, 2 * (last_m - first + 1)))
                    e_down, e_mid = loaded[0:2], loaded[-2:]
                elif n % 2 == 0:
                    loaded[:] = load_experts(2 * item(i, n - 2)[0], 8)
                    e_down, e_mid = loaded[0:2], loaded[4:6]
                else:
                    e_down, e_mid = loaded[2:4], loaded[6:8]
                if tr:
                    m, before_m, b = item(i, n + 1)
                    pe.wait_ge(S["xs_in0"] if b == 0 else S["xs_in1"], 16 * before_m + 16)
                    if later(m):
                        pe.wait_ge(S["lox"], m - 1)
                    for a in range(2):
                        for h in range(2):
                            last = pe.transpose(TRX[b][:, (2 * a + h) * P:(2 * a + h + 1) * P], xs[:, b, a, h * P:(h + 1) * P], ident[:])
                    last.then_inc(S["trx"], 1)
                if mid:
                    m, _, b = item(i, n)
                    pe.wait_ge(S["lox"], m + 1)
                    if later(m):
                        pe.wait_ge(S["gsd"], m - 1)
                        pe.wait_ge(S["usd"], m - 1)
                    for a in range(2):
                        e = e_mid[a]
                        gu_a = GU[b][:, a * 2 * P:(a + 1) * 2 * P]
                        for j, (h, (p, q)) in enumerate(hp):
                            pe.matmul(gu_a, xs_w[:, b, p, a, h, :], gu_w[:, q, bass.ds(e, 1), h, :].rearrange("p o c -> p (o c)"), start=(j == 0), stop=False)
                        last = pe.matmul(gu_a, sel[0:96, :], bias_w[0:96, bass.ds(e, 1), 0, :].rearrange("p o c -> p (o c)"), start=False, stop=True)
                    last.then_inc(S["gu"], 1)
                if at:
                    m, _, b = item(i, n - 1)
                    pe.wait_ge(S["acd"], m + 1)
                    if later(m):
                        pe.wait_ge(S["loa"], m - 1)
                    for a in range(2):
                        last = pe.transpose(AT[b][:, a * P:(a + 1) * P], us[:, b, a, :], ident[:])
                    last.then_inc(S["att"], 1)
                if down:
                    m, _, b = item(i, n - 2)
                    pe.wait_ge(S["loa"], m + 1)
                    if later(m):
                        pe.wait_ge(S["yev"], m - 1)
                    for a in range(2):
                        e = e_down[a]
                        dn_a = DN[b][:, a * DM:(a + 1) * DM]
                        for j, (p, q) in enumerate(PASSES):
                            pe.matmul(dn_a, ac_w[:, b, p, a, :], dn_w[:, q, bass.ds(e, 1), :].rearrange("p o c -> p (o c)"), start=(j == 0), stop=False)
                        last = pe.matmul(dn_a, sel[0:96, :], bias_w[0:96, bass.ds(e, 1), 1, :].rearrange("p o c -> p (o c)"), start=False, stop=True)
                    last.then_inc(S["dn"], 1)

            steps(pe, step)


def program(nc, ids, emb, pos, A_diag, Bw, Cw, Dw, w1, w2, b2, cols, lnf, wqkv, wbm, wo, conv, norm_w, wr, wgu, bias, wd, out):
    NSEQ, DM = ids.shape[1], emb.shape[1]
    scr_g = nc.dram_tensor("scr_g", (P, 32, 32), F32, kind="Internal").ap()
    scr_b = nc.dram_tensor("scr_b", (32, P), F32, kind="Internal").ap()
    scr_t = nc.dram_tensor("scr_t", (P, 32, 64), F16, kind="Internal").ap()
    SLOTS = P * slot_tiles(NSEQ * P, wr.shape[1])
    slots = nc.dram_tensor("slots", (SLOTS, DM), F32, kind="Internal").ap()
    slot_out = nc.dram_tensor("slot_out", (SLOTS, DM), F32, kind="Internal").ap()
    with ExitStack() as ctx:
        x = ctx.enter_context(nc.sbuf_tensor("x", [P, NSEQ, DM], F32))
        ident = ctx.enter_context(nc.sbuf_tensor("ident", [P, P], F32))
        half = ctx.enter_context(nc.sbuf_tensor("half", [P, 1], F32))
        lnf_sb = ctx.enter_context(nc.sbuf_tensor("lnf_sb", [P, 2, DM], F32))
        def give_back(phase_sems):
            nc.all_engine_barrier()
            nc.clear_and_free_semaphores(phase_sems)
            nc.all_engine_barrier()

        phase_sems = []
        tower(nc, phase_sems, x, ident, half, lnf_sb, ids, emb, pos, A_diag, Bw, Cw, Dw, w1, w2, b2, cols, lnf)
        give_back(phase_sems)
        phase_sems = []
        attention(nc, phase_sems, x, ident, half, lnf_sb, wqkv, wbm, wo, conv, norm_w, scr_g, scr_b, scr_t)
        give_back(phase_sems)
        experts(nc, ctx, x, ident, half, slots, slot_out, wr, wgu, bias, wd, out)


def kernel(**inputs):
    import numpy as np
    import concourse.bacc as bacc
    from concourse.bass_utils import run_bass_kernel_spmd as run

    a = {k: np.asarray(v) for k, v in inputs.items()}
    tok, attn, ffn = "L0_tok_", "L0_attn_", "L0_ffn_"

    def columns(v):
        return v.reshape(v.shape[0], -1, P).transpose(0, 2, 1)

    gate_up, gate_up_bias = a[ffn + "gate_up_proj"], a[ffn + "gate_up_proj_bias"]
    arrays = {
        "ids": a["x"].T, "emb": a[tok + "emb"], "pos": a[tok + "pos_emb"], "A_diag": a[tok + "A_diag"].T,
        "Bw": a[tok + "B"], "Cw": a[tok + "C"], "Dw": a[tok + "D"], "w1": a[tok + "w1"], "w2": a[tok + "w2"], "b2": a[tok + "b2"],
        "cols": np.concatenate([columns(a[tok + n]) for n in ("ln1_s", "ln1_b", "ln2_s", "ln2_b", "b1")], axis=2),
        "lnf": np.stack([a[tok + "lnf_s"], a[tok + "lnf_b"]]),
        "wqkv": np.concatenate([a[attn + n].T for n in ("Wq", "Wk", "Wv")], axis=1),
        "wbm": np.concatenate([a[attn + "Wb"].T, a[attn + "Wmix"].T], axis=1),
        "wo": a[attn + "Wo"].T,
        "conv": np.concatenate([a[attn + n] for n in ("conv_q", "conv_k", "conv_v")]),
        "norm_w": np.concatenate([a[attn + "norm_w"]] * 2)[:, None],
        "wr": a[ffn + "router_weight"],
        "wgu": np.concatenate([gate_up[:, :, 0::2], gate_up[:, :, 1::2]], axis=2),
        "bias": np.stack([np.concatenate([gate_up_bias[:, 0::2], gate_up_bias[:, 1::2]], axis=1), a[ffn + "down_proj_bias"]], axis=1),
        "wd": a[ffn + "down_proj"],
    }
    arrays = {k: np.ascontiguousarray(v) for k, v in arrays.items()}
    nc = bacc.Bacc("TRN2", target_bir_lowering=False, num_devices=1)
    aps = {k: nc.dram_tensor(k, v.shape, mybir.dt.from_np(v.dtype), kind="ExternalInput").ap() for k, v in arrays.items()}
    shape = (a["x"].shape[0], a["x"].shape[1], a[tok + "emb"].shape[1])
    aps["out"] = nc.dram_tensor("out", shape, F32, kind="ExternalOutput").ap()
    program(nc, **aps)
    return run(nc, [arrays], core_ids=[0]).results[0]["out"]
```
